# Optimizing a Trainium2 kernel written in Bass

```python
import numpy as np
import jax
import jax.numpy as jnp

def _softmax(x, axis=-1):
    return jax.nn.softmax(x, axis=axis)

def _gelu(x):
    return jax.nn.gelu(x, approximate=True)

def _silu(x):
    return jax.nn.silu(x)

def _sigmoid(x):
    return jax.nn.sigmoid(x)

def _layernorm(x, axis=-1, eps=1e-05):
    m = jnp.mean(x, axis=axis, keepdims=True)
    v = jnp.var(x, axis=axis, keepdims=True)
    return (x - m) / jnp.sqrt(v + eps)

def _scatter_add(tgt, idx, src, axis=0):
    return tgt.at[idx].add(src)

def _segment_sum(src, seg, n):
    return jax.ops.segment_sum(src, seg, n)
kernel_name = 'mk_gnn_ffn_d1_gnn_r8_2809fb'

def setup_inputs(seed: int=0):
    np.random.seed(seed)
    _w = jnp.asarray

    def _rec_inputs():
        import jax
        import jax.numpy as jnp
        _gk = jax.random.key(seed)
        x = -0.0005963 + 1.001 * jax.random.normal(jax.random.fold_in(_gk, 1), (384, 1024), jnp.float32)
        src = jax.random.randint(jax.random.fold_in(_gk, 2), (6144,), 0, 384, jnp.int32)
        dst = jax.random.randint(jax.random.fold_in(_gk, 3), (6144,), 0, 384, jnp.int32)
        _o = jnp.argsort(dst, stable=True)
        src = src[_o]
        dst = dst[_o]
        edge_type_5 = jax.random.randint(jax.random.fold_in(_gk, 12), (6144,), 0, 5, jnp.int32)
        return (x, src, dst, edge_type_5)
    x, src, dst, edge_type_5 = _rec_inputs()

    def _L0_gnn_setup():
        import jax, jax.numpy as jnp
        import numpy as np
        N = 384
        E = 12288
        IN_F = 1024
        OUT_F = 1024
        H = 16
        D = OUT_F // H
        NUM_ETYPES = 4

        def _build_mask(edge_index, edge_type, edge_type_weights, dtype):
            src, dst = (edge_index[0], edge_index[1])
            w = jax.nn.softplus(edge_type_weights)
            mask = jnp.full((N, N), -jnp.inf, dtype=dtype)
            mask = mask.at[src, dst].set(w[edge_type - 1])
            diag = jnp.diagonal(mask)
            idx = jnp.arange(N)
            mask = mask.at[idx, idx].set(jnp.where(jnp.isneginf(diag), w[3], diag))
            return mask
        key = jax.random.key(seed)
        ks = jax.random.split(key, 20)
        p = lambda k, shape: jax.random.normal(k, shape, dtype=jnp.float32) * 0.02
        return {'x': jax.random.normal(ks[0], (N, IN_F), dtype=jnp.float32), 'edge_index': jax.random.randint(ks[1], (2, E), 0, N), 'edge_type': jax.random.randint(ks[2], (E,), 1, NUM_ETYPES + 1), 'edge_type_weights': jnp.ones((NUM_ETYPES,), jnp.float32) + 0.1 * jax.random.normal(ks[3], (NUM_ETYPES,), dtype=jnp.float32), 'wq': p(ks[4], (OUT_F, IN_F)), 'bq': p(ks[5], (OUT_F,)), 'wk': p(ks[6], (OUT_F, IN_F)), 'bk': p(ks[7], (OUT_F,)), 'wv': p(ks[8], (OUT_F, IN_F)), 'bv': p(ks[9], (OUT_F,)), 'wiq': p(ks[10], (OUT_F, OUT_F)), 'biq': p(ks[11], (OUT_F,)), 'wik': p(ks[12], (OUT_F, OUT_F)), 'bik': p(ks[13], (OUT_F,)), 'wiv': p(ks[14], (OUT_F, OUT_F)), 'biv': p(ks[15], (OUT_F,)), 'wo': p(ks[16], (OUT_F, OUT_F)), 'bo': p(ks[17], (OUT_F,))}
    _L0_gnn_all = _L0_gnn_setup()
    _L0_gnn_in = {k: v for k, v in _L0_gnn_all.items() if k in ('edge_type_weights', 'wq', 'bq', 'wk', 'bk', 'wv', 'bv', 'wiq', 'biq', 'wik', 'bik', 'wiv', 'biv', 'wo', 'bo')}
    del _L0_gnn_all

    def _L0_ffn_setup():
        import jax, jax.numpy as jnp
        import numpy as np
        B, S, D = (2, 256, 1024)
        E, H, K = (8, 704, 2)
        N_RESERVED = 4
        key = jax.random.key(seed)
        ks = jax.random.split(key, 5)
        scale = 0.02
        x = jax.random.normal(ks[0], (B, S, D), dtype=jnp.float32)
        gate_w = jax.random.normal(ks[1], (E, D), dtype=jnp.float32) * scale
        w1 = jax.random.normal(ks[2], (E, D, H), dtype=jnp.float32) * scale
        w3 = jax.random.normal(ks[3], (E, D, H), dtype=jnp.float32) * scale
        w2 = jax.random.normal(ks[4], (E, H, D), dtype=jnp.float32) * scale
        return {'x': x, 'gate_w': gate_w, 'w1': w1, 'w2': w2, 'w3': w3}
    _L0_ffn_all = _L0_ffn_setup()
    _L0_ffn_in = {k: v for k, v in _L0_ffn_all.items() if k in ('gate_w', 'w1', 'w2', 'w3')}
    del _L0_ffn_all
    return {'x': x, 'src': src, 'dst': dst, 'edge_type_5': edge_type_5, 'L0_gnn_edge_type_weights': _L0_gnn_in['edge_type_weights'], 'L0_gnn_wq': _L0_gnn_in['wq'], 'L0_gnn_bq': _L0_gnn_in['bq'], 'L0_gnn_wk': _L0_gnn_in['wk'], 'L0_gnn_bk': _L0_gnn_in['bk'], 'L0_gnn_wv': _L0_gnn_in['wv'], 'L0_gnn_bv': _L0_gnn_in['bv'], 'L0_gnn_wiq': _L0_gnn_in['wiq'], 'L0_gnn_biq': _L0_gnn_in['biq'], 'L0_gnn_wik': _L0_gnn_in['wik'], 'L0_gnn_bik': _L0_gnn_in['bik'], 'L0_gnn_wiv': _L0_gnn_in['wiv'], 'L0_gnn_biv': _L0_gnn_in['biv'], 'L0_gnn_wo': _L0_gnn_in['wo'], 'L0_gnn_bo': _L0_gnn_in['bo'], 'L0_ffn_gate_w': _L0_ffn_in['gate_w'], 'L0_ffn_w1': _L0_ffn_in['w1'], 'L0_ffn_w2': _L0_ffn_in['w2'], 'L0_ffn_w3': _L0_ffn_in['w3']}

def reference(x, src, dst, edge_type_5, L0_gnn_edge_type_weights, L0_gnn_wq, L0_gnn_bq, L0_gnn_wk, L0_gnn_bk, L0_gnn_wv, L0_gnn_bv, L0_gnn_wiq, L0_gnn_biq, L0_gnn_wik, L0_gnn_bik, L0_gnn_wiv, L0_gnn_biv, L0_gnn_wo, L0_gnn_bo, L0_ffn_gate_w, L0_ffn_w1, L0_ffn_w2, L0_ffn_w3):
    import jax
    import jax.numpy as jnp

    def _L0_gnn_ref(x, edge_index, edge_type, edge_type_weights, wq, bq, wk, bk, wv, bv, wiq, biq, wik, bik, wiv, biv, wo, bo):
        import jax, jax.numpy as jnp
        import numpy as np
        N = 384
        E = 12288
        IN_F = 1024
        OUT_F = 1024
        H = 16
        D = OUT_F // H
        NUM_ETYPES = 4

        def _build_mask(edge_index, edge_type, edge_type_weights, dtype):
            src, dst = (edge_index[0], edge_index[1])
            w = jax.nn.softplus(edge_type_weights)
            mask = jnp.full((N, N), -jnp.inf, dtype=dtype)
            mask = mask.at[src, dst].set(w[edge_type - 1])
            diag = jnp.diagonal(mask)
            idx = jnp.arange(N)
            mask = mask.at[idx, idx].set(jnp.where(jnp.isneginf(diag), w[3], diag))
            return mask
        q = x @ wq.T + bq
        k = x @ wk.T + bk
        v = x @ wv.T + bv
        q2 = (q @ wiq.T + biq).reshape(N, H, D).transpose(1, 0, 2)
        k2 = (k @ wik.T + bik).reshape(N, H, D).transpose(1, 0, 2)
        v2 = (v @ wiv.T + biv).reshape(N, H, D).transpose(1, 0, 2)
        mask = _build_mask(edge_index, edge_type, edge_type_weights, x.dtype)
        scale = 1.0 / np.sqrt(D).astype(np.float32)
        scores = jnp.einsum('hnd,hmd->hnm', q2, k2) * scale + mask[None]
        attn = jax.nn.softmax(scores, axis=-1)
        out = jnp.einsum('hnm,hmd->hnd', attn, v2)
        out = out.transpose(1, 0, 2).reshape(N, OUT_F)
        return out @ wo.T + bo

    def _L0_ffn_ref(x, gate_w, w1, w2, w3):
        import jax, jax.numpy as jnp
        import numpy as np
        B, S, D = (2, 256, 1024)
        E, H, K = (8, 704, 2)
        N_RESERVED = 4
        b, s, d = x.shape
        T = b * s
        xf = x.reshape(T, d)
        logits = xf @ gate_w.T
        expert_ids = jnp.arange(E)
        logits = jnp.where(expert_ids[None, :] >= E - N_RESERVED, -jnp.inf, logits)
        weights = jax.nn.softmax(logits, axis=-1)
        top_w, top_idx = jax.lax.top_k(weights, K)
        top_w = top_w / jnp.sum(top_w, axis=-1, keepdims=True)
        cw = jnp.zeros((T, E), dtype=x.dtype).at[jnp.arange(T)[:, None], top_idx].add(top_w)
        h = jax.nn.silu(jnp.einsum('td,edh->teh', xf, w1)) * jnp.einsum('td,edh->teh', xf, w3)
        y = jnp.einsum('teh,ehd->ted', h, w2)
        out = jnp.einsum('te,ted->td', cw, y)
        return out.reshape(b, s, d)
    edge_index = jnp.stack([src, dst])
    x = x + _L0_gnn_ref(_layernorm(x, axis=-1), edge_index, edge_type_5, L0_gnn_edge_type_weights, L0_gnn_wq, L0_gnn_bq, L0_gnn_wk, L0_gnn_bk, L0_gnn_wv, L0_gnn_bv, L0_gnn_wiq, L0_gnn_biq, L0_gnn_wik, L0_gnn_bik, L0_gnn_wiv, L0_gnn_biv, L0_gnn_wo, L0_gnn_bo)
    x = x + _L0_ffn_ref(_layernorm(x, axis=-1)[None], L0_ffn_gate_w, L0_ffn_w1, L0_ffn_w2, L0_ffn_w3)[0]
    return x

_drawn_inputs = setup_inputs


def setup_inputs(seed=0):
    import zlib

    import numpy as np

    out = dict(_drawn_inputs(seed))
    spreads = {}
    factors = {'L0_gnn_edge_type_weights': 22.16,
     'L0_gnn_wq': 4.69,
     'L0_gnn_bq': 8.0,
     'L0_gnn_wk': 4.993,
     'L0_gnn_bk': 64.0,
     'L0_gnn_bv': 5.794,
     'L0_gnn_wiq': 4.964,
     'L0_gnn_biq': 8.0,
     'L0_gnn_wik': 4.603,
     'L0_gnn_bik': 64.0,
     'L0_gnn_biv': 4.081,
     'L0_gnn_bo': 2.73}
    for name, (base, spread) in spreads.items():
        noise = np.random.default_rng([zlib.crc32(name.encode()), seed]).standard_normal(out[name].shape)
        drawn = base * np.exp(spread * noise) if base else spread * noise
        out[name] = jnp.asarray(drawn.astype(out[name].dtype))
    for name, factor in factors.items():
        out[name] = (out[name] * factor).astype(out[name].dtype)
    return out
```

```python
from contextlib import ExitStack

import concourse.bass as bass
from concourse import mybir

P = 128
F32 = mybir.dt.float32
F16 = mybir.dt.float16
BF16 = mybir.dt.bfloat16
I32 = mybir.dt.int32
ALU = mybir.AluOpType
ACT = mybir.ActivationFunctionType
AX = mybir.AxisListType

ds = bass.ds

W_SCALE = 64.0
W_BACK = 1.0 / W_SCALE
ABSENT = 1.0e30
EPS = 1e-5
SLOTS = 6


def gnn_moe_kernel(nc, x_d, src_d, dst_d, etype_d, etw_d, wq, bq, wk, bk, wv, bv, wiq, biq,
                   wik, bik, wiv, biv, wo, bo, gate_w, w1, w2, w3, out_d):
    N, D = x_d.shape
    T = N // P
    KD = D // P
    E = src_d.shape[0]
    NB = E // P
    DH = 64
    NE = 4
    HID = w1.shape[2]
    FULL = HID // P
    HALF = HID - FULL * P
    NS = NE * HID // P
    assert (N, D, HID, HALF, NS, NB) == (384, 1024, 704, 64, 22, 48)

    def tile_col(e, i):
        return (HALF if e % 2 else 0) + P * i

    with ExitStack() as ctx:
        def sb(name, shape, dt=F32):
            return ctx.enter_context(nc.sbuf_tensor(name, shape, dt))

        def sem(name):
            return ctx.enter_context(nc.semaphore(name))

        bank = [ctx.enter_context(nc.psum_tensor(f"bank{i}", [P, 512], F32)) for i in range(8)]
        turn_bank = bank[0:2]
        acc_bank = bank[2:4]
        score_bank = bank[4:6]
        t3_bank = bank[6]
        pv_bank = bank[7]
        edge_bank = [bank[4], bank[5], bank[7]]
        out_bank = bank[2:8]

        x = sb("x", [P, T, D])
        xn = sb("xn", [P, T, D])
        xt = [sb("xt_hi", [P, KD, N], F16), sb("xt_lo", [P, KD, N], F16)]
        proj = {n: [sb(f"{n}t_hi", [P, KD, N], F16), sb(f"{n}t_lo", [P, KD, N], F16)] for n in "qkv"}
        q2 = [[sb(f"q2_{b}_{h}", [P, N], F16) for h in range(2)] for b in range(2)]
        k2 = [[sb(f"k2_{b}_{h}", [P, N], F16) for h in range(2)] for b in range(2)]
        v2 = [[sb(f"v2_{b}_{h}", [P, T, P], F16) for h in range(2)] for b in range(2)]
        ot = [sb("ot_hi", [P, KD, N], F16), sb("ot_lo", [P, KD, N], F16)]
        raw = [sb(f"raw{i}", [P, D]) for i in range(SLOTS)]
        wb = [[sb(f"w{b}_{h}", [P, KD, P], F16) for h in range(2)] for b in range(3)]
        ybuf = [sb(f"y{b}", [P, N]) for b in range(2)]
        yv = sb("yv", [P, N])
        bias = sb("bias", [P, 7, KD])
        biasq = sb("biasq", [P, KD])
        bias_rows = sb("bias_rows", [7 * KD, P])
        masked = [sb(f"masked{b}", [P, N]) for b in range(2)]
        probs = [sb(f"probs{b}", [P, N]) for b in range(2)]
        pt = [[sb(f"pt_{b}_{h}", [P, T, P], F16) for h in range(2)] for b in range(2)]
        att = [sb(f"att{b}", [P, T, P]) for b in range(2)]
        negmax = sb("negmax", [P, 6])
        rowsum = sb("rowsum", [P, 6])
        rinv = sb("rinv", [P, 6])
        negmask = sb("negmask", [P, T, N])
        stats = sb("stats", [P, T, 2, 6])
        mv = sb("mv", [P, T, 2])
        veps = sb("veps", [P, T])
        rstd = sb("rstd", [P, T])
        mhalf = sb("mhalf", [P, T])
        ident = sb("ident", [P, P])
        upper = sb("upper", [P, P])
        iota_i = sb("iota_i", [P, N], I32)
        iota = sb("iota", [P, N], F16)
        diag_w = sb("diag_w", [P, P], BF16)
        diag_col = sb("diag_col", [P, T, N], BF16)
        edges_i = sb("edges_i", [NB, 3, P], I32)
        edges_f = sb("edges_f", [NB, 4, P])
        edge = sb("edge", [P, 4, NB])
        batch_i = sb("batch_i", [P, NB], I32)
        batch_e = sb("batch_e", [P, NB])
        keyb = sb("keyb", [P, NB, P])
        later = sb("later", [P, NB])
        keep = sb("keep", [P, NB])
        expo = sb("expo", [P, NB])
        val_i = sb("val_i", [P, NB], I32)
        val = sb("val", [P, NB])
        OH = 4
        oh_src = [sb(f"oh_src{i}", [P, N], BF16) for i in range(OH)]
        oh_dst = [sb(f"oh_dst{i}", [P, N], BF16) for i in range(OH)]
        esum = sb("esum", [P, T, N])
        etyp = sb("etyp", [P, T, N], I32)
        mtmp = sb("mtmp", [P, T, N])
        same = mtmp[:].rearrange("p t n -> p (t n)")
        etw = sb("etw", [P, 4])
        sp_a = sb("sp_a", [P, 4])
        sp_b = sb("sp_b", [P, 4])
        sp_c = sb("sp_c", [P, 4])
        nsoft = sb("nsoft", [P, 4])
        def room(name, half, n):
            flat = proj[name][half][:].rearrange("p k n -> p (k n)").bitcast(F32)
            return [flat[:, N * i:N * (i + 1)] for i in range(n)]

        gate_n = esum[0:NE, :, :].rearrange("p t n -> p (t n)")[:, 0:D]
        gt = [sb("gt_hi", [P, KD, NE], F16), sb("gt_lo", [P, KD, NE], F16)]
        lg = sb("lg", [P, T, NE])
        lmax = sb("lmax", [P, T])
        pr = sb("pr", [P, T, NE])
        cmp_a = sb("cmp_a", [P, T, NE, NE])
        cmp_b = sb("cmp_b", [P, T, NE, NE])
        before = sb("before", [P, NE, NE])
        after = sb("after", [P, NE, NE])
        rank = sb("rank", [P, T, NE])
        csum = sb("csum", [P, T])
        cinv = sb("cinv", [P, T])
        cw = sb("cw", [P, T, NE])
        cwx = [a.rearrange("p (t c) -> p t c", t=T) for a in room("q", 0, NE)]
        cwb = room("q", 1, NE)
        sig, g1 = room("k", 0, 4)[0:2], room("k", 0, 4)[2:4]
        g3, hid = room("k", 1, 4)[0:2], room("k", 1, 4)[2:4]
        ht = [[proj["v"][b][:, h, :] for h in range(2)] for b in range(2)]
        res = xn

        x_in = [sem(f"x_in{t}") for t in range(T)]
        edges_in = sem("edges_in")
        bias_in = sem("bias_in")
        bias_turned = sem("bias_turned")
        bias_ready = sem("bias_ready")
        etw_in = sem("etw_in")
        gate_in = sem("gate_in")
        raw_in = [sem(f"raw_in{i}") for i in range(SLOTS)]
        out_done = sem("out_done")
        consts = sem("consts")
        pool_step = sem("pool_step")
        norm_step = sem("norm_step")
        rstd_made = sem("rstd_made")
        xn_ready = sem("xn_ready")
        edge_step = sem("edge_step")
        edges_f_ready = sem("edges_f_ready")
        edges_turned = sem("edges_turned")
        keyb_ready = sem("keyb_ready")
        keys_turned = sem("keys_turned")
        keys_compared = sem("keys_compared")
        oh_ready = sem("oh_ready")
        oh_used = sem("oh_used")
        edges_summed = sem("edges_summed")
        mask_step = sem("mask_step")
        mask_ready = sem("mask_ready")
        soft_a = sem("soft_a")
        soft_b = sem("soft_b")
        w_turned = sem("w_turned")
        w_hi = sem("w_hi")
        w_lo = sem("w_lo")
        mm_done = sem("mm_done")
        y_ready = sem("y_ready")
        y_hi = sem("y_hi")
        y_split = sem("y_split")
        t3_turned = sem("t3_turned")
        t3_hi = sem("t3_hi")
        t3_split = sem("t3_split")
        scored = sem("scored")
        masked_max = sem("masked_max")
        prob_ready = sem("prob_ready")
        inv_ready = sem("inv_ready")
        pv_done = sem("pv_done")
        att_ready = sem("att_ready")
        gate_turned = sem("gate_turned")
        gate_hi = sem("gate_hi")
        gate_split = sem("gate_split")
        logits_done = sem("logits_done")
        route_step = sem("route_step")
        route_exp = sem("route_exp")
        cwx_ready = sem("cwx_ready")
        cw_turned = sem("cw_turned")
        cw_ready = sem("cw_ready")
        f_hi = sem("f_hi")
        f_lo = sem("f_lo")
        f_used = sem("f_used")
        sig_ready = sem("sig_ready")
        gated = sem("gated")
        hid_ready = sem("hid_ready")
        hid_hi = sem("hid_hi")
        hid_split = sem("hid_split")
        tile_done = sem("tile_done")
        res_ready = sem("res_ready")

        block = ctx.enter_context(nc.Block())

        U_INNER = 3 * KD
        U_OUT = 6 * KD
        U_ALL = 7 * KD
        C_LN = KD

        def c_base(r):
            return C_LN + 6 + 8 * (r - 2)

        C_OUT = c_base(9) + 2
        C_LN2 = C_OUT + KD

        def turn_count(r, what, first):
            if first:
                return C_LN + ["V", "P0", "P1", "P2", "P3", "P4"].index(what)
            order = ["P5", "O"] if isinstance(r, int) and r == 9 else ["V", "P5", "P0", "P1", "P2", "O", "P3", "P4"]
            return c_base(r) + order.index(what)

        def f_w1(s):
            return 3 * s - 1 if not (isinstance(s, int) and s == 0) else 0

        def f_w3(s):
            return f_w1(s) + 1

        def f_w2(s):
            return 3 * s + (2 if isinstance(s, int) and s == NS - 1 else 4)

        w1_slot = [0, 3]
        w2_slot = [5, 2]

        def slot_count(slot, nth):
            return 16 * (nth + (11 if slot < 2 else 10))

        def w1_landed(s_half, par, w):
            return slot_count(w1_slot[par] + w, s_half + 1)

        def w2_landed(s_half, par):
            return slot_count(w2_slot[par], s_half + 1)

        inner = [(wiq, "q"), (wik, "k"), (wiv, "v")]
        rows = lambda w: w.rearrange("(r p) i -> r p i", p=P)

        @block.sync
        def _(sp):
            for t in range(T):
                sp.dma_start(x[:, t, :], x_d[P * t:P * (t + 1), :]).then_inc(x_in[t], 16)
            for j, w in enumerate((wq, wk, wv)):
                for i in range(2):
                    sp.dma_start(raw[2 * j + i][:], rows(w)[i]).then_inc(raw_in[2 * j + i], 16)
            with sp.Fori(1, 4) as it:
                for j, w in enumerate((wq, wk, wv)):
                    for i in range(2):
                        s = 2 * j + i
                        sp.wait_ge(w_turned, 12 * it + 2 * s - 10)
                        sp.dma_start(raw[s][:], rows(w)[2 * it + i]).then_inc(raw_in[s], 16)
            with sp.Fori(4, 8) as it:
                for i in range(2):
                    for j, (w, _) in enumerate(inner):
                        s = 3 * i + j
                        sp.wait_ge(w_turned, 12 * it + 2 * s - 10)
                        sp.dma_start(raw[s][:], rows(w)[2 * it + (i - 8)]).then_inc(raw_in[s], 16)
            for r in range(KD):
                u = U_OUT + r
                sp.wait_ge(w_turned, 2 * u - 10)
                sp.dma_start(raw[u % SLOTS][:], rows(wo)[r]).then_inc(raw_in[u % SLOTS], 16)

            def load13(slot, w, e, col):
                dst = raw[slot][:].rearrange("p (k c) -> p k c", k=KD)
                sp.dma_start(dst, w[e].rearrange("(k p) c -> p k c", p=P)[:, :, ds(col, P)]
                             ).then_inc(raw_in[slot], 16)

            for s in range(2):
                for w, slot in ((w1, w1_slot[s]), (w3, w1_slot[s] + 1)):
                    prev = {0: U_ALL - 2, 1: U_ALL - 1, 3: U_ALL - 5, 4: U_ALL - 4}[slot]
                    sp.wait_ge(w_turned, 2 * prev + 2)
                    dst = raw[slot][:].rearrange("p (k c) -> p k c", k=KD)
                    for half, e, col in ((0, 2 * s, HID - HALF), (1, 2 * s + 1, 0)):
                        sp.dma_start(dst[:, :, HALF * half:HALF * (half + 1)],
                                     w[e].rearrange("(k p) c -> p k c", p=P)[:, :, col:col + HALF]
                                     ).then_inc(raw_in[slot], 16)
            for half, row in ((0, HID - HALF), (1, 0)):
                sp.dma_start(raw[5][HALF * half:HALF * (half + 1), :], w2[half, row:row + HALF, :]
                             ).then_inc(raw_in[5], 16)

            def step_loads(i, e, first):
                par = e % 2
                s = 4 * i + (2 + e)
                col = P * i + (HALF if par else 0)
                for j, w in enumerate((w1, w3)):
                    sp.wait_ge(f_lo, f_w1(s - 2) + j + 1)
                    load13(w1_slot[par] + j, w, e, col)
                slot = w2_slot[1 - par]
                if first and e == 0:
                    sp.wait_ge(w_turned, 2 * (U_ALL - 6) + 2)
                    for half, row in ((0, HID - HALF), (1, 0)):
                        sp.dma_start(raw[slot][HALF * half:HALF * (half + 1), :],
                                     w2[2 + half, row:row + HALF, :]).then_inc(raw_in[slot], 16)
                    return
                pe_, pi = (NE - 1, i - 1) if e == 0 else (e - 1, i)
                row = P * pi + (HALF if pe_ % 2 else 0)
                sp.wait_ge(f_lo, f_w2(s - 3) + 1)
                sp.dma_start(raw[slot][:], w2[pe_][ds(row, P), :]
                             ).then_inc(raw_in[slot], 16)

            for e in range(NE):
                step_loads(0, e, True)
            with sp.Fori(1, FULL) as i:
                for e in range(NE):
                    step_loads(i, e, False)
            sp.wait_ge(f_lo, f_w2(NS - 3) + 1)
            sp.dma_start(raw[w2_slot[1]][:], w2[NE - 1, HID - P:HID, :]).then_inc(raw_in[w2_slot[1]], 16)

            for t in range(T):
                sp.wait_ge(res_ready, 2 * t + 2)
                sp.dma_start(out_d[P * t:P * (t + 1), :], res[:, t, :]).then_inc(out_done, 16)
            sp.wait_ge(out_done, 16 * T)

        @block.gpsimd
        def _(pool):
            steps = [0]

            def link(ins):
                steps[0] += 1
                ins.then_inc(pool_step, 1)
                pool.wait_ge(pool_step, steps[0])

            pool.memset(mhalf[:], -0.5)
            pool.memset(ident[:], 0.0)
            pool.memset(upper[:], 1.0)
            pool.memset(before[:], 1.0)
            pool.memset(after[:], 1.0)
            pool.iota(batch_i[:], pattern=[[4, NB]], base=32, channel_multiplier=0)
            pool.iota(iota_i[:], pattern=[[1, N]], base=0, channel_multiplier=0)
            link(pool.memset(diag_col[:], 0.0))
            link(pool.affine_select(out=ident[:], in_=ident[:], compare_op=ALU.not_equal, fill=1.0, base=0,
                                    pattern=[[-1, P]], channel_multiplier=1))
            pool.affine_select(out=upper[:], in_=upper[:], compare_op=ALU.is_gt, fill=0.0, base=0,
                               pattern=[[1, P]], channel_multiplier=-1)
            pool.affine_select(out=before[:], in_=before[:], compare_op=ALU.is_gt, fill=0.0, base=0,
                               pattern=[[1, NE], [-1, NE]], channel_multiplier=0)
            pool.affine_select(out=after[:], in_=after[:], compare_op=ALU.is_gt, fill=0.0, base=0,
                               pattern=[[-1, NE], [1, NE]], channel_multiplier=0)
            pool.affine_select(out=diag_col[:], in_=diag_col[:], compare_op=ALU.not_equal, fill=1.0, base=0,
                               pattern=[[-P, T], [1, N]], channel_multiplier=-1)
            pool.tensor_copy(iota[:], iota_i[:])
            pool.tensor_copy(batch_e[:], batch_i[:])
            link(pool.tensor_scalar(diag_w[:], ident[:], 2.0 ** (30 - 127), None, ALU.mult))
            pool.memset(negmax[:], 0.0).then_inc(consts, 1)
            pool.wait_ge(edge_step, 2)
            pool.tensor_copy(keyb[:, 0:24, :], edge[:, 3, 0:24].unsqueeze(2).to_broadcast([P, 24, P])
                             ).then_inc(keyb_ready, 1)
            pool.tensor_copy(keyb[:, 24:NB, :], edge[:, 3, 24:NB].unsqueeze(2).to_broadcast([P, 24, P])
                             ).then_inc(keyb_ready, 1)
            for n in range(2):
                pool.wait_ge(norm_step, (n + 1) * 10)
                pool.tensor_tensor(rstd[:], veps[:], mhalf[:], ALU.pow).then_inc(rstd_made, 1)
            pool.wait_ge(route_step, 11)
            for e in range(NE):
                ins = pool.tensor_copy(cwx[e], cw[:, :, e].unsqueeze(2).to_broadcast([P, T, P]))
            ins.then_inc(cwx_ready, 1)

        @block.tensor
        def _(pe):
            def turn3(c, out_bank_, srcs):
                for j in range(3):
                    mm = pe.transpose(out_bank_[:, P * j:P * (j + 1)], srcs(j), ident[:])
                mm.then_inc(t3_turned, 1)

            def layer_norm_turns(c0):
                for t in range(T):
                    pe.wait_ge(xn_ready, T * (1 if c0 else 0) + t + 1)
                for k in range(KD):
                    c = c0 + k
                    if c >= 3:
                        pe.wait_ge(t3_split, c - 2)
                    turn3(c, bank[4 + k % 3], lambda j: xn[:, j, P * k:P * (k + 1)])

            def turn_w(it, k, first=False):
                pe.wait_ge(raw_in[k], 16 * (it + 1))
                for half in range(2):
                    if not first:
                        pe.wait_ge(w_lo, 12 * it + (2 * k - 1 + half))
                    for j in range(4):
                        kk = 4 * half + j
                        mm = pe.transpose(turn_bank[half][:, P * j:P * (j + 1)],
                                          raw[k][:, P * kk:P * (kk + 1)], ident[:])
                    mm.then_inc(w_turned, 1)

            def product(acc, w, act, ks, last):
                for k in ks:
                    for wi, ai in ((0, 0), (0, 1), (1, 0)):
                        mm = pe.matmul(acc, w[wi][:, k, :], act[ai][:, k, :],
                                       start=(k == 0 and wi == 0 and ai == 0),
                                       stop=(k == KD - 1 and wi == 1))
                if last:
                    mm.then_inc(mm_done, 1)

            def key_turns(n):
                pe.wait_ge(keyb_ready, 1 if n < 6 else 2)
                if n >= 2:
                    pe.wait_ge(keys_compared, n - 1)
                for j in range(4):
                    mm = pe.transpose(score_bank[n % 2][:, P * j:P * (j + 1)], keyb[:, 4 * n + j, :], ident[:])
                mm.then_inc(keys_turned, 1)

            def diagonal(start):
                for t in range(T):
                    mm = pe.matmul(edge_bank[t][:, 0:N], diag_w[:], diag_col[:, t, :], start=start, stop=not start)
                if not start:
                    mm.then_inc(edges_summed, 1)

            def add_batch(it, n):
                pe.wait_ge(oh_ready, 16 * it + (n - 15))
                for t in range(T):
                    mm = pe.matmul(edge_bank[t][:, 0:N], oh_src[n % OH][:, P * t:P * (t + 1)], oh_dst[n % OH][:],
                                   start=False, stop=False)
                mm.then_inc(oh_used, 1)

            pe.wait_ge(consts, 1)
            pe.wait_ge(edges_f_ready, 1)
            for j in range(4):
                mm = pe.transpose(bank[7][:, 64 * j:64 * j + NB], edges_f[:, j, :], ident[0:NB, 0:NB])
            mm.then_inc(edges_turned, 1)
            pe.wait_ge(bias_in, 16 * 7)
            pe.transpose(bank[3][:, 0:7 * KD], bias_rows[:], ident[0:7 * KD, 0:7 * KD]).then_inc(bias_turned, 1)
            layer_norm_turns(0)
            turn_w(0, 0, first=True)

            pe.wait_ge(t3_split, KD)
            for k in range(6):
                turn_w(0 if k < 5 else 1, (k + 1) % 6)
                pe.wait_ge(w_lo, 2 * k + 2)
                if k >= 2:
                    pe.wait_ge(y_hi, k - 1)
                    pe.wait_ge(y_ready, k - 1)
                product(acc_bank[k % 2][:, 0:N], wb[k % 3], xt, range(KD), True)
                key_turns(2 * k)
                key_turns(2 * k + 1)
            pe.wait_ge(keys_compared, NB // 4)
            diagonal(True)
            per_unit = [3, 3, 3, 3, 2, 2]
            with pe.Fori(1, 4) as it:
                n = 0
                for k in range(6):
                    turn_w(it if k < 5 else it + 1, (k + 1) % 6)
                    pe.wait_ge(w_lo, 12 * it + (2 * k + 2))
                    pe.wait_ge(y_hi, 6 * it + (k - 1))
                    pe.wait_ge(y_ready, 6 * it + (k - 1))
                    product(acc_bank[k % 2][:, 0:N], wb[k % 3], xt, range(KD), True)
                    for _ in range(per_unit[k]):
                        add_batch(it, n)
                        n += 1
            diagonal(False)

            def att_step(r, par, k, scores, tail, first):
                a = 6 * r + (k - 6)
                tp = 1 - par
                if k == 0 and scores:
                    c = turn_count(r, "V", first)
                    pe.wait_ge(y_ready, 3 * r + U_INNER)
                    pe.wait_ge(t3_split, c)
                    turn3(c, t3_bank, lambda j: yv[:, P * j:P * (j + 1)])
                if scores:
                    hh, t = k // 3, k % 3
                    lo, hi = DH * hh, DH * (hh + 1)
                    if k < 2:
                        pe.wait_ge(y_split, 2 * r + U_INNER)
                    if not (first and k < 2):
                        pe.wait_ge(masked_max, a - 1)
                    for n, (qi, ki) in enumerate(((0, 0), (0, 1), (1, 0))):
                        mm = pe.matmul(score_bank[k % 2][:, 0:N], q2[par][qi][lo:hi, P * t:P * (t + 1)],
                                       k2[par][ki][lo:hi, :], start=(n == 0), stop=(n == 2))
                    mm.then_inc(scored, 1)
                if (k == 0 and tail) or (k > 0 and scores):
                    c = turn_count(r, f"P{(k - 1) % 6}", first)
                    pe.wait_ge(prob_ready, a)
                    pe.wait_ge(t3_split, c)
                    turn3(c, t3_bank, lambda j: probs[(k - 1) % 2][:, P * j:P * (j + 1)])
                if (k < 2 and tail) or (k >= 2 and scores):
                    kk = (k - 2) % 6
                    vb = v2[tp if k < 2 else par]
                    hh = kk // 3
                    c = turn_count(r, f"P{kk}", first) if k >= 2 else None
                    if k >= 2:
                        pe.wait_ge(t3_split, c + 1)
                    elif k == 1:
                        pe.wait_ge(t3_split, turn_count(r, "P5", False) + 1)
                    else:
                        pe.wait_ge(t3_split, c_base(r))
                    if not (first and k == 2):
                        pe.wait_ge(att_ready, a - 2)
                    n = 0
                    for j in range(T):
                        for pi, vi in ((0, 0), (0, 1), (1, 0)):
                            mm = pe.matmul(pv_bank[:, 0:DH], pt[k % 2][pi][:, j, :],
                                           vb[vi][:, j, DH * hh:DH * (hh + 1)], start=(n == 0), stop=(n == 8))
                            n += 1
                    mm.then_inc(pv_done, 1)
                if k == 3 and tail:
                    c = turn_count(r, "O", False)
                    pe.wait_ge(att_ready, 6 * r - 6)
                    pe.wait_ge(t3_split, c)
                    turn3(c, t3_bank, lambda j: att[tp][:, j, :])

            def inner_phase(r, it, i, first, att_on, tail):
                for m, n in enumerate("qkv"):
                    k6 = 3 * i + m
                    turn_w(it if k6 < 5 else it + 1, (k6 + 1) % 6)
                    pe.wait_ge(w_lo, 12 * it + (2 * k6 + 2))
                    if first:
                        pe.wait_ge(y_split, U_INNER - 4 + 2 * m)
                    pe.wait_ge(y_ready, 6 * it + (k6 - 1))
                    pe.wait_ge(y_hi, 2 * r + (U_INNER + (m == 2)) if not (first and m == 0) else U_INNER - 1)
                    acc = acc_bank[(i + m) % 2][:, 0:N]
                    product(acc, wb[m], proj[n], range(0, 3), False)
                    if att_on:
                        att_step(r, 1 - i, 2 * m, True, tail, not tail)
                    product(acc, wb[m], proj[n], range(3, 6), False)
                    if att_on:
                        att_step(r, 1 - i, 2 * m + 1, True, tail, not tail)
                    product(acc, wb[m], proj[n], range(6, KD), True)

            inner_phase(0, 4, 0, True, False, False)
            pe.wait_ge(mask_ready, 1)
            inner_phase(1, 4, 1, False, True, False)
            with pe.Fori(5, 8) as it:
                for i in range(2):
                    inner_phase(2 * it + (i - 8), it, i, False, True, True)
            for k in range(6):
                att_step(8, 1, k, True, True, False)
            for k in range(4):
                att_step(9, 0, k, False, True, False)

            def out_turn(r):
                c = C_OUT + r
                pe.wait_ge(y_ready, U_OUT + r + 1)
                pe.wait_ge(t3_split, c)
                turn3(c, t3_bank, lambda j: ybuf[r % 2][:, P * j:P * (j + 1)])

            pe.wait_ge(t3_split, C_OUT)
            for r in range(KD):
                u = U_OUT + r
                if r < KD - 1:
                    turn_w((u + 1) // 6, (u + 1) % 6)
                pe.wait_ge(w_lo, 2 * u + 2)
                pe.wait_ge(y_ready, u - 1)
                acc = acc_bank[u % 2][:, 0:N]
                product(acc, wb[u % 3], ot, range(4), False)
                if r >= 1:
                    out_turn(r - 1)
                product(acc, wb[u % 3], ot, range(4, KD), True)
            pe.wait_ge(gate_in, 16)
            for k in range(KD):
                mm = pe.transpose(bank[7][:, NE * k:NE * (k + 1)], gate_n[:, P * k:P * (k + 1)], ident[0:NE, 0:NE])
            mm.then_inc(gate_turned, 1)
            out_turn(KD - 1)
            layer_norm_turns(C_LN2)

            pe.wait_ge(t3_split, C_LN2 + KD)
            pe.wait_ge(gate_split, 1)
            for t in range(T):
                n = 0
                for k in range(KD):
                    for xi, gi in ((0, 0), (0, 1), (1, 0)):
                        mm = pe.matmul(bank[7][:, 64 + NE * t:64 + NE * (t + 1)], xt[xi][:, k, P * t:P * (t + 1)],
                                       gt[gi][:, k, :], start=(n == 0), stop=(n == 3 * KD - 1))
                        n += 1
            mm.then_inc(logits_done, 1)

            def up(s, which):
                pe.wait_ge(f_lo, f_w1(s) + which + 1)
                if not (isinstance(s, int) and s == 0):
                    pe.wait_ge(gated, 2 * s - 1 + which)
                w = wb[which]
                for k in range(KD):
                    for wi, ai in ((0, 0), (0, 1), (1, 0)):
                        mm = pe.matmul(bank[which][:, 0:N], w[wi][:, k, :], xt[ai][:, k, :],
                                       start=(k == 0 and wi == 0 and ai == 0), stop=(k == KD - 1 and wi == 1))
                mm.then_inc(f_used, 1)

            def down(s, par, first=False, last=False):
                pe.wait_ge(f_lo, f_w2(s) + 1)
                pe.wait_ge(hid_split, s + 1)
                w = [wb[2][i][:].rearrange("p k c -> p (k c)") for i in range(2)]
                for t in range(T):
                    for half in range(2):
                        for n, (hi_, wi) in enumerate(((0, 0), (0, 1), (1, 0))):
                            mm = pe.matmul(out_bank[2 * t + half][:], ht[par][hi_][:, P * t:P * (t + 1)],
                                           w[wi][:, 512 * half:512 * (half + 1)],
                                           start=(first and n == 0), stop=(last and n == 2))
                        if last:
                            mm.then_inc(tile_done, 1)
                if not last:
                    mm.then_inc(f_used, 1)

            up(0, 0)
            up(0, 1)
            pe.wait_ge(cwx_ready, 1)
            for e in range(NE):
                for t in range(T):
                    mm = pe.transpose(bank[2 + e][:, P * t:P * (t + 1)], cwx[e][:, t, :], ident[:])
                mm.then_inc(cw_turned, 1)
            up(1, 0)
            up(1, 1)
            pe.wait_ge(cw_ready, NE)
            down(0, 0, first=True)
            with pe.Fori(0, FULL) as i:
                for e in range(NE):
                    s = 4 * i + (2 + e)
                    up(s, 0)
                    up(s, 1)
                    down(s - 1, (e + 1) % 2)
            down(NS - 1, 1, last=True)

        @block.scalar
        def _(act):
            act.dma_start(edges_i[:, 0, :], src_d.rearrange("(b p) -> b p", p=P)).then_inc(edges_in, 16)
            act.dma_start(edges_i[:, 1, :], dst_d.rearrange("(b p) -> b p", p=P)).then_inc(edges_in, 16)
            act.dma_start(edges_i[:, 2, :], etype_d.rearrange("(b p) -> b p", p=P)).then_inc(edges_in, 16)
            act.dma_start(etw[:], etw_d.partition_broadcast(P)).then_inc(etw_in, 16)
            for n, b in enumerate((bq, bk, bv, biq, bik, biv, bo)):
                act.dma_start(bias_rows[KD * n:KD * (n + 1), :], b.rearrange("(r p) -> r p", p=P)).then_inc(bias_in, 16)

            def split_turn(c, hi_count, src, dst):
                act.wait_ge(t3_turned, c + 1)
                act.activation(dst, src[:, 0:N], ACT.Copy).then_inc(t3_hi, 1)

            def w_halves(it, k, b, wait_mm):
                for half in range(2):
                    if half == 0 and wait_mm is not None:
                        act.wait_ge(mm_done, wait_mm)
                    act.wait_ge(w_turned, 12 * it + (2 * k + half + 1))
                    act.activation(wb[b][0][:, 4 * half:4 * half + 4, :],
                                   turn_bank[half][:].rearrange("p (k c) -> p k c", k=4), ACT.Copy,
                                   scale=W_SCALE).then_inc(w_hi, 1)

            act.wait_ge(soft_a, 1)
            act.activation(sp_b[:], sp_a[:], ACT.Exp, scale=-1.0).then_inc(soft_b, 1)
            act.wait_ge(soft_b, 1)
            act.activation(sp_c[:], sp_b[:], ACT.Ln, bias=1.0).then_inc(soft_b, 1)

            for k in range(KD):
                split_turn(k, k, bank[4 + k % 3], xt[0][:, k, :])
            w_halves(0, 0, 0, None)

            def y_part(it, k, n, b, dst, count, scale):
                act.wait_ge(mm_done, 6 * it + (k + 1))
                act.activation(dst, acc_bank[k % 2][:, 0:N], ACT.Identity, bias=b, scale=scale).then_inc(y_hi, 1)

            act.wait_ge(bias_ready, 1)
            for k in range(6):
                if k < 5:
                    w_halves(0, k + 1, (k + 1) % 3, k - 1 if k >= 2 else None)
                else:
                    w_halves(1, 0, 0, k - 1)
                n, i = k // 2, k % 2
                y_part(0, k, n, bias[:, n, i:i + 1], proj["qkv"[n]][0][:, i, :], k + 1, W_BACK)
            with act.Fori(1, 4) as it:
                for k in range(6):
                    w_halves(it if k < 5 else it + 1, (k + 1) % 6, (k + 1) % 3, 6 * it + (k - 1))
                    n, i = k // 2, k % 2
                    y_part(it, k, n, bias[:, n, ds(2 * it + i, 1)], proj["qkv"[n]][0][:, 2 * it + i, :],
                           6 * it + (k + 1), W_BACK)

            def att_step(r, par, k, scores, tail, first):
                a = 6 * r + (k - 6)
                tp = 1 - par
                if k == 0 and scores:
                    c = turn_count(r, "V", first)
                    act.wait_ge(t3_turned, c + 1)
                    act.activation(v2[par][0][:].rearrange("p t c -> p (t c)"), t3_bank[:, 0:N],
                                   ACT.Copy).then_inc(t3_hi, 1)
                if (k == 0 and tail) or (k > 0 and scores):
                    c = turn_count(r, f"P{(k - 1) % 6}", first)
                    if not (first and k < 3):
                        act.wait_ge(pv_done, a - 2)
                    act.wait_ge(t3_turned, c + 1)
                    act.activation(pt[k % 2 ^ 1][0][:].rearrange("p t c -> p (t c)"), t3_bank[:, 0:N],
                                   ACT.Copy).then_inc(t3_hi, 1)
                if scores:
                    act.wait_ge(masked_max, a + 1)
                    act.activation(probs[k % 2][:], masked[k % 2][:], ACT.Exp, scale=-1.0,
                                   bias=negmax[:, k:k + 1], accum_out=rowsum[:, k:k + 1]).then_inc(prob_ready, 1)
                if k == 3 and tail:
                    c = turn_count(r, "O", False)
                    act.wait_ge(t3_turned, c + 1)
                    act.activation(ot[0][:, r - 2, :], t3_bank[:, 0:N], ACT.Copy).then_inc(t3_hi, 1)

            def inner_phase(r, it, i, att_on, tail):
                for m in range(3):
                    k6 = 3 * i + m
                    w_halves(it if k6 < 5 else it + 1, (k6 + 1) % 6, (m + 1) % 3, 6 * it + (k6 - 1))
                    if att_on:
                        att_step(r, 1 - i, 2 * m, True, tail, not tail)
                        att_step(r, 1 - i, 2 * m + 1, True, tail, not tail)
                    if m == 0:
                        y_part(it, k6, 3, biasq[:, ds(r, 1)], q2[i][0][:], None, -0.125 * W_BACK)
                    elif m == 1:
                        y_part(it, k6, 4, bias[:, 4, ds(r, 1)], k2[i][0][:], None, W_BACK)

            inner_phase(0, 4, 0, False, False)
            act.wait_ge(mask_ready, 1)
            act.dma_start(gate_n, gate_w[0:NE, :]).then_inc(gate_in, 16)
            inner_phase(1, 4, 1, True, False)
            with act.Fori(5, 8) as it:
                for i in range(2):
                    inner_phase(2 * it + (i - 8), it, i, True, True)
            for k in range(6):
                att_step(8, 1, k, True, True, False)
            for k in range(4):
                att_step(9, 0, k, False, True, False)
            for r in range(KD - 1):
                u = U_OUT + r + 1
                w_halves(u // 6, u % 6, u % 3, u - 2)

            def f_part(slot, landed, b, wait):
                act.wait_ge(raw_in[slot], landed)
                if wait is not None:
                    act.wait_ge(*wait)
                act.activation(wb[b][0][:].rearrange("p k c -> p (k c)"), raw[slot][:], ACT.Copy,
                               scale=W_SCALE).then_inc(f_hi, 1)

            f_part(0, w1_landed(0, 0, 0), 0, (mm_done, U_ALL - 1))
            f_part(1, w1_landed(0, 0, 1), 1, (mm_done, U_ALL))
            act.wait_ge(gate_turned, 1)
            act.activation(gt[0][:].rearrange("p k e -> p (k e)"), bank[7][:, 0:NE * KD], ACT.Copy,
                           scale=W_SCALE).then_inc(gate_hi, 1)
            for k in range(KD):
                split_turn(C_LN2 + k, 0, bank[4 + k % 3], xt[0][:, k, :])
            act.wait_ge(route_step, 3)
            act.activation(pr[:], lg[:], ACT.Exp).then_inc(route_exp, 1)

            def step(s, s_half, par, nxt):
                b = par
                if nxt:
                    nh = s_half + (1 if par else 0)
                    f_part(w1_slot[1 - par], w1_landed(nh, 1 - par, 0), 0, (f_used, f_w1(s) + 1))
                act.wait_ge(f_used, f_w1(s) + 1)
                if not (isinstance(s, int) and s < 2):
                    act.wait_ge(gated, 2 * s - 3)
                act.activation(sig[b], bank[0][:, 0:N], ACT.Sigmoid, scale=W_BACK).then_inc(sig_ready, 1)
                if nxt:
                    f_part(w1_slot[1 - par] + 1, w1_landed(nh, 1 - par, 1), 1, (f_used, f_w3(s) + 1))
                act.wait_ge(hid_ready, s + 1)
                if not (isinstance(s, int) and s < 2):
                    act.wait_ge(f_used, f_w2(s - 2) + 1)
                act.activation(ht[b][0], hid[b], ACT.Copy).then_inc(hid_hi, 1)
                wait = (f_used, f_w2(s - 1) + 1) if not (isinstance(s, int) and s == 0) else (mm_done, U_ALL - 2)
                f_part(w2_slot[par], w2_landed(s_half, par), 2, wait)

            step(0, 0, 0, True)
            step(1, 0, 1, True)
            with act.Fori(0, FULL - 1) as i:
                for e in range(NE):
                    step(4 * i + (2 + e), 2 * i + (1 + e // 2), e % 2, True)
            for e in range(NE):
                step(4 * (FULL - 1) + 2 + e, 2 * (FULL - 1) + 1 + e // 2, e % 2, e < NE - 1)

        @block.vector
        def _(dve):
            counts = {}

            def link(ins, s):
                counts[s] = counts.get(s, 0) + 1
                ins.then_inc(s, 1)
                dve.wait_ge(s, counts[s])

            def layer_norm(n, wait_x):
                for t in range(T):
                    if wait_x:
                        dve.wait_ge(x_in[t], 16)
                    for h in range(2):
                        counts[norm_step] = counts.get(norm_step, 0) + 1
                        dve.bn_stats(stats[:, t, h, :], x[:, t, 512 * h:512 * (h + 1)]).then_inc(norm_step, 1)
                dve.wait_ge(norm_step, 10 * n + 6)
                for t in range(T):
                    dve.bn_aggr(mv[:, t, :], stats[:, t].rearrange("p h s -> p (h s)")).then_inc(norm_step, 1)
                dve.wait_ge(norm_step, 10 * n + 9)
                dve.tensor_scalar(veps[:], mv[:, :, 1], EPS, None, ALU.add).then_inc(norm_step, 1)
                counts[norm_step] = 10 * (n + 1)
                dve.wait_ge(rstd_made, n + 1)
                for t in range(T):
                    dve.tensor_scalar(xn[:, t, :], x[:, t, :], mv[:, t, 0:1], rstd[:, t:t + 1],
                                      ALU.subtract, ALU.mult).then_inc(xn_ready, 1)

            def lo_of_turn(c, hi_count, src, hi_part, lo_part):
                dve.wait_ge(t3_hi, hi_count)
                dve.tensor_tensor(lo_part, src, hi_part, ALU.subtract).then_inc(t3_split, 1)

            def w_halves(it, k, b):
                for half in range(2):
                    dve.wait_ge(w_hi, 12 * it + (2 * k + half + 1))
                    part = slice(4 * half, 4 * half + 4)
                    dve.scalar_tensor_tensor(out=wb[b][1][:, part, :],
                                             in0=turn_bank[half][:].rearrange("p (k c) -> p k c", k=4),
                                             scalar=W_SCALE, in1=wb[b][0][:, part, :],
                                             op0=ALU.mult, op1=ALU.subtract).then_inc(w_lo, 1)

            dve.wait_ge(edges_in, 48)
            dve.tensor_copy(edges_f[:, 0, :], edges_i[:, 0, :])
            dve.tensor_copy(edges_f[:, 1, :], edges_i[:, 1, :])
            link(dve.tensor_scalar(edges_f[:, 3, :], edges_i[:, 2, :], 0.0, 4.0, ALU.is_equal, ALU.mult), mask_step)
            link(dve.scalar_tensor_tensor(out=edges_f[:, 2, :], in0=edges_i[:, 2, :], scalar=-1.0,
                                          in1=edges_f[:, 3, :], op0=ALU.add, op1=ALU.add), mask_step)
            dve.scalar_tensor_tensor(out=edges_f[:, 3, :], in0=edges_i[:, 0, :], scalar=float(N),
                                     in1=edges_i[:, 1, :], op0=ALU.mult, op1=ALU.add).then_inc(edges_f_ready, 1)
            dve.wait_ge(etw_in, 16)
            link(dve.tensor_scalar(sp_c[:], etw[:], -1.0, None, ALU.mult), mask_step)
            dve.tensor_tensor(sp_a[:], etw[:], sp_c[:], ALU.max).then_inc(soft_a, 1)
            dve.wait_ge(edges_turned, 1)
            dve.tensor_copy(edge[:, 3, :], bank[7][:, 192:192 + NB]).then_inc(edge_step, 1)
            dve.tensor_copy(edge[:, 0:3, :], bank[7][:, 0:192].rearrange("p (j b) -> p j b", j=3)[:, :, 0:NB]
                            ).then_inc(edge_step, 1)

            dve.wait_ge(bias_turned, 1)
            dve.tensor_copy(bias[:].rearrange("p n r -> p (n r)"), bank[3][:, 0:7 * KD]).then_inc(bias_ready, 1)
            dve.wait_ge(bias_ready, 1)
            layer_norm(0, True)
            for k in range(KD):
                lo_of_turn(k, k + 1, bank[4 + k % 3][:, 0:N], xt[0][:, k, :], xt[1][:, k, :])
            w_halves(0, 0, 0)
            link(dve.tensor_scalar(biasq[:], bias[:, 3, :], -0.125, None, ALU.mult), mask_step)

            def y_part(it, k, b, y, scale, hi_count=None):
                if hi_count is None:
                    dve.wait_ge(mm_done, 6 * it + (k + 1))
                else:
                    dve.wait_ge(y_hi, hi_count)
                dve.tensor_scalar(y, acc_bank[k % 2][:, 0:N], scale, b, ALU.mult, ALU.add).then_inc(y_ready, 1)

            def y_lo(u1, hi_count, y, hi_part, lo_part):
                dve.wait_ge(y_ready, u1)
                dve.wait_ge(y_hi, hi_count)
                dve.tensor_tensor(lo_part, y, hi_part, ALU.subtract).then_inc(y_split, 1)

            def compare_keys(n):
                dve.wait_ge(keys_turned, n + 1)
                if n >= 2:
                    dve.wait_ge(keys_compared, n - 1)
                for j in range(4):
                    b = 4 * n + j
                    ins = dve.scalar_tensor_tensor(out=same[:, P * (4 * (n % 2) + j):P * (4 * (n % 2) + j + 1)], in0=score_bank[n % 2][:, P * j:P * (j + 1)],
                                                   scalar=edge[:, 3, b:b + 1], in1=upper[:], op0=ALU.is_equal,
                                                   op1=ALU.mult, accum_out=later[:, b:b + 1])
                ins.then_inc(keys_compared, 1)

            for k in range(6):
                w_halves(0 if k < 5 else 1, (k + 1) % 6, (k + 1) % 3)
                compare_keys(2 * k)
                compare_keys(2 * k + 1)
                n, i = k // 2, k % 2
                y_part(0, k, bias[:, n, i:i + 1], ybuf[k % 2][:], W_BACK, k + 1)
                y_lo(k + 1, k + 1, ybuf[k % 2][:], proj["qkv"[n]][0][:, i, :], proj["qkv"[n]][1][:, i, :])

            dve.wait_ge(keys_compared, NB // 4)
            link(dve.tensor_scalar(keep[:], later[:], 0.5, None, ALU.is_lt), mask_step)
            link(dve.tensor_tensor(expo[:], edge[:, 2, :], batch_e[:], ALU.add), mask_step)
            link(dve.tensor_scalar(val_i[:], expo[:], float(2 ** 23), None, ALU.mult), mask_step)
            link(dve.tensor_tensor(val[:], val_i[:].bitcast(F32), keep[:], ALU.mult), mask_step)

            def one_hots(it, n):
                b = 16 * it + (n - 16)
                if n >= OH:
                    dve.wait_ge(oh_used, b - (OH - 1))
                else:
                    dve.wait_ge(oh_used, b - (OH - 1)) if not isinstance(it, int) else None
                dve.tensor_scalar(oh_src[n % OH][:], iota[:], edge[:, 0, ds(b, 1)], None, ALU.is_equal)
                dve.tensor_scalar(oh_dst[n % OH][:], iota[:], edge[:, 1, ds(b, 1)], val[:, ds(b, 1)],
                                  ALU.is_equal, ALU.mult).then_inc(oh_ready, 1)

            per_unit = [3, 3, 3, 3, 2, 2]

            def round_(it, static):
                n = 0
                for k in range(6):
                    w_halves(it if k < 5 else it + 1, (k + 1) % 6, (k + 1) % 3)
                    for _ in range(per_unit[k]):
                        if static and n < OH:
                            b = n
                            dve.tensor_scalar(oh_src[n % OH][:], iota[:], edge[:, 0, b:b + 1], None, ALU.is_equal)
                            dve.tensor_scalar(oh_dst[n % OH][:], iota[:], edge[:, 1, b:b + 1], val[:, b:b + 1],
                                              ALU.is_equal, ALU.mult).then_inc(oh_ready, 1)
                        else:
                            one_hots(it, n)
                        n += 1
                    m, i = k // 2, k % 2
                    y_part(it, k, bias[:, m, ds(2 * it + i, 1)], ybuf[k % 2][:], W_BACK, 6 * it + (k + 1))
                    y_lo(6 * it + (k + 1), 6 * it + (k + 1), ybuf[k % 2][:], proj["qkv"[m]][0][:, 2 * it + i, :],
                         proj["qkv"[m]][1][:, 2 * it + i, :])

            round_(1, True)
            with dve.Fori(2, 4) as it:
                round_(it, False)

            def read_edge_sums():
                dve.wait_ge(edges_summed, 1)
                for t in range(T):
                    ins = dve.tensor_copy(esum[:, t, :], edge_bank[t][:, 0:N])
                link(ins, mask_step)
                dve.wait_ge(soft_b, 2)
                link(dve.scalar_tensor_tensor(out=nsoft[:], in0=etw[:], scalar=0.0, in1=sp_c[:],
                                              op0=ALU.max, op1=ALU.add), mask_step)
                link(dve.tensor_scalar(nsoft[:], nsoft[:], -1.0, None, ALU.mult), mask_step)
                flat = lambda a: a[:].rearrange("p t n -> p (t n)")
                link(dve.tensor_scalar(flat(etyp), flat(esum).bitcast(I32), 23, 3,
                                       ALU.logical_shift_right, ALU.bitwise_and), mask_step)
                link(dve.tensor_scalar(flat(negmask), flat(esum), 0.0, ABSENT, ALU.is_le, ALU.mult), mask_step)
                for k in range(4):
                    link(dve.tensor_scalar(flat(mtmp), flat(etyp), float(k), nsoft[:, k:k + 1],
                                           ALU.is_equal, ALU.mult), mask_step)
                    link(dve.tensor_tensor(flat(negmask), flat(negmask), flat(mtmp), ALU.add), mask_step)
                dve.tensor_scalar(negmax[:], negmax[:], 1.0, None, ALU.mult).then_inc(mask_ready, 1)

            def att_step(r, par, k, scores, tail, first):
                a = 6 * r + (k - 6)
                tp = 1 - par
                if k == 0 and scores:
                    c = turn_count(r, "V", first)
                    lo_of_turn(c, c + 1, t3_bank[:, 0:N], v2[par][0][:].rearrange("p t c -> p (t c)"),
                               v2[par][1][:].rearrange("p t c -> p (t c)"))
                if scores:
                    dve.wait_ge(scored, a + 1)
                if (k == 0 and tail) or (k > 0 and scores):
                    kk = (k - 1) % 6
                    dve.wait_ge(prob_ready, a)
                    dve.reciprocal(rinv[:, kk:kk + 1], rowsum[:, kk:kk + 1]).then_inc(inv_ready, 1)
                if scores:
                    dve.tensor_tensor_reduce(out=masked[k % 2][:], in0=score_bank[k % 2][:, 0:N],
                                             in1=negmask[:, k % 3, :], scale=1.0, scalar=3.0e38, op0=ALU.add,
                                             op1=ALU.min, accum_out=negmax[:, k:k + 1]).then_inc(masked_max, 1)
                if (k == 0 and tail) or (k > 0 and scores):
                    c = turn_count(r, f"P{(k - 1) % 6}", first)
                    b = k % 2 ^ 1
                    lo_of_turn(c, c + 1, t3_bank[:, 0:N], pt[b][0][:].rearrange("p t c -> p (t c)"),
                               pt[b][1][:].rearrange("p t c -> p (t c)"))
                if (k < 2 and tail) or (k >= 2 and scores):
                    kk = (k - 2) % 6
                    dve.wait_ge(pv_done, a - 1)
                    dve.wait_ge(inv_ready, a - 1)
                    dve.tensor_scalar(att[tp if k < 2 else par][:, kk % 3, DH * (kk // 3):DH * (kk // 3 + 1)],
                                      pv_bank[:, 0:DH], rinv[:, kk:kk + 1], None, ALU.mult).then_inc(att_ready, 1)
                if k == 3 and tail:
                    c = turn_count(r, "O", False)
                    lo_of_turn(c, c + 1, t3_bank[:, 0:N], ot[0][:, r - 2, :], ot[1][:, r - 2, :])

            def inner_phase(r, it, i, att_on, tail):
                for m in range(3):
                    k6 = 3 * i + m
                    w_halves(it if k6 < 5 else it + 1, (k6 + 1) % 6, (m + 1) % 3)
                    if att_on:
                        att_step(r, 1 - i, 2 * m, True, tail, not tail)
                        att_step(r, 1 - i, 2 * m + 1, True, tail, not tail)
                    u1 = 6 * it + (k6 + 1)
                    if m == 0:
                        y_part(it, k6, biasq[:, ds(r, 1)], ybuf[0][:], -0.125 * W_BACK, 2 * r + (U_INNER + 1))
                        y_lo(u1, 2 * r + (U_INNER + 1), ybuf[0][:], q2[i][0][:], q2[i][1][:])
                    elif m == 1:
                        y_part(it, k6, bias[:, 4, ds(r, 1)], ybuf[1][:], W_BACK, 2 * r + (U_INNER + 2))
                        y_lo(u1, 2 * r + (U_INNER + 2), ybuf[1][:], k2[i][0][:], k2[i][1][:])
                    else:
                        y_part(it, k6, bias[:, 5, ds(r, 1)], yv[:], W_BACK)

            inner_phase(0, 4, 0, False, False)
            read_edge_sums()
            inner_phase(1, 4, 1, True, False)
            with dve.Fori(5, 8) as it:
                for i in range(2):
                    inner_phase(2 * it + (i - 8), it, i, True, True)
            for k in range(6):
                att_step(8, 1, k, True, True, False)
            for k in range(4):
                att_step(9, 0, k, False, True, False)

            def residual(r):
                c = C_OUT + r
                dve.wait_ge(t3_turned, c + 1)
                part = x[:, :, P * r:P * (r + 1)]
                dve.tensor_tensor(part, t3_bank[:, 0:N].rearrange("p (t c) -> p t c", t=T), part,
                                  ALU.add).then_inc(t3_split, 1)

            for r in range(KD):
                u = U_OUT + r
                if r < KD - 1:
                    w_halves((u + 1) // 6, (u + 1) % 6, (u + 1) % 3)
                if r >= 1:
                    residual(r - 1)
                y_part(u // 6, u % 6, bias[:, 6, r:r + 1], ybuf[r % 2][:], W_BACK)

            def f_part(f1, slot, b):
                dve.wait_ge(f_hi, f1)
                dve.scalar_tensor_tensor(out=wb[b][1][:].rearrange("p k c -> p (k c)"), in0=raw[slot][:],
                                         scalar=W_SCALE, in1=wb[b][0][:].rearrange("p k c -> p (k c)"),
                                         op0=ALU.mult, op1=ALU.subtract).then_inc(f_lo, 1)

            residual(KD - 1)
            dve.wait_ge(t3_split, C_LN2)
            f_part(1, 0, 0)
            f_part(2, 1, 1)
            dve.wait_ge(gate_hi, 1)
            dve.scalar_tensor_tensor(out=gt[1][:].rearrange("p k e -> p (k e)"), in0=bank[7][:, 0:NE * KD],
                                     scalar=W_SCALE, in1=gt[0][:].rearrange("p k e -> p (k e)"),
                                     op0=ALU.mult, op1=ALU.subtract).then_inc(gate_split, 1)
            layer_norm(1, False)
            for k in range(KD):
                c = C_LN2 + k
                lo_of_turn(c, c + 1 - KD, bank[4 + k % 3][:, 0:N], xt[0][:, k, :], xt[1][:, k, :])

            dve.wait_ge(logits_done, 1)
            logits = bank[7][:, 64:64 + T * NE].rearrange("p (t e) -> p t e", e=NE)
            spread = lambda a: a.unsqueeze(2).to_broadcast([P, T, NE])
            link(dve.tensor_scalar(lg[:], logits, W_BACK, None, ALU.mult), route_step)
            link(dve.tensor_reduce(lmax[:], lg[:], AX.X, ALU.max), route_step)
            link(dve.tensor_tensor(lg[:], lg[:], spread(lmax[:]), ALU.subtract), route_step)
            dve.wait_ge(route_exp, 1)
            mine = pr[:].unsqueeze(3).to_broadcast([P, T, NE, NE])
            other = pr[:].unsqueeze(2).to_broadcast([P, T, NE, NE])
            dve.tensor_tensor(cmp_a[:], other, mine, ALU.is_ge)
            link(dve.tensor_tensor(cmp_b[:], other, mine, ALU.is_gt), route_step)
            for t in range(T):
                dve.tensor_tensor(cmp_a[:, t], cmp_a[:, t], before[:], ALU.mult)
                ins = dve.tensor_tensor(cmp_b[:, t], cmp_b[:, t], after[:], ALU.mult)
            link(ins, route_step)
            link(dve.tensor_tensor(cmp_a[:], cmp_a[:], cmp_b[:], ALU.add), route_step)
            link(dve.tensor_reduce(rank[:], cmp_a[:], AX.X, ALU.add), route_step)
            link(dve.scalar_tensor_tensor(out=cw[:], in0=rank[:], scalar=1.5, in1=pr[:],
                                          op0=ALU.is_lt, op1=ALU.mult), route_step)
            link(dve.tensor_reduce(csum[:], cw[:], AX.X, ALU.add), route_step)
            link(dve.reciprocal(cinv[:], csum[:]), route_step)
            link(dve.tensor_tensor(cw[:], cw[:], spread(cinv[:]), ALU.mult), route_step)

            def step(s, par, nxt, e, mixed=None):
                b = par
                if nxt:
                    f_part(f_w1(s + 1) + 1, w1_slot[1 - par], 0)
                dve.wait_ge(sig_ready, s + 1)
                dve.scalar_tensor_tensor(out=g1[b], in0=bank[0][:, 0:N], scalar=W_BACK, in1=sig[b],
                                         op0=ALU.mult, op1=ALU.mult).then_inc(gated, 1)
                if nxt:
                    f_part(f_w3(s + 1) + 1, w1_slot[1 - par] + 1, 1)
                dve.wait_ge(f_used, f_w3(s) + 1)
                if mixed is not None:
                    if mixed == 0:
                        for e_ in range(NE):
                            dve.wait_ge(cw_turned, e_ + 1)
                            dve.tensor_copy(cwb[e_], bank[2 + e_][:, 0:N]).then_inc(cw_ready, 1)
                        dve.wait_ge(cw_ready, NE)
                    for h in range(2):
                        rows_ = slice(HALF * h, HALF * (h + 1))
                        ins = dve.scalar_tensor_tensor(out=g3[b][rows_, :], in0=bank[1][rows_, 0:N], scalar=W_BACK,
                                                       in1=cwb[2 * mixed + h][rows_, :], op0=ALU.mult, op1=ALU.mult)
                else:
                    ins = dve.scalar_tensor_tensor(out=g3[b], in0=bank[1][:, 0:N], scalar=W_BACK,
                                                   in1=cwb[e], op0=ALU.mult, op1=ALU.mult)
                ins.then_inc(gated, 1)
                dve.wait_ge(gated, 2 * s + 2)
                dve.tensor_tensor(hid[b], g1[b], g3[b], ALU.mult).then_inc(hid_ready, 1)
                dve.wait_ge(hid_hi, s + 1)
                dve.tensor_tensor(ht[b][1], hid[b], ht[b][0], ALU.subtract).then_inc(hid_split, 1)
                f_part(f_w2(s) + 1, w2_slot[par], 2)

            step(0, 0, True, None, mixed=0)
            step(1, 1, True, None, mixed=1)
            with dve.Fori(0, FULL - 1) as i:
                for e in range(NE):
                    step(4 * i + (2 + e), e % 2, True, e)
            for e in range(NE):
                step(4 * (FULL - 1) + 2 + e, e % 2, e < NE - 1, e)

            for t in range(T):
                for half in range(2):
                    dve.wait_ge(tile_done, 2 * t + half + 1)
                    cols = slice(512 * half, 512 * (half + 1))
                    dve.scalar_tensor_tensor(out=res[:, t, cols], in0=out_bank[2 * t + half][:], scalar=W_BACK,
                                             in1=x[:, t, cols], op0=ALU.mult, op1=ALU.add).then_inc(res_ready, 1)


_INS = ["x", "src", "dst", "edge_type_5", "L0_gnn_edge_type_weights", "L0_gnn_wq", "L0_gnn_bq", "L0_gnn_wk",
        "L0_gnn_bk", "L0_gnn_wv", "L0_gnn_bv", "L0_gnn_wiq", "L0_gnn_biq", "L0_gnn_wik", "L0_gnn_bik",
        "L0_gnn_wiv", "L0_gnn_biv", "L0_gnn_wo", "L0_gnn_bo", "L0_ffn_gate_w", "L0_ffn_w1", "L0_ffn_w2",
        "L0_ffn_w3"]


def kernel(**inputs):
    import numpy as _np
    import concourse.bacc as _bacc
    from concourse import mybir as _mybir
    from concourse.bass_utils import run_bass_kernel_spmd as _run

    nc = _bacc.Bacc("TRN2", target_bir_lowering=False, num_devices=1)
    arrays, args = {}, []
    for name in _INS:
        a = _np.ascontiguousarray(inputs[name])
        arrays[f"in_{name}"] = a
        args.append(nc.dram_tensor(f"in_{name}", a.shape, _mybir.dt.from_np(a.dtype), kind="ExternalInput").ap())
    shape = tuple(inputs["x"].shape)
    args.append(nc.dram_tensor("out_0", shape, F32, kind="ExternalOutput").ap())
    gnn_moe_kernel(nc, *args)
    r = _run(nc, [arrays], core_ids=[0])
    return r.results[0]["out_0"]
```

```python
from contextlib import ExitStack

import concourse.bass as bass
from concourse import mybir

P = 128
F32 = mybir.dt.float32
F16 = mybir.dt.float16
BF16 = mybir.dt.bfloat16
I32 = mybir.dt.int32
ALU = mybir.AluOpType
ACT = mybir.ActivationFunctionType
AX = mybir.AxisListType

ds = bass.ds

W_SCALE = 64.0
W_BACK = 1.0 / W_SCALE
ABSENT = 1.0e30
EPS = 1e-5
SLOTS = 6


def gnn_moe_kernel(nc, x_d, src_d, dst_d, etype_d, etw_d, wq, bq, wk, bk, wv, bv, wiq, biq,
                   wik, bik, wiv, biv, wo, bo, gate_w, w1, w2, w3, out_d):
    N, D = x_d.shape
    T = N // P
    KD = D // P
    E = src_d.shape[0]
    NB = E // P
    DH = 64
    NE = 4
    HID = w1.shape[2]
    FULL = HID // P
    HALF = HID - FULL * P
    NS = NE * HID // P
    assert (N, D, HID, HALF, NS, NB) == (384, 1024, 704, 64, 22, 48)

    def tile_col(e, i):
        return (HALF if e % 2 else 0) + P * i

    with ExitStack() as ctx:
        def sb(name, shape, dt=F32):
            return ctx.enter_context(nc.sbuf_tensor(name, shape, dt))

        def sem(name):
            return ctx.enter_context(nc.semaphore(name))

        bank = [ctx.enter_context(nc.psum_tensor(f"bank{i}", [P, 512], F32)) for i in range(8)]
        turn_bank = bank[0:2]
        acc_bank = bank[2:4]
        score_bank = bank[4:6]
        t3_bank = bank[6]
        pv_bank = bank[7]
        ln_bank = bank[4:8]
        edge_bank = [bank[4], bank[5], bank[7]]
        out_bank = bank[2:8]

        x = sb("x", [P, T, D])
        xn = sb("xn", [P, T, D])
        xt = [sb("xt_hi", [P, KD, N], F16), sb("xt_lo", [P, KD, N], F16)]
        proj = {n: [sb(f"{n}t_hi", [P, KD, N], F16), sb(f"{n}t_lo", [P, KD, N], F16)] for n in "qkv"}
        q2 = [[sb(f"q2_{b}_{h}", [P, N], F16) for h in range(2)] for b in range(2)]
        k2 = [[sb(f"k2_{b}_{h}", [P, N], F16) for h in range(2)] for b in range(2)]
        v2 = [[sb(f"v2_{b}_{h}", [P, T, P], F16) for h in range(2)] for b in range(2)]
        raw = [sb(f"raw{i}", [P, D]) for i in range(SLOTS)]
        wb = [[sb(f"w{b}_{h}", [P, KD, P], F16) for h in range(2)] for b in range(3)]
        ybuf = [sb(f"y{b}", [P, N]) for b in range(2)]
        yv = sb("yv", [P, N])
        bias = sb("bias", [P, 7, KD])
        biasq = sb("biasq", [P, KD])
        bias_rows = sb("bias_rows", [7 * KD, P])
        masked = [sb(f"masked{b}", [P, N]) for b in range(2)]
        probs = [sb(f"probs{b}", [P, N]) for b in range(2)]
        pt = [[sb(f"pt_{b}_{h}", [P, T, P], F16) for h in range(2)] for b in range(2)]
        att = [sb(f"att{b}", [P, T, P]) for b in range(2)]
        negmax = sb("negmax", [P, 6])
        rowsum = sb("rowsum", [P, 6])
        rinv = sb("rinv", [P, 6])
        negmask = sb("negmask", [P, T, N])
        stats = sb("stats", [P, T, KD, 6])
        mv = sb("mv", [P, T, 2])
        veps = sb("veps", [P, T])
        rstd = sb("rstd", [P, T])
        mhalf = sb("mhalf", [P, T])
        ident = sb("ident", [P, P])
        upper = sb("upper", [P, P])
        iota_i = sb("iota_i", [P, N], I32)
        iota = sb("iota", [P, N], F16)
        diag_w = sb("diag_w", [P, P], BF16)
        diag_col = sb("diag_col", [P, T, N], BF16)
        edges_i = sb("edges_i", [NB, 3, P], I32)
        edges_f = sb("edges_f", [NB, 4, P])
        edge = sb("edge", [P, 4, NB])
        batch_i = sb("batch_i", [P, NB], I32)
        batch_e = sb("batch_e", [P, NB])
        keyb = sb("keyb", [P, NB, P])
        ot_room = keyb[:].rearrange("p b c -> p (b c)").bitcast(F16)
        ot = [ot_room[:, KD * N * h:KD * N * (h + 1)].rearrange("p (k n) -> p k n", k=KD) for h in range(2)]
        later = sb("later", [P, NB])
        keep = sb("keep", [P, NB])
        expo = sb("expo", [P, NB])
        val_i = sb("val_i", [P, NB], I32)
        val = sb("val", [P, NB])
        OH = 4
        oh_src = [sb(f"oh_src{i}", [P, N], BF16) for i in range(OH)]
        oh_dst = [sb(f"oh_dst{i}", [P, N], BF16) for i in range(OH)]
        etyp = sb("etyp", [P, T, N], I32)
        type_part = keyb[:].rearrange("p b c -> p (b c)")[:, 0:T * 4 * N].rearrange("p (t k n) -> p t k n", t=T, k=4)
        same = sb("same", [P, 8 * P])
        etw = sb("etw", [P, 4])
        sp_a = sb("sp_a", [P, 4])
        sp_b = sb("sp_b", [P, 4])
        sp_c = sb("sp_c", [P, 4])
        nsoft = sb("nsoft", [P, 4])
        def room(name, half, n):
            flat = proj[name][half][:].rearrange("p k n -> p (k n)").bitcast(F32)
            return [flat[:, N * i:N * (i + 1)] for i in range(n)]

        gate_n = sb("gate_n", [NE, D])
        gt = [sb("gt_hi", [P, KD, NE], F16), sb("gt_lo", [P, KD, NE], F16)]
        lg = sb("lg", [P, T, NE])
        lmax = sb("lmax", [P, T])
        pr = sb("pr", [P, T, NE])
        cmp_a = sb("cmp_a", [P, T, NE, NE])
        cmp_b = sb("cmp_b", [P, T, NE, NE])
        before = sb("before", [P, NE, NE])
        after = sb("after", [P, NE, NE])
        rank = sb("rank", [P, T, NE])
        csum = sb("csum", [P, T])
        cinv = sb("cinv", [P, T])
        cw = sb("cw", [P, T, NE])
        cwx = [a.rearrange("p (t c) -> p t c", t=T) for a in room("q", 0, NE)]
        cwb = room("q", 1, NE)
        sig, g1 = room("k", 0, 4)[0:2], room("k", 0, 4)[2:4]
        g3, hid = room("k", 1, 4)[0:2], room("k", 1, 4)[2:4]
        ht = [[proj["v"][b][:, h, :] for h in range(2)] for b in range(2)]
        res = xn

        x_in = [sem(f"x_in{t}") for t in range(T)]
        edges_in = sem("edges_in")
        bias_in = sem("bias_in")
        bias_turned = sem("bias_turned")
        bias_ready = sem("bias_ready")
        etw_in = sem("etw_in")
        gate_in = sem("gate_in")
        raw_in = [sem(f"raw_in{i}") for i in range(SLOTS)]
        out_done = sem("out_done")
        ident_ready = sem("ident_ready")
        consts = sem("consts")
        pool_step = sem("pool_step")
        norm_step = sem("norm_step")
        norm2_step = sem("norm2_step")
        rstd_made = sem("rstd_made")
        xn_ready = sem("xn_ready")
        edge_step = sem("edge_step")
        edges_f_ready = sem("edges_f_ready")
        edges_turned = sem("edges_turned")
        keyb_ready = sem("keyb_ready")
        keys_turned = sem("keys_turned")
        keys_compared = sem("keys_compared")
        oh_ready = sem("oh_ready")
        oh_used = sem("oh_used")
        edges_summed = sem("edges_summed")
        mask_step = sem("mask_step")
        types_ready = sem("types_ready")
        mask_ready = sem("mask_ready")
        soft_a = sem("soft_a")
        soft_b = sem("soft_b")
        w_turned = sem("w_turned")
        w_hi = sem("w_hi")
        w_lo = sem("w_lo")
        mm_done = sem("mm_done")
        y_ready = sem("y_ready")
        y_hi = sem("y_hi")
        y_split = sem("y_split")
        t3_turned = sem("t3_turned")
        t3_hi = sem("t3_hi")
        t3_split = sem("t3_split")
        scored = sem("scored")
        masked_max = sem("masked_max")
        prob_ready = sem("prob_ready")
        inv_ready = sem("inv_ready")
        pv_done = sem("pv_done")
        att_ready = sem("att_ready")
        gate_turned = sem("gate_turned")
        gate_hi = sem("gate_hi")
        gate_split = sem("gate_split")
        logits_done = sem("logits_done")
        route_step = sem("route_step")
        route_exp = sem("route_exp")
        cwx_ready = sem("cwx_ready")
        cw_turned = sem("cw_turned")
        cw_ready = sem("cw_ready")
        f_hi = sem("f_hi")
        f_lo = sem("f_lo")
        f_used = sem("f_used")
        sig_ready = sem("sig_ready")
        gated = sem("gated")
        hid_ready = sem("hid_ready")
        hid_hi = sem("hid_hi")
        hid_split = sem("hid_split")
        tile_done = sem("tile_done")
        res_ready = sem("res_ready")

        block = ctx.enter_context(nc.Block())

        def flat(a):
            return a[:].rearrange("p t n -> p (t n)")

        keys_per_unit = [0, 2, 2, 2, 3, 3]
        WARM_UP = 24

        U_INNER = 3 * KD
        U_OUT = 6 * KD
        U_ALL = 7 * KD
        C_LN = 2 * T

        def c_base(r):
            return C_LN + 6 + 8 * (r - 2)

        C_OUT = c_base(9) + 2
        C_LN2 = C_OUT + KD

        def turn_count(r, what, first):
            if first:
                return C_LN + turn_order(True).index(what)
            return c_base(r) + turn_order(False, r).index(what)

        def turn_order(first, r=None):
            if first:
                return ["V", "P0", "P1", "P2", "P3", "P4"]
            if isinstance(r, int) and r == 9:
                return ["P5", "O"]
            return ["V", "P5", "P0", "O", "P1", "P2", "P3", "P4"]

        def turn_parity(what, first, r=None):
            return turn_order(first, r).index(what) % 2

        def f_w1(s):
            return 3 * s - 1 if not (isinstance(s, int) and s == 0) else 0

        def f_w3(s):
            return f_w1(s) + 1

        def f_w2(s):
            return 3 * s + (2 if isinstance(s, int) and s == NS - 1 else 4)

        w1_slot = [0, 3]
        w2_slot = [5, 2]

        def slot_count(slot, nth):
            return 16 * (nth + (11 if slot < 2 else 10))

        def w1_landed(s_half, par, w):
            return slot_count(w1_slot[par] + w, s_half + 1)

        def w2_landed(s_half, par):
            return slot_count(w2_slot[par], s_half + 1)

        inner = [(wiq, "q"), (wik, "k"), (wiv, "v")]
        rows = lambda w: w.rearrange("(r p) i -> r p i", p=P)

        @block.sync
        def _(sp):
            for t in range(T):
                sp.dma_start(x[:, t, :], x_d[P * t:P * (t + 1), :]).then_inc(x_in[t], 16)
            outer = [(w, i) for w in (wq, wk, wv) for i in range(2)]
            inner_w = [(w, i) for i in range(2) for w, _ in inner]
            for k, (w, i) in enumerate(outer):
                sp.dma_start(raw[k][:], rows(w)[i]).then_inc(raw_in[k], 16)

            def round_(it, blocks, base):
                for k, (w, i) in enumerate(blocks):
                    sp.wait_ge(w_turned, 12 * it + (2 * k - 10))
                    sp.dma_start(raw[k][:], rows(w)[base + i]).then_inc(raw_in[k], 16)

            with sp.Fori(1, 4) as it:
                round_(it, outer, 2 * it)
            with sp.Fori(4, 8) as it:
                round_(it, inner_w, 2 * it - 8)
            round_(8, [(wo, i) for i in range(6)], 0)
            round_(9, [(wo, i) for i in range(2)], 6)

            def load13(slot, w, e, col):
                dst = raw[slot][:].rearrange("p (k c) -> p k c", k=KD)
                sp.dma_start(dst, w[e].rearrange("(k p) c -> p k c", p=P)[:, :, ds(col, P)]
                             ).then_inc(raw_in[slot], 16)

            for s in range(2):
                for w, slot in ((w1, w1_slot[s]), (w3, w1_slot[s] + 1)):
                    sp.wait_ge(w_turned, 2 * (U_OUT + (6 if slot < 2 else 0) + slot) + 2)
                    dst = raw[slot][:].rearrange("p (k c) -> p k c", k=KD)
                    for half, e, col in ((0, 2 * s, HID - HALF), (1, 2 * s + 1, 0)):
                        sp.dma_start(dst[:, :, HALF * half:HALF * (half + 1)],
                                     w[e].rearrange("(k p) c -> p k c", p=P)[:, :, col:col + HALF]
                                     ).then_inc(raw_in[slot], 16)
            sp.wait_ge(w_turned, 2 * (U_OUT + 5) + 2)
            for half, row in ((0, HID - HALF), (1, 0)):
                sp.dma_start(raw[5][HALF * half:HALF * (half + 1), :], w2[half, row:row + HALF, :]
                             ).then_inc(raw_in[5], 16)

            def step_loads(i, e, first):
                par = e % 2
                s = 4 * i + (2 + e)
                col = P * i + (HALF if par else 0)
                for j, w in enumerate((w1, w3)):
                    sp.wait_ge(f_lo, f_w1(s - 2) + j + 1)
                    load13(w1_slot[par] + j, w, e, col)
                slot = w2_slot[1 - par]
                if first and e == 0:
                    sp.wait_ge(w_turned, 2 * (U_OUT + slot) + 2)
                    for half, row in ((0, HID - HALF), (1, 0)):
                        sp.dma_start(raw[slot][HALF * half:HALF * (half + 1), :],
                                     w2[2 + half, row:row + HALF, :]).then_inc(raw_in[slot], 16)
                    return
                pe_, pi = (NE - 1, i - 1) if e == 0 else (e - 1, i)
                row = P * pi + (HALF if pe_ % 2 else 0)
                sp.wait_ge(f_lo, f_w2(s - 3) + 1)
                sp.dma_start(raw[slot][:], w2[pe_][ds(row, P), :]
                             ).then_inc(raw_in[slot], 16)

            for e in range(NE):
                step_loads(0, e, True)
            with sp.Fori(1, FULL) as i:
                for e in range(NE):
                    step_loads(i, e, False)
            sp.wait_ge(f_lo, f_w2(NS - 3) + 1)
            sp.dma_start(raw[w2_slot[1]][:], w2[NE - 1, HID - P:HID, :]).then_inc(raw_in[w2_slot[1]], 16)

            for t in range(T):
                sp.wait_ge(res_ready, 2 * t + 2)
                sp.dma_start(out_d[P * t:P * (t + 1), :], res[:, t, :]).then_inc(out_done, 16)
            sp.wait_ge(out_done, 16 * T)

        @block.gpsimd
        def _(pool):
            steps = [0]

            def link(ins):
                steps[0] += 1
                ins.then_inc(pool_step, 1)
                pool.wait_ge(pool_step, steps[0])

            pool.memset(ident[:], 0.0)
            link(pool.memset(mhalf[:], -0.5))
            pool.affine_select(out=ident[:], in_=ident[:], compare_op=ALU.not_equal, fill=1.0, base=0,
                               pattern=[[-1, P]], channel_multiplier=1).then_inc(ident_ready, 1)
            pool.memset(upper[:], 1.0)
            pool.memset(before[:], 1.0)
            pool.memset(after[:], 1.0)
            pool.iota(batch_i[:], pattern=[[4, NB]], base=32, channel_multiplier=0)
            link(pool.iota(iota_i[:], pattern=[[1, N]], base=0, channel_multiplier=0))

            def rstd_of(t, step, count):
                pool.wait_ge(step, count)
                pool.tensor_tensor(rstd[:, t:t + 1], veps[:, t:t + 1], mhalf[:, t:t + 1], ALU.pow).then_inc(rstd_made, 1)

            for t in range(T):
                rstd_of(t, norm_step, 4 * t + 4)
            pool.affine_select(out=upper[:], in_=upper[:], compare_op=ALU.is_gt, fill=0.0, base=0,
                               pattern=[[1, P]], channel_multiplier=-1)
            pool.affine_select(out=before[:], in_=before[:], compare_op=ALU.is_gt, fill=0.0, base=0,
                               pattern=[[1, NE], [-1, NE]], channel_multiplier=0)
            pool.affine_select(out=after[:], in_=after[:], compare_op=ALU.is_gt, fill=0.0, base=0,
                               pattern=[[-1, NE], [1, NE]], channel_multiplier=0)
            pool.tensor_copy(batch_e[:], batch_i[:]).then_inc(consts, 1)
            pool.wait_ge(edge_step, 1)
            for n in range(NB // 4):
                pool.tensor_copy(keyb[:, 4 * n:4 * n + 4, :],
                                 edge[:, 3, 4 * n:4 * n + 4].unsqueeze(2).to_broadcast([P, 4, P])
                                 ).then_inc(keyb_ready, 1)
            link(pool.memset(diag_col[:], 0.0))
            pool.affine_select(out=diag_col[:], in_=diag_col[:], compare_op=ALU.not_equal, fill=1.0, base=0,
                               pattern=[[-P, T], [1, N]], channel_multiplier=-1)
            pool.tensor_copy(iota[:], iota_i[:])
            pool.tensor_scalar(diag_w[:], ident[:], 2.0 ** (30 - 127), None, ALU.mult).then_inc(consts, 1)
            for t in range(T):
                pool.wait_ge(types_ready, t + 1)
                for k in range(4):
                    ins = pool.tensor_tensor(negmask[:, t, :], negmask[:, t, :], type_part[:, t, k, :], ALU.add)
                    if k < 3:
                        link(ins)
                ins.then_inc(mask_ready, 1)
            for t in range(T):
                rstd_of(t, norm2_step, KD * T + 2 * (t + 1))
            pool.wait_ge(route_step, 11)
            for e in range(NE):
                ins = pool.tensor_copy(cwx[e], cw[:, :, e].unsqueeze(2).to_broadcast([P, T, P]))
            ins.then_inc(cwx_ready, 1)

        @block.tensor
        def _(pe):
            def turn3(c, out_bank_, srcs):
                for j in range(3):
                    mm = pe.transpose(out_bank_[:, P * j:P * (j + 1)], srcs(j), ident[:])
                mm.then_inc(t3_turned, 1)

            def layer_norm_turns(c0, t):
                pe.wait_ge(xn_ready, (T if c0 else 0) + t + 1)
                for c in (2 * t, 2 * t + 1):
                    if c0 + c >= 4:
                        pe.wait_ge(t3_split, c0 + c - 3)
                    for j in range(4):
                        k = 4 * (c % 2) + j
                        mm = pe.transpose(ln_bank[c % 4][:, P * j:P * (j + 1)], xn[:, t, P * k:P * (k + 1)], ident[:])
                    mm.then_inc(t3_turned, 1)

            def turn_w(it, k, first=False):
                pe.wait_ge(raw_in[k], 16 * (it + 1))
                for half in range(2):
                    if not first:
                        pe.wait_ge(w_lo, 12 * it + (2 * k - 1 + half))
                    for j in range(4):
                        kk = 4 * half + j
                        mm = pe.transpose(turn_bank[half][:, P * j:P * (j + 1)],
                                          raw[k][:, P * kk:P * (kk + 1)], ident[:])
                    mm.then_inc(w_turned, 1)

            def turn_next(it, k):
                turn_w(it if k < 5 else it + 1, (k + 1) % 6)

            def w_ready(it, k):
                pe.wait_ge(w_lo, 12 * it + (2 * k + 2))

            def product(acc, w, act, ks, last):
                for k in ks:
                    for wi, ai in ((0, 0), (0, 1), (1, 0)):
                        mm = pe.matmul(acc, w[wi][:, k, :], act[ai][:, k, :],
                                       start=(k == 0 and wi == 0 and ai == 0),
                                       stop=(k == KD - 1 and wi == 1))
                if last:
                    mm.then_inc(mm_done, 1)

            def key_turns(n):
                pe.wait_ge(keyb_ready, n + 1)
                if n >= 2:
                    pe.wait_ge(keys_compared, n - 1)
                for j in range(4):
                    mm = pe.transpose(score_bank[n % 2][:, P * j:P * (j + 1)], keyb[:, 4 * n + j, :], ident[:])
                mm.then_inc(keys_turned, 1)

            def diagonal(start):
                for t in range(T):
                    mm = pe.matmul(edge_bank[t][:, 0:N], diag_w[:], diag_col[:, t, :], start=start, stop=not start)
                if not start:
                    mm.then_inc(edges_summed, 1)

            def add_batch(it, n):
                pe.wait_ge(oh_ready, 16 * it + (n - 15))
                for t in range(T):
                    mm = pe.matmul(edge_bank[t][:, 0:N], oh_src[n % OH][:, P * t:P * (t + 1)], oh_dst[n % OH][:],
                                   start=False, stop=False)
                mm.then_inc(oh_used, 1)

            pe.wait_ge(ident_ready, 1)
            for _ in range(WARM_UP):
                pe.transpose(turn_bank[1][:, 0:P], ident[:], ident[:])
            layer_norm_turns(0, 0)
            turn_w(0, 0, first=True)
            pe.wait_ge(edges_f_ready, 1)
            for j in range(4):
                mm = pe.transpose(acc_bank[1][:, 64 * j:64 * j + NB], edges_f[:, j, :], ident[0:NB, 0:NB])
            mm.then_inc(edges_turned, 1)
            layer_norm_turns(0, 1)
            layer_norm_turns(0, 2)
            w_ready(0, 0)
            for t in range(T):
                pe.wait_ge(t3_split, 2 * (t + 1))
                cols = slice(P * t, P * (t + 1))
                product(acc_bank[0][:, cols], wb[0], [xt[0][:, :, cols], xt[1][:, :, cols]], range(KD), t == T - 1)
                if t == 0:
                    turn_next(0, 0)
                elif t == 1:
                    pe.wait_ge(bias_in, 16 * 7)
                    pe.transpose(pv_bank[:, 0:7 * KD], bias_rows[:],
                                 ident[0:7 * KD, 0:7 * KD]).then_inc(bias_turned, 1)
            n = 0
            for k in range(1, 6):
                turn_next(0, k)
                w_ready(0, k)
                if k == 1:
                    pe.wait_ge(edge_step, 2)
                else:
                    pe.wait_ge(y_hi, k - 1)
                    pe.wait_ge(y_ready, k - 1)
                product(acc_bank[k % 2][:, 0:N], wb[k % 3], xt, range(KD), True)
                for _ in range(keys_per_unit[k]):
                    key_turns(n)
                    n += 1
            pe.wait_ge(keys_compared, NB // 4)
            pe.wait_ge(consts, 2)
            diagonal(True)
            per_unit = [3, 3, 3, 3, 2, 2]
            with pe.Fori(1, 4) as it:
                n = 0
                for k in range(6):
                    turn_next(it, k)
                    w_ready(it, k)
                    pe.wait_ge(y_hi, 6 * it + (k - 1))
                    pe.wait_ge(y_ready, 6 * it + (k - 1))
                    product(acc_bank[k % 2][:, 0:N], wb[k % 3], xt, range(KD), True)
                    for _ in range(per_unit[k]):
                        add_batch(it, n)
                        n += 1
            diagonal(False)

            def att_step(r, par, k, scores, tail, first):
                a = 6 * r + (k - 6)
                tp = 1 - par
                if scores:
                    hh, t = k // 3, k % 3
                    lo, hi = DH * hh, DH * (hh + 1)
                    if k < 2:
                        pe.wait_ge(y_split, 2 * r + U_INNER)
                    if not (first and k < 2):
                        pe.wait_ge(masked_max, a - 1)
                    for n, (qi, ki) in enumerate(((0, 0), (0, 1), (1, 0))):
                        mm = pe.matmul(score_bank[k % 2][:, 0:N], q2[par][qi][lo:hi, P * t:P * (t + 1)],
                                       k2[par][ki][lo:hi, :], start=(n == 0), stop=(n == 2))
                    mm.then_inc(scored, 1)
                if (k == 0 and tail) or (k > 0 and scores):
                    c = turn_count(r, f"P{(k - 1) % 6}", first)
                    pe.wait_ge(prob_ready, a)
                    pe.wait_ge(t3_split, c)
                    turn3(c, t3_bank, lambda j: probs[(k - 1) % 2][:, P * j:P * (j + 1)])
                if (k < 2 and tail) or (k >= 2 and scores):
                    kk = (k - 2) % 6
                    vb = v2[tp if k < 2 else par]
                    hh = kk // 3
                    c = turn_count(r, f"P{kk}", first) if k >= 2 else None
                    if k >= 2:
                        pe.wait_ge(t3_split, c + 1)
                    elif k == 1:
                        pe.wait_ge(t3_split, turn_count(r, "P5", False) + 1)
                    else:
                        pe.wait_ge(t3_split, c_base(r))
                    if not (first and k == 2):
                        pe.wait_ge(att_ready, a - 2)
                    n = 0
                    for j in range(T):
                        for pi, vi in ((0, 0), (0, 1), (1, 0)):
                            mm = pe.matmul(pv_bank[:, 0:DH], pt[k % 2][pi][:, j, :],
                                           vb[vi][:, j, DH * hh:DH * (hh + 1)], start=(n == 0), stop=(n == 8))
                            n += 1
                    mm.then_inc(pv_done, 1)

            def value_turn(r, first):
                c = turn_count(r, "V", first)
                pe.wait_ge(y_ready, 3 * r + U_INNER)
                pe.wait_ge(t3_split, c)
                turn3(c, t3_bank, lambda j: yv[:, P * j:P * (j + 1)])

            def output_turn(r, tp):
                c = turn_count(r, "O", False)
                pe.wait_ge(att_ready, 6 * r - 6)
                pe.wait_ge(t3_split, c)
                turn3(c, t3_bank, lambda j: att[tp][:, j, :])

            def inner_phase(r, it, i, first, att_on, tail):
                for m, n in enumerate("qkv"):
                    k6 = 3 * i + m
                    turn_next(it, k6)
                    w_ready(it, k6)
                    if first:
                        pe.wait_ge(y_split, U_INNER - 4 + 2 * m)
                    pe.wait_ge(y_ready, 6 * it + (k6 - 1))
                    pe.wait_ge(y_hi, 2 * r + (U_INNER + (m == 2)) if not (first and m == 0) else U_INNER - 1)
                    acc = acc_bank[(i + m) % 2][:, 0:N]
                    product(acc, wb[m], proj[n], range(0, 1), False)
                    if m == 0 and att_on:
                        value_turn(r, not tail)
                    if m == 1 and tail:
                        output_turn(r, i)
                    product(acc, wb[m], proj[n], range(1, 3), False)
                    if att_on:
                        att_step(r, 1 - i, 2 * m, True, tail, not tail)
                    product(acc, wb[m], proj[n], range(3, 6), False)
                    if att_on:
                        att_step(r, 1 - i, 2 * m + 1, True, tail, not tail)
                    product(acc, wb[m], proj[n], range(6, KD), True)

            inner_phase(0, 4, 0, True, False, False)
            pe.wait_ge(types_ready, T)
            inner_phase(1, 4, 1, False, True, False)
            with pe.Fori(5, 8) as it:
                for i in range(2):
                    inner_phase(2 * it + (i - 8), it, i, False, True, True)
            def early(r, ks):
                product(acc_bank[r][:, 0:N], wb[r], ot, ks, False)

            turn_next(8, 0)
            w_ready(8, 0)
            pe.wait_ge(y_ready, U_OUT)
            value_turn(8, False)
            for k in range(6):
                if k == 2:
                    output_turn(8, 0)
                early(0, [k])
                att_step(8, 1, k, True, True, False)
            w_ready(8, 1)
            early(1, [0])
            att_step(9, 0, 0, False, True, False)
            early(1, [1, 2])
            att_step(9, 0, 1, False, True, False)
            early(1, [3, 4, 5])
            output_turn(9, 1)

            def out_turn(r):
                c = C_OUT + r
                pe.wait_ge(y_ready, U_OUT + r + 1)
                pe.wait_ge(t3_split, c)
                turn3(c, t3_bank, lambda j: ybuf[r % 2][:, P * j:P * (j + 1)])

            pe.wait_ge(t3_split, C_OUT)
            for r in range(KD):
                u = U_OUT + r
                if 1 <= r < KD - 1:
                    turn_w((u + 1) // 6, (u + 1) % 6)
                if r >= 2:
                    w_ready(u // 6, u % 6)
                    pe.wait_ge(y_ready, u - 1)
                acc = acc_bank[u % 2][:, 0:N]
                if r >= 2:
                    product(acc, wb[u % 3], ot, range(3), False)
                if r >= 1:
                    out_turn(r - 1)
                product(acc, wb[u % 3], ot, range(3 if r >= 2 else 6, KD), True)
            pe.wait_ge(gate_in, 16)
            pe.wait_ge(y_ready, U_ALL)
            for k in range(KD):
                mm = pe.transpose(acc_bank[1][:, NE * k:NE * (k + 1)], gate_n[:, P * k:P * (k + 1)], ident[0:NE, 0:NE])
            mm.then_inc(gate_turned, 1)
            out_turn(KD - 1)
            for t in range(T):
                layer_norm_turns(C_LN2, t)

            pe.wait_ge(t3_split, C_LN2 + C_LN)
            pe.wait_ge(gate_split, 1)
            for t in range(T):
                n = 0
                for k in range(KD):
                    for xi, gi in ((0, 0), (0, 1), (1, 0)):
                        mm = pe.matmul(acc_bank[1][:, 64 + NE * t:64 + NE * (t + 1)], xt[xi][:, k, P * t:P * (t + 1)],
                                       gt[gi][:, k, :], start=(n == 0), stop=(n == 3 * KD - 1))
                        n += 1
            mm.then_inc(logits_done, 1)

            def up(s, which):
                pe.wait_ge(f_lo, f_w1(s) + which + 1)
                if not (isinstance(s, int) and s == 0):
                    pe.wait_ge(gated, 2 * s - 1 + which)
                w = wb[which]
                for k in range(KD):
                    for wi, ai in ((0, 0), (0, 1), (1, 0)):
                        mm = pe.matmul(bank[which][:, 0:N], w[wi][:, k, :], xt[ai][:, k, :],
                                       start=(k == 0 and wi == 0 and ai == 0), stop=(k == KD - 1 and wi == 1))
                mm.then_inc(f_used, 1)

            def down(s, par, first=False, last=False):
                pe.wait_ge(f_lo, f_w2(s) + 1)
                pe.wait_ge(hid_split, s + 1)
                w = [wb[2][i][:].rearrange("p k c -> p (k c)") for i in range(2)]
                for t in range(T):
                    for half in range(2):
                        for n, (hi_, wi) in enumerate(((0, 0), (0, 1), (1, 0))):
                            mm = pe.matmul(out_bank[2 * t + half][:], ht[par][hi_][:, P * t:P * (t + 1)],
                                           w[wi][:, 512 * half:512 * (half + 1)],
                                           start=(first and n == 0), stop=(last and n == 2))
                        if last:
                            mm.then_inc(tile_done, 1)
                if not last:
                    mm.then_inc(f_used, 1)

            up(0, 0)
            up(0, 1)
            pe.wait_ge(cwx_ready, 1)
            for e in range(NE):
                for t in range(T):
                    mm = pe.transpose(bank[2 + e][:, P * t:P * (t + 1)], cwx[e][:, t, :], ident[:])
                mm.then_inc(cw_turned, 1)
            up(1, 0)
            up(1, 1)
            pe.wait_ge(cw_ready, NE)
            down(0, 0, first=True)
            with pe.Fori(0, FULL) as i:
                for e in range(NE):
                    s = 4 * i + (2 + e)
                    up(s, 0)
                    up(s, 1)
                    down(s - 1, (e + 1) % 2)
            down(NS - 1, 1, last=True)

        @block.scalar
        def _(act):
            act.dma_start(edges_i[:, 0, :], src_d.rearrange("(b p) -> b p", p=P)).then_inc(edges_in, 16)
            act.dma_start(edges_i[:, 1, :], dst_d.rearrange("(b p) -> b p", p=P)).then_inc(edges_in, 16)
            act.dma_start(edges_i[:, 2, :], etype_d.rearrange("(b p) -> b p", p=P)).then_inc(edges_in, 16)
            act.dma_start(etw[:], etw_d.partition_broadcast(P)).then_inc(etw_in, 16)
            for n, b in enumerate((bq, bk, bv, biq, bik, biv, bo)):
                act.dma_start(bias_rows[KD * n:KD * (n + 1), :], b.rearrange("(r p) -> r p", p=P)).then_inc(bias_in, 16)

            def layer_norm_hi(c0, t):
                for c in (2 * t, 2 * t + 1):
                    half = c % 2
                    act.wait_ge(t3_turned, c0 + c + 1)
                    act.activation(xt[0][:, 4 * half:4 * half + 4, P * t:P * (t + 1)],
                                   ln_bank[c % 4][:].rearrange("p (k c) -> p k c", k=4), ACT.Copy).then_inc(t3_hi, 1)

            def w_part(it, k):
                if not (isinstance(it, int) and 6 * it + k < 3):
                    act.wait_ge(mm_done, 6 * it + (k - 2))
                for half in range(2):
                    act.wait_ge(w_turned, 12 * it + (2 * k + half + 1))
                    act.activation(wb[k % 3][0][:, 4 * half:4 * half + 4, :],
                                   turn_bank[half][:].rearrange("p (k c) -> p k c", k=4), ACT.Copy,
                                   scale=W_SCALE).then_inc(w_hi, 1)

            def w_ahead(it, k):
                w_part(it if k < 5 else it + 1, (k + 1) % 6)

            layer_norm_hi(0, 0)
            w_part(0, 0)
            layer_norm_hi(0, 1)
            layer_norm_hi(0, 2)
            def y_part(it, k, n, b, dst, count, scale):
                act.wait_ge(mm_done, 6 * it + (k + 1))
                act.activation(dst, acc_bank[k % 2][:, 0:N], ACT.Identity, bias=b, scale=scale).then_inc(y_hi, 1)

            act.wait_ge(bias_ready, 1)
            for k in range(6):
                w_ahead(0, k)
                n, i = k // 2, k % 2
                y_part(0, k, n, bias[:, n, i:i + 1], proj["qkv"[n]][0][:, i, :], k + 1, W_BACK)
                if k == 2:
                    act.wait_ge(soft_a, 1)
                    act.activation(sp_b[:], sp_a[:], ACT.Exp, scale=-1.0).then_inc(soft_b, 1)
                    act.wait_ge(soft_b, 1)
                    act.activation(sp_c[:], sp_b[:], ACT.Ln, bias=1.0).then_inc(soft_b, 1)
            with act.Fori(1, 4) as it:
                for k in range(6):
                    w_ahead(it, k)
                    n, i = k // 2, k % 2
                    y_part(it, k, n, bias[:, n, ds(2 * it + i, 1)], proj["qkv"[n]][0][:, 2 * it + i, :],
                           6 * it + (k + 1), W_BACK)

            def att_step(r, par, k, scores, tail, first):
                a = 6 * r + (k - 6)
                tp = 1 - par
                if (k == 0 and tail) or (k > 0 and scores):
                    c = turn_count(r, f"P{(k - 1) % 6}", first)
                    if not (first and k < 3):
                        act.wait_ge(pv_done, a - 2)
                    act.wait_ge(t3_turned, c + 1)
                    act.activation(pt[k % 2 ^ 1][0][:].rearrange("p t c -> p (t c)"), t3_bank[:, 0:N],
                                   ACT.Copy).then_inc(t3_hi, 1)
                if scores:
                    act.wait_ge(masked_max, a + 1)
                    act.activation(probs[k % 2][:], masked[k % 2][:], ACT.Exp, scale=-1.0,
                                   bias=negmax[:, k:k + 1], accum_out=rowsum[:, k:k + 1]).then_inc(prob_ready, 1)

            def value_part(r, par, first):
                c = turn_count(r, "V", first)
                act.wait_ge(t3_turned, c + 1)
                act.activation(v2[par][0][:].rearrange("p t c -> p (t c)"), t3_bank[:, 0:N],
                               ACT.Copy).then_inc(t3_hi, 1)

            def output_part(r):
                c = turn_count(r, "O", False)
                act.wait_ge(t3_turned, c + 1)
                act.activation(ot[0][:, r - 2, :], t3_bank[:, 0:N], ACT.Copy).then_inc(t3_hi, 1)

            def inner_phase(r, it, i, att_on, tail):
                for m in range(3):
                    k6 = 3 * i + m
                    w_ahead(it, k6)
                    if m == 0 and att_on:
                        value_part(r, 1 - i, not tail)
                    if m == 1 and tail:
                        output_part(r)
                    if att_on:
                        att_step(r, 1 - i, 2 * m, True, tail, not tail)
                        att_step(r, 1 - i, 2 * m + 1, True, tail, not tail)
                    if m == 0:
                        y_part(it, k6, 3, biasq[:, ds(r, 1)], q2[i][0][:], None, -0.125 * W_BACK)
                    elif m == 1:
                        y_part(it, k6, 4, bias[:, 4, ds(r, 1)], k2[i][0][:], None, W_BACK)

            inner_phase(0, 4, 0, False, False)
            act.dma_start(gate_n[:], gate_w[0:NE, :]).then_inc(gate_in, 16)
            inner_phase(1, 4, 1, True, False)
            with act.Fori(5, 8) as it:
                for i in range(2):
                    inner_phase(2 * it + (i - 8), it, i, True, True)
            w_part(8, 1)
            value_part(8, 1, False)
            for k in range(6):
                if k == 2:
                    output_part(8)
                att_step(8, 1, k, True, True, False)
            for k in range(2):
                att_step(9, 0, k, False, True, False)
            output_part(9)
            for r in range(2, KD):
                w_part((U_OUT + r) // 6, (U_OUT + r) % 6)

            def f_part(slot, landed, b, wait):
                act.wait_ge(raw_in[slot], landed)
                if wait is not None:
                    act.wait_ge(*wait)
                act.activation(wb[b][0][:].rearrange("p k c -> p (k c)"), raw[slot][:], ACT.Copy,
                               scale=W_SCALE).then_inc(f_hi, 1)

            f_part(0, w1_landed(0, 0, 0), 0, (mm_done, U_ALL - 1))
            f_part(1, w1_landed(0, 0, 1), 1, (mm_done, U_ALL))
            act.wait_ge(gate_turned, 1)
            act.activation(gt[0][:].rearrange("p k e -> p (k e)"), acc_bank[1][:, 0:NE * KD], ACT.Copy,
                           scale=W_SCALE).then_inc(gate_hi, 1)
            for t in range(T):
                layer_norm_hi(C_LN2, t)
            act.wait_ge(route_step, 3)
            act.activation(pr[:], lg[:], ACT.Exp).then_inc(route_exp, 1)

            def step(s, s_half, par, nxt):
                b = par
                if nxt:
                    nh = s_half + (1 if par else 0)
                    f_part(w1_slot[1 - par], w1_landed(nh, 1 - par, 0), 0, (f_used, f_w1(s) + 1))
                act.wait_ge(f_used, f_w1(s) + 1)
                if not (isinstance(s, int) and s < 2):
                    act.wait_ge(gated, 2 * s - 3)
                act.activation(sig[b], bank[0][:, 0:N], ACT.Sigmoid, scale=W_BACK).then_inc(sig_ready, 1)
                if nxt:
                    f_part(w1_slot[1 - par] + 1, w1_landed(nh, 1 - par, 1), 1, (f_used, f_w3(s) + 1))
                act.wait_ge(hid_ready, s + 1)
                if not (isinstance(s, int) and s < 2):
                    act.wait_ge(f_used, f_w2(s - 2) + 1)
                act.activation(ht[b][0], hid[b], ACT.Copy).then_inc(hid_hi, 1)
                wait = (f_used, f_w2(s - 1) + 1) if not (isinstance(s, int) and s == 0) else (mm_done, U_ALL - 2)
                f_part(w2_slot[par], w2_landed(s_half, par), 2, wait)

            step(0, 0, 0, True)
            step(1, 0, 1, True)
            with act.Fori(0, FULL - 1) as i:
                for e in range(NE):
                    step(4 * i + (2 + e), 2 * i + (1 + e // 2), e % 2, True)
            for e in range(NE):
                step(4 * (FULL - 1) + 2 + e, 2 * (FULL - 1) + 1 + e // 2, e % 2, e < NE - 1)

        @block.vector
        def _(dve):
            counts = {}

            def link(ins, s):
                counts[s] = counts.get(s, 0) + 1
                ins.then_inc(s, 1)
                dve.wait_ge(s, counts[s])

            def var_of(t, n, chunks, step, base):
                dve.bn_aggr(mv[:, t, :], stats[:, t, 0:chunks].rearrange("p h s -> p (h s)")).then_inc(step, 1)
                dve.wait_ge(step, base + 1)
                dve.tensor_scalar(veps[:, t:t + 1], mv[:, t, 1:2], EPS, None, ALU.add).then_inc(step, 1)

            def norm1_stats(t):
                dve.wait_ge(x_in[t], 16)
                for h in range(2):
                    dve.bn_stats(stats[:, t, h, :], x[:, t, 512 * h:512 * (h + 1)]).then_inc(norm_step, 1)
                dve.wait_ge(norm_step, 4 * t + 2)
                var_of(t, 1, 2, norm_step, 4 * t + 2)

            def normed(n, t):
                dve.wait_ge(rstd_made, T * (n - 1) + t + 1)
                dve.tensor_scalar(xn[:, t, :], x[:, t, :], mv[:, t, 0:1], rstd[:, t:t + 1],
                                  ALU.subtract, ALU.mult).then_inc(xn_ready, 1)

            def layer_norm_lo(c0, hi0, t):
                for c in (2 * t, 2 * t + 1):
                    half = c % 2
                    part = (slice(None), slice(4 * half, 4 * half + 4), slice(P * t, P * (t + 1)))
                    lo_of_turn(c0 + c, hi0 + c + 1, ln_bank[c % 4][:].rearrange("p (k c) -> p k c", k=4),
                               xt[0][part], xt[1][part])

            def lo_of_turn(c, hi_count, src, hi_part, lo_part):
                dve.wait_ge(t3_hi, hi_count)
                dve.tensor_tensor(lo_part, src, hi_part, ALU.subtract).then_inc(t3_split, 1)

            def w_part(it, k):
                for half in range(2):
                    dve.wait_ge(w_hi, 12 * it + (2 * k + half + 1))
                    part = slice(4 * half, 4 * half + 4)
                    dve.scalar_tensor_tensor(out=wb[k % 3][1][:, part, :],
                                             in0=turn_bank[half][:].rearrange("p (k c) -> p k c", k=4),
                                             scalar=W_SCALE, in1=wb[k % 3][0][:, part, :],
                                             op0=ALU.mult, op1=ALU.subtract).then_inc(w_lo, 1)

            def w_ahead(it, k):
                w_part(it if k < 5 else it + 1, (k + 1) % 6)

            norm1_stats(0)
            norm1_stats(1)
            normed(1, 0)
            dve.wait_ge(edges_in, 48)
            dve.tensor_copy(edges_f[:, 0, :], edges_i[:, 0, :])
            dve.tensor_copy(edges_f[:, 1, :], edges_i[:, 1, :])
            link(dve.tensor_scalar(edges_f[:, 3, :], edges_i[:, 2, :], 0.0, 4.0, ALU.is_equal, ALU.mult), mask_step)
            link(dve.scalar_tensor_tensor(out=edges_f[:, 2, :], in0=edges_i[:, 2, :], scalar=-1.0,
                                          in1=edges_f[:, 3, :], op0=ALU.add, op1=ALU.add), mask_step)
            dve.scalar_tensor_tensor(out=edges_f[:, 3, :], in0=edges_i[:, 0, :], scalar=float(N),
                                     in1=edges_i[:, 1, :], op0=ALU.mult, op1=ALU.add).then_inc(edges_f_ready, 1)
            norm1_stats(2)
            normed(1, 1)
            layer_norm_lo(0, 0, 0)
            normed(1, 2)
            w_part(0, 0)
            layer_norm_lo(0, 0, 1)
            dve.wait_ge(edges_turned, 1)
            dve.tensor_copy(edge[:, 3, :], acc_bank[1][:, 192:192 + NB]).then_inc(edge_step, 1)
            layer_norm_lo(0, 0, 2)
            dve.tensor_copy(edge[:, 0:3, :], acc_bank[1][:, 0:192].rearrange("p (j b) -> p j b", j=3)[:, :, 0:NB]
                            ).then_inc(edge_step, 1)
            dve.wait_ge(bias_turned, 1)
            dve.tensor_copy(bias[:].rearrange("p n r -> p (n r)"), pv_bank[:, 0:7 * KD]).then_inc(bias_ready, 1)
            dve.wait_ge(bias_ready, 1)
            link(dve.tensor_scalar(biasq[:], bias[:, 3, :], -0.125, None, ALU.mult), mask_step)

            def y_part(it, k, b, y, scale, hi_count=None):
                if hi_count is None:
                    dve.wait_ge(mm_done, 6 * it + (k + 1))
                else:
                    dve.wait_ge(y_hi, hi_count)
                dve.tensor_scalar(y, acc_bank[k % 2][:, 0:N], scale, b, ALU.mult, ALU.add).then_inc(y_ready, 1)

            def y_lo(u1, hi_count, y, hi_part, lo_part):
                dve.wait_ge(y_ready, u1)
                dve.wait_ge(y_hi, hi_count)
                dve.tensor_tensor(lo_part, y, hi_part, ALU.subtract).then_inc(y_split, 1)

            def compare_keys(n):
                dve.wait_ge(keys_turned, n + 1)
                if n >= 2:
                    dve.wait_ge(keys_compared, n - 1)
                for j in range(4):
                    b = 4 * n + j
                    ins = dve.scalar_tensor_tensor(out=same[:, P * (4 * (n % 2) + j):P * (4 * (n % 2) + j + 1)], in0=score_bank[n % 2][:, P * j:P * (j + 1)],
                                                   scalar=edge[:, 3, b:b + 1], in1=upper[:], op0=ALU.is_equal,
                                                   op1=ALU.mult, accum_out=later[:, b:b + 1])
                ins.then_inc(keys_compared, 1)

            c = 0
            for k in range(6):
                w_ahead(0, k)
                if k == 1:
                    dve.wait_ge(edge_step, 1)
                    dve.wait_ge(consts, 1)
                for _ in range(keys_per_unit[k]):
                    compare_keys(c)
                    c += 1
                if k == 2:
                    dve.wait_ge(etw_in, 16)
                    link(dve.tensor_scalar(sp_c[:], etw[:], -1.0, None, ALU.mult), mask_step)
                    dve.tensor_tensor(sp_a[:], etw[:], sp_c[:], ALU.max).then_inc(soft_a, 1)
                n, i = k // 2, k % 2
                y_part(0, k, bias[:, n, i:i + 1], ybuf[k % 2][:], W_BACK, k + 1)
                y_lo(k + 1, k + 1, ybuf[k % 2][:], proj["qkv"[n]][0][:, i, :], proj["qkv"[n]][1][:, i, :])

            dve.wait_ge(consts, 2)
            dve.wait_ge(keys_compared, NB // 4)
            link(dve.tensor_scalar(keep[:], later[:], 0.5, None, ALU.is_lt), mask_step)
            link(dve.tensor_tensor(expo[:], edge[:, 2, :], batch_e[:], ALU.add), mask_step)
            link(dve.tensor_scalar(val_i[:], expo[:], float(2 ** 23), None, ALU.mult), mask_step)
            link(dve.tensor_tensor(val[:], val_i[:].bitcast(F32), keep[:], ALU.mult), mask_step)

            def one_hots(it, n):
                b = 16 * it + (n - 16)
                dve.wait_ge(oh_used, b - (OH - 1))
                dve.tensor_scalar(oh_src[n % OH][:], iota[:], edge[:, 0, ds(b, 1)], None, ALU.is_equal)
                dve.tensor_scalar(oh_dst[n % OH][:], iota[:], edge[:, 1, ds(b, 1)], val[:, ds(b, 1)],
                                  ALU.is_equal, ALU.mult).then_inc(oh_ready, 1)

            per_unit = [3, 3, 3, 3, 2, 2]

            def round_(it, static):
                n = 0
                for k in range(6):
                    w_ahead(it, k)
                    for _ in range(per_unit[k]):
                        if static and n < OH:
                            b = n
                            dve.tensor_scalar(oh_src[n % OH][:], iota[:], edge[:, 0, b:b + 1], None, ALU.is_equal)
                            dve.tensor_scalar(oh_dst[n % OH][:], iota[:], edge[:, 1, b:b + 1], val[:, b:b + 1],
                                              ALU.is_equal, ALU.mult).then_inc(oh_ready, 1)
                        else:
                            one_hots(it, n)
                        n += 1
                    m, i = k // 2, k % 2
                    y_part(it, k, bias[:, m, ds(2 * it + i, 1)], ybuf[k % 2][:], W_BACK, 6 * it + (k + 1))
                    y_lo(6 * it + (k + 1), 6 * it + (k + 1), ybuf[k % 2][:], proj["qkv"[m]][0][:, 2 * it + i, :],
                         proj["qkv"[m]][1][:, 2 * it + i, :])

            round_(1, True)
            with dve.Fori(2, 4) as it:
                round_(it, False)

            def minus_softplus():
                dve.wait_ge(soft_b, 2)
                link(dve.scalar_tensor_tensor(out=nsoft[:], in0=etw[:], scalar=0.0, in1=sp_c[:],
                                              op0=ALU.max, op1=ALU.add), mask_step)
                link(dve.tensor_scalar(nsoft[:], nsoft[:], -1.0, None, ALU.mult), mask_step)

            def read_edge_sums(t):
                dve.tensor_scalar(negmask[:, t, :], edge_bank[t][:, 0:N], 0.0, ABSENT, ALU.is_le, ALU.mult)
                link(dve.tensor_scalar(etyp[:, t, :], edge_bank[t][:, 0:N].bitcast(I32), 23, 3,
                                       ALU.logical_shift_right, ALU.bitwise_and), mask_step)
                for k in range(4):
                    ins = dve.tensor_scalar(type_part[:, t, k, :], etyp[:, t, :], float(k), nsoft[:, k:k + 1],
                                            ALU.is_equal, ALU.mult)
                ins.then_inc(types_ready, 1)

            def att_step(r, par, k, scores, tail, first):
                a = 6 * r + (k - 6)
                tp = 1 - par
                if scores:
                    dve.wait_ge(scored, a + 1)
                if (k == 0 and tail) or (k > 0 and scores):
                    kk = (k - 1) % 6
                    dve.wait_ge(prob_ready, a)
                    dve.reciprocal(rinv[:, kk:kk + 1], rowsum[:, kk:kk + 1]).then_inc(inv_ready, 1)
                if first and scores and k < T:
                    dve.wait_ge(mask_ready, k + 1)
                if scores:
                    dve.tensor_tensor_reduce(out=masked[k % 2][:], in0=score_bank[k % 2][:, 0:N],
                                             in1=negmask[:, k % 3, :], scale=1.0, scalar=3.0e38, op0=ALU.add,
                                             op1=ALU.min, accum_out=negmax[:, k:k + 1]).then_inc(masked_max, 1)
                if (k == 0 and tail) or (k > 0 and scores):
                    c = turn_count(r, f"P{(k - 1) % 6}", first)
                    b = k % 2 ^ 1
                    lo_of_turn(c, c + 1, t3_bank[:, 0:N], pt[b][0][:].rearrange("p t c -> p (t c)"),
                               pt[b][1][:].rearrange("p t c -> p (t c)"))
                if (k < 2 and tail) or (k >= 2 and scores):
                    kk = (k - 2) % 6
                    dve.wait_ge(pv_done, a - 1)
                    dve.wait_ge(inv_ready, a - 1)
                    dve.tensor_scalar(att[tp if k < 2 else par][:, kk % 3, DH * (kk // 3):DH * (kk // 3 + 1)],
                                      pv_bank[:, 0:DH], rinv[:, kk:kk + 1], None, ALU.mult).then_inc(att_ready, 1)

            def value_part(r, par, first):
                c = turn_count(r, "V", first)
                lo_of_turn(c, c + 1, t3_bank[:, 0:N], v2[par][0][:].rearrange("p t c -> p (t c)"),
                           v2[par][1][:].rearrange("p t c -> p (t c)"))

            def output_part(r):
                c = turn_count(r, "O", False)
                lo_of_turn(c, c + 1, t3_bank[:, 0:N], ot[0][:, r - 2, :], ot[1][:, r - 2, :])

            def inner_phase(r, it, i, att_on, tail):
                for m in range(3):
                    k6 = 3 * i + m
                    w_ahead(it, k6)
                    if not att_on:
                        read_edge_sums(m)
                    if m == 0 and att_on:
                        value_part(r, 1 - i, not tail)
                    if m == 1 and tail:
                        output_part(r)
                    if att_on:
                        att_step(r, 1 - i, 2 * m, True, tail, not tail)
                        att_step(r, 1 - i, 2 * m + 1, True, tail, not tail)
                    u1 = 6 * it + (k6 + 1)
                    if m == 0:
                        y_part(it, k6, biasq[:, ds(r, 1)], ybuf[0][:], -0.125 * W_BACK, 2 * r + (U_INNER + 1))
                        y_lo(u1, 2 * r + (U_INNER + 1), ybuf[0][:], q2[i][0][:], q2[i][1][:])
                    elif m == 1:
                        y_part(it, k6, bias[:, 4, ds(r, 1)], ybuf[1][:], W_BACK, 2 * r + (U_INNER + 2))
                        y_lo(u1, 2 * r + (U_INNER + 2), ybuf[1][:], k2[i][0][:], k2[i][1][:])
                    else:
                        y_part(it, k6, bias[:, 5, ds(r, 1)], yv[:], W_BACK)

            minus_softplus()
            dve.wait_ge(edges_summed, 1)
            inner_phase(0, 4, 0, False, False)
            inner_phase(1, 4, 1, True, False)
            with dve.Fori(5, 8) as it:
                for i in range(2):
                    inner_phase(2 * it + (i - 8), it, i, True, True)
            w_part(8, 1)
            value_part(8, 1, False)
            for k in range(6):
                if k == 2:
                    output_part(8)
                att_step(8, 1, k, True, True, False)
            for k in range(2):
                att_step(9, 0, k, False, True, False)
            output_part(9)

            def residual(r):
                c = C_OUT + r
                dve.wait_ge(t3_turned, c + 1)
                part = x[:, :, P * r:P * (r + 1)]
                dve.tensor_tensor(part, t3_bank[:, 0:N].rearrange("p (t c) -> p t c", t=T), part,
                                  ALU.add).then_inc(t3_split, 1)
                dve.wait_ge(t3_split, c + 1)
                for t in range(T):
                    dve.bn_stats(stats[:, t, r, :], x[:, t, P * r:P * (r + 1)]).then_inc(norm2_step, 1)

            for r in range(KD):
                u = U_OUT + r
                if 1 <= r < KD - 1:
                    w_part((u + 1) // 6, (u + 1) % 6)
                if r >= 1:
                    residual(r - 1)
                y_part(u // 6, u % 6, bias[:, 6, r:r + 1], ybuf[r % 2][:], W_BACK)

            def f_part(f1, slot, b):
                dve.wait_ge(f_hi, f1)
                dve.scalar_tensor_tensor(out=wb[b][1][:].rearrange("p k c -> p (k c)"), in0=raw[slot][:],
                                         scalar=W_SCALE, in1=wb[b][0][:].rearrange("p k c -> p (k c)"),
                                         op0=ALU.mult, op1=ALU.subtract).then_inc(f_lo, 1)

            residual(KD - 1)
            dve.wait_ge(norm2_step, KD * T)
            for t in range(T):
                var_of(t, 2, KD, norm2_step, KD * T + 2 * t)
            for t in range(T):
                normed(2, t)
            dve.wait_ge(gate_hi, 1)
            dve.scalar_tensor_tensor(out=gt[1][:].rearrange("p k e -> p (k e)"), in0=acc_bank[1][:, 0:NE * KD],
                                     scalar=W_SCALE, in1=gt[0][:].rearrange("p k e -> p (k e)"),
                                     op0=ALU.mult, op1=ALU.subtract).then_inc(gate_split, 1)
            f_part(1, 0, 0)
            for t in range(T):
                layer_norm_lo(C_LN2, C_LN2 - KD, t)
            f_part(2, 1, 1)

            dve.wait_ge(logits_done, 1)
            logits = acc_bank[1][:, 64:64 + T * NE].rearrange("p (t e) -> p t e", e=NE)
            spread = lambda a: a.unsqueeze(2).to_broadcast([P, T, NE])
            link(dve.tensor_scalar(lg[:], logits, W_BACK, None, ALU.mult), route_step)
            link(dve.tensor_reduce(lmax[:], lg[:], AX.X, ALU.max), route_step)
            link(dve.tensor_tensor(lg[:], lg[:], spread(lmax[:]), ALU.subtract), route_step)
            dve.wait_ge(route_exp, 1)
            mine = pr[:].unsqueeze(3).to_broadcast([P, T, NE, NE])
            other = pr[:].unsqueeze(2).to_broadcast([P, T, NE, NE])
            dve.tensor_tensor(cmp_a[:], other, mine, ALU.is_ge)
            link(dve.tensor_tensor(cmp_b[:], other, mine, ALU.is_gt), route_step)
            for t in range(T):
                dve.tensor_tensor(cmp_a[:, t], cmp_a[:, t], before[:], ALU.mult)
                ins = dve.tensor_tensor(cmp_b[:, t], cmp_b[:, t], after[:], ALU.mult)
            link(ins, route_step)
            link(dve.tensor_tensor(cmp_a[:], cmp_a[:], cmp_b[:], ALU.add), route_step)
            link(dve.tensor_reduce(rank[:], cmp_a[:], AX.X, ALU.add), route_step)
            link(dve.scalar_tensor_tensor(out=cw[:], in0=rank[:], scalar=1.5, in1=pr[:],
                                          op0=ALU.is_lt, op1=ALU.mult), route_step)
            link(dve.tensor_reduce(csum[:], cw[:], AX.X, ALU.add), route_step)
            link(dve.reciprocal(cinv[:], csum[:]), route_step)
            link(dve.tensor_tensor(cw[:], cw[:], spread(cinv[:]), ALU.mult), route_step)

            def step(s, par, nxt, e, mixed=None):
                b = par
                if nxt:
                    f_part(f_w1(s + 1) + 1, w1_slot[1 - par], 0)
                dve.wait_ge(sig_ready, s + 1)
                dve.scalar_tensor_tensor(out=g1[b], in0=bank[0][:, 0:N], scalar=W_BACK, in1=sig[b],
                                         op0=ALU.mult, op1=ALU.mult).then_inc(gated, 1)
                if nxt:
                    f_part(f_w3(s + 1) + 1, w1_slot[1 - par] + 1, 1)
                dve.wait_ge(f_used, f_w3(s) + 1)
                if mixed is not None:
                    if mixed == 0:
                        for e_ in range(NE):
                            dve.wait_ge(cw_turned, e_ + 1)
                            dve.tensor_copy(cwb[e_], bank[2 + e_][:, 0:N]).then_inc(cw_ready, 1)
                        dve.wait_ge(cw_ready, NE)
                    for h in range(2):
                        rows_ = slice(HALF * h, HALF * (h + 1))
                        ins = dve.scalar_tensor_tensor(out=g3[b][rows_, :], in0=bank[1][rows_, 0:N], scalar=W_BACK,
                                                       in1=cwb[2 * mixed + h][rows_, :], op0=ALU.mult, op1=ALU.mult)
                else:
                    ins = dve.scalar_tensor_tensor(out=g3[b], in0=bank[1][:, 0:N], scalar=W_BACK,
                                                   in1=cwb[e], op0=ALU.mult, op1=ALU.mult)
                ins.then_inc(gated, 1)
                dve.wait_ge(gated, 2 * s + 2)
                dve.tensor_tensor(hid[b], g1[b], g3[b], ALU.mult).then_inc(hid_ready, 1)
                dve.wait_ge(hid_hi, s + 1)
                dve.tensor_tensor(ht[b][1], hid[b], ht[b][0], ALU.subtract).then_inc(hid_split, 1)
                f_part(f_w2(s) + 1, w2_slot[par], 2)

            step(0, 0, True, None, mixed=0)
            step(1, 1, True, None, mixed=1)
            with dve.Fori(0, FULL - 1) as i:
                for e in range(NE):
                    step(4 * i + (2 + e), e % 2, True, e)
            for e in range(NE):
                step(4 * (FULL - 1) + 2 + e, e % 2, e < NE - 1, e)

            for t in range(T):
                for half in range(2):
                    dve.wait_ge(tile_done, 2 * t + half + 1)
                    cols = slice(512 * half, 512 * (half + 1))
                    dve.scalar_tensor_tensor(out=res[:, t, cols], in0=out_bank[2 * t + half][:], scalar=W_BACK,
                                             in1=x[:, t, cols], op0=ALU.mult, op1=ALU.add).then_inc(res_ready, 1)


_INS = ["x", "src", "dst", "edge_type_5", "L0_gnn_edge_type_weights", "L0_gnn_wq", "L0_gnn_bq", "L0_gnn_wk",
        "L0_gnn_bk", "L0_gnn_wv", "L0_gnn_bv", "L0_gnn_wiq", "L0_gnn_biq", "L0_gnn_wik", "L0_gnn_bik",
        "L0_gnn_wiv", "L0_gnn_biv", "L0_gnn_wo", "L0_gnn_bo", "L0_ffn_gate_w", "L0_ffn_w1", "L0_ffn_w2",
        "L0_ffn_w3"]


def kernel(**inputs):
    import numpy as _np
    import concourse.bacc as _bacc
    from concourse import mybir as _mybir
    from concourse.bass_utils import run_bass_kernel_spmd as _run

    nc = _bacc.Bacc("TRN2", target_bir_lowering=False, num_devices=1)
    arrays, args = {}, []
    for name in _INS:
        a = _np.ascontiguousarray(inputs[name])
        arrays[f"in_{name}"] = a
        args.append(nc.dram_tensor(f"in_{name}", a.shape, _mybir.dt.from_np(a.dtype), kind="ExternalInput").ap())
    shape = tuple(inputs["x"].shape)
    args.append(nc.dram_tensor("out_0", shape, F32, kind="ExternalOutput").ap())
    gnn_moe_kernel(nc, *args)
    r = _run(nc, [arrays], core_ids=[0])
    return r.results[0]["out_0"]
```

```python
from contextlib import ExitStack

import concourse.bass as bass
from concourse import mybir

P = 128
F32 = mybir.dt.float32
F16 = mybir.dt.float16
BF16 = mybir.dt.bfloat16
I32 = mybir.dt.int32
ALU = mybir.AluOpType
ACT = mybir.ActivationFunctionType
AX = mybir.AxisListType

ds = bass.ds

W_SCALE = 64.0
W_BACK = 1.0 / W_SCALE
ABSENT = 1.0e30
EPS = 1e-5
SLOTS = 6


def gnn_moe_kernel(nc, x_d, src_d, dst_d, etype_d, etw_d, wq, bq, wk, bk, wv, bv, wiq, biq,
                   wik, bik, wiv, biv, wo, bo, gate_w, w1, w2, w3, out_d):
    N, D = x_d.shape
    T = N // P
    KD = D // P
    E = src_d.shape[0]
    NB = E // P
    DH = 64
    NE = 4
    HID = w1.shape[2]
    FULL = HID // P
    HALF = HID - FULL * P
    NS = NE * HID // P
    CAP = 240
    SR = (P, CAP - P)
    ST = len(SR)
    assert (N, D, HID, HALF, NS, NB) == (384, 1024, 704, 64, 22, 48)

    with ExitStack() as ctx:
        def sb(name, shape, dt=F32):
            return ctx.enter_context(nc.sbuf_tensor(name, shape, dt))

        def sem(name):
            return ctx.enter_context(nc.semaphore(name))

        bank = [ctx.enter_context(nc.psum_tensor(f"bank{i}", [P, 512], F32)) for i in range(8)]
        turn_bank = bank[0:2]
        acc_bank = bank[2:4]
        score_bank = bank[4:6]
        t3_bank = bank[6]
        pv_bank = bank[7]
        ln_bank = bank[4:8]
        edge_bank = [bank[4], bank[5], bank[7]]
        slot_bank, tok_bank = bank[6], bank[7]
        out_bank = bank[2:8]

        x = sb("x", [P, T, D])
        xn = sb("xn", [P, T, D])
        xt = [sb("xt_hi", [P, KD, N], F16), sb("xt_lo", [P, KD, N], F16)]
        proj = {n: [sb(f"{n}t_hi", [P, KD, N], F16), sb(f"{n}t_lo", [P, KD, N], F16)] for n in "qkv"}
        q2 = [[sb(f"q2_{b}_{h}", [P, N], F16) for h in range(2)] for b in range(2)]
        k2 = [[sb(f"k2_{b}_{h}", [P, N], F16) for h in range(2)] for b in range(2)]
        q2_hi = [[q2[b][0], sb(f"q2_stack_{b}", [P, N], F16)] for b in range(2)]
        k2_hi = [[k2[b][0], sb(f"k2_stack_{b}", [P, N], F16)] for b in range(2)]
        v2 = [[sb(f"v2_{b}_{h}", [P, T, P], F16) for h in range(2)] for b in range(2)]
        raw = [sb(f"raw{i}", [P, D]) for i in range(SLOTS)]
        wb = [[sb(f"w{b}_{h}", [P, KD, P], F16) for h in range(2)] for b in range(3)]
        ybuf = [sb(f"y{b}", [P, N]) for b in range(2)]
        yv = sb("yv", [P, N])
        bias = sb("bias", [P, 7, KD])
        biasq = sb("biasq", [P, KD])
        bias_rows = sb("bias_rows", [7 * KD, P])
        masked = [sb(f"masked{b}", [P, N]) for b in range(2)]
        probs = [sb(f"probs{b}", [P, N]) for b in range(2)]
        pt = [[sb(f"pt_{b}_{h}", [P, T, P], F16) for h in range(2)] for b in range(2)]
        att = [sb(f"att{b}", [P, T, P]) for b in range(2)]
        negmax = sb("negmax", [P, 6])
        rowsum = sb("rowsum", [P, 6])
        rinv = sb("rinv", [P, 6])
        negmask = sb("negmask", [P, T, N])
        stats = sb("stats", [P, T, KD, 6])
        mv = sb("mv", [P, T, 2])
        veps = sb("veps", [P, T])
        rstd = sb("rstd", [P, T])
        mhalf = sb("mhalf", [P, T])
        ident = sb("ident", [P, P])
        upper = sb("upper", [P, P])
        iota_i = sb("iota_i", [P, N], I32)
        iota = sb("iota", [P, N], F16)
        diag_w = sb("diag_w", [P, P], BF16)
        diag_col = sb("diag_col", [P, T, N], BF16)
        edges_i = sb("edges_i", [NB, 3, P], I32)
        edges_f = sb("edges_f", [NB, 4, P])
        edge = sb("edge", [P, 4, NB])
        batch_i = sb("batch_i", [P, NB], I32)
        batch_e = sb("batch_e", [P, NB])
        keyb = sb("keyb", [P, NB, P])
        ot_room = keyb[:].rearrange("p b c -> p (b c)").bitcast(F16)
        ot = [ot_room[:, KD * N * h:KD * N * (h + 1)].rearrange("p (k n) -> p k n", k=KD) for h in range(2)]
        later = sb("later", [P, NB])
        keep = sb("keep", [P, NB])
        expo = sb("expo", [P, NB])
        val_i = sb("val_i", [P, NB], I32)
        val = sb("val", [P, NB])
        OH = 4
        oh_src = [sb(f"oh_src{i}", [P, N], BF16) for i in range(OH)]
        oh_dst = [sb(f"oh_dst{i}", [P, N], BF16) for i in range(OH)]
        etyp = sb("etyp", [P, T, N], I32)
        type_part = keyb[:].rearrange("p b c -> p (b c)")[:, 0:T * 4 * N].rearrange("p (t k n) -> p t k n", t=T, k=4)
        same = sb("same", [P, 8 * P])
        etw = sb("etw", [P, 4])
        sp_a = sb("sp_a", [P, 4])
        sp_b = sb("sp_b", [P, 4])
        sp_c = sb("sp_c", [P, 4])
        nsoft = sb("nsoft", [P, 4])
        def room(name, half, n):
            flat = proj[name][half][:].rearrange("p k n -> p (k n)").bitcast(F32)
            return [flat[:, N * i:N * (i + 1)] for i in range(n)]

        gate_n = sb("gate_n", [NE, D])
        gt = [sb("gt_hi", [P, KD, NE], F16), sb("gt_lo", [P, KD, NE], F16)]
        lg = sb("lg", [P, T, NE])
        lmax = sb("lmax", [P, T])
        pr = sb("pr", [P, T, NE])
        cmp_a = sb("cmp_a", [P, T, NE, NE])
        cmp_b = sb("cmp_b", [P, T, NE, NE])
        before = sb("before", [P, NE, NE])
        after = sb("after", [P, NE, NE])
        rank = sb("rank", [P, T, NE])
        csum = sb("csum", [P, T])
        cinv = sb("cinv", [P, T])
        cw = sb("cw", [P, T, NE])
        cwx = [a.rearrange("p (t c) -> p t c", t=T) for a in room("q", 0, NE)]
        cwb = room("q", 1, NE)
        sig, g1 = room("k", 0, 4)[0:2], room("k", 0, 4)[2:4]
        g3, hid = room("k", 1, 4)[0:2], room("k", 1, 4)[2:4]
        ht = [[proj["v"][b][:, h, :] for h in range(2)] for b in range(2)]
        res = xn
        upper16 = sb("upper16", [P, P], F16)
        ones16 = sb("ones16", [P, P], F16)
        ids_i = sb("ids_i", [P, T], I32)
        ids = sb("ids", [P, T], F16)
        chosen = sb("chosen", [P, T, NE])
        chosen16 = sb("chosen16", [P, T, NE], F16)
        pos = sb("pos", [P, T, NE])
        posm = sb("posm", [P, T, NE])
        count_max = sb("count_max", [P, 1])
        flag = sb("flag", [P, 1], I32)
        tok = sb("tok", [P, NE * ST], I32)
        cum = sb("cum", [P, T, NE])
        pick = [sb(f"pick{n}", [P, T, NE]) for n in range(2)]
        row_f = [sb(f"row_f{n}", [P, T]) for n in range(2)]
        row_i = [sb(f"row_i{n}", [P, T], I32) for n in range(2)]
        wgt = [sb(f"wgt{n}", [P, T]) for n in range(2)]
        spick = sb("spick", [P, T, NE])
        slot_hot = [proj["v"][e // 2][:, 2 + 2 * (e % 2):4 + 2 * (e % 2), :].rearrange("p a n -> p (a n)")[:, 0:T * CAP]
                    .rearrange("p (t c) -> p t c", t=T) for e in range(NE)]
        keyb_flat = keyb[:].rearrange("p b c -> p (b c)")
        area = lambda n: keyb_flat[:, 2 * D * n:2 * D * (n + 1)].rearrange("p (s d) -> p s d", s=ST)
        xrows = [area(0), area(1)]
        staged = area(2)
        xn16 = xn[:].rearrange("p t d -> p (t d)").bitcast(F16)
        xg_flat = [[xn16[:, 2048 * n:2048 * (n + 1)] for n in (0, 1)],
                   [xn16[:, 4096:6144], negmask[:].rearrange("p t n -> p (t n)").bitcast(F16)[:, 0:2048]]]
        xg = [[a[:, 0:KD * CAP].rearrange("p (k c) -> p k c", k=KD) for a in pair] for pair in xg_flat]
        low = [xt[0][:].rearrange("p k n -> p (k n)").bitcast(F32)[:, 0:D],
               xt[1][:].rearrange("p k n -> p (k n)").bitcast(F32)[:, 0:D], same[:]]
        high = [xrows[1][:, 0, :], xrows[1][:, 1, :], staged[:, 0, :]]
        neg16 = negmask[:].rearrange("p t n -> p (t n)").bitcast(F16)
        w2b = [[w[:].rearrange("p k c -> p (k c)") for w in wb[2]],
               [proj["q"][n][:].rearrange("p k n -> p (k n)")[:, 0:D] for n in range(2)]]
        mixed_w = [neg16[:, D * n:D * (n + 1)] for n in range(2)]
        last16 = [a.rearrange("p (s d) -> p s d", s=ST) for a in xg_flat[0]]
        last_hot = proj["v"][1][:, 4:6, :]
        early_sig = sb("early_sig", [P, T])
        tok_f = sb("tok_f", [P, NE * ST])
        xn_dram = nc.dram_tensor("normed_rows", [N, D], F32).ap()
        y_dram = nc.dram_tensor("expert_rows", [NE * CAP, D], F32).ap()

        x_in = [sem(f"x_in{t}") for t in range(T)]
        edges_in = sem("edges_in")
        bias_in = sem("bias_in")
        bias_turned = sem("bias_turned")
        bias_ready = sem("bias_ready")
        etw_in = sem("etw_in")
        gate_in = sem("gate_in")
        raw_in = [sem(f"raw_in{i}") for i in range(SLOTS)]
        out_done = sem("out_done")
        ident_ready = sem("ident_ready")
        consts = sem("consts")
        pool_step = sem("pool_step")
        norm_step = sem("norm_step")
        norm2_step = sem("norm2_step")
        rstd_made = sem("rstd_made")
        xn_ready = sem("xn_ready")
        edge_step = sem("edge_step")
        edges_f_ready = sem("edges_f_ready")
        edges_turned = sem("edges_turned")
        keyb_ready = sem("keyb_ready")
        keys_turned = sem("keys_turned")
        keys_compared = sem("keys_compared")
        oh_ready = sem("oh_ready")
        oh_used = sem("oh_used")
        edges_summed = sem("edges_summed")
        mask_step = sem("mask_step")
        types_ready = sem("types_ready")
        mask_ready = sem("mask_ready")
        soft_a = sem("soft_a")
        soft_b = sem("soft_b")
        w_turned = sem("w_turned")
        w_hi = sem("w_hi")
        w_lo = sem("w_lo")
        mm_done = sem("mm_done")
        y_ready = sem("y_ready")
        y_hi = sem("y_hi")
        y_split = sem("y_split")
        t3_turned = sem("t3_turned")
        t3_hi = sem("t3_hi")
        t3_split = sem("t3_split")
        stack_copied = sem("stack_copied")
        stacked = [sem(f"stacked{b}") for b in range(2)]
        scored = sem("scored")
        masked_max = sem("masked_max")
        prob_ready = sem("prob_ready")
        inv_ready = sem("inv_ready")
        pv_done = sem("pv_done")
        att_ready = sem("att_ready")
        gate_turned = sem("gate_turned")
        gate_hi = sem("gate_hi")
        gate_split = sem("gate_split")
        logits_done = sem("logits_done")
        route_step = sem("route_step")
        route_exp = sem("route_exp")
        cwx_ready = sem("cwx_ready")
        cw_turned = sem("cw_turned")
        cw_ready = sem("cw_ready")
        f_hi = sem("f_hi")
        f_lo = sem("f_lo")
        f_used = sem("f_used")
        sig_ready = sem("sig_ready")
        gated = sem("gated")
        hid_ready = sem("hid_ready")
        hid_hi = sem("hid_hi")
        hid_split = sem("hid_split")
        tile_done = sem("tile_done")
        res_ready = sem("res_ready")
        chosen_ready = sem("chosen_ready")
        slots_counted = sem("slots_counted")
        flag_ready = sem("flag_ready")
        slot_step = sem("slot_step")
        hot_ready = sem("hot_ready")
        tok_made = sem("tok_made")
        tok_ready = sem("tok_ready")
        rows_made = sem("rows_made")
        scratch_written = sem("scratch_written")
        rows_in = [sem(f"rows_in{n}") for n in range(2)]
        xg_turned = sem("xg_turned")
        xg_hi = sem("xg_hi")
        xg_split = sem("xg_split")
        banks_read = sem("banks_read")
        expert_done = sem("expert_done")
        low_in = [sem(f"low_in{t}") for t in range(T)]
        low_added = sem("low_added")
        high_added = sem("high_added")
        last_hi = sem("last_hi")
        last_split = sem("last_split")
        last_spread = sem("last_spread")
        high_in = [sem(f"high_in{t}") for t in range(T)]

        block = ctx.enter_context(nc.Block())

        def flat(a):
            return a[:].rearrange("p t n -> p (t n)")

        keys_per_unit = [0, 2, 2, 2, 3, 3]
        WARM_UP = 24
        KEEP_UP = 26

        U_INNER = 3 * KD
        U_OUT = 6 * KD
        U_ALL = 7 * KD
        C_LN = 2 * T

        def c_base(r):
            return C_LN + 6 + 8 * (r - 2)

        C_OUT = c_base(9) + 2
        C_LN2 = C_OUT + KD

        def turn_count(r, what, first):
            if first:
                return C_LN + turn_order(True).index(what)
            return c_base(r) + turn_order(False, r).index(what)

        def turn_order(first, r=None):
            if first:
                return ["V", "P0", "P1", "P2", "P3", "P4"]
            if isinstance(r, int) and r == 9:
                return ["P5", "O"]
            return ["V", "P5", "P0", "O", "P1", "P2", "P3", "P4"]

        def turn_parity(what, first, r=None):
            return turn_order(first, r).index(what) % 2

        def f_w1(s):
            return 3 * s - 1 if not (isinstance(s, int) and s == 0) else 0

        def f_w3(s):
            return f_w1(s) + 1

        def f_w2(s):
            return 3 * s + (2 if isinstance(s, int) and s == NS - 1 else 4)

        w1_slot = [0, 3]
        w2_slot = [5, 2]

        def slot_count(slot, nth):
            return 16 * (nth + (11 if slot < 2 else 9 if slot in w2_slot else 10))

        def w1_landed(s_half, par, w):
            return slot_count(w1_slot[par] + w, s_half + 1)

        def w2_landed(s_half, par):
            return slot_count(w2_slot[par], s_half + 1)

        PT = 2 * FULL

        def l_w1(g, j):
            return 3 * PT * g + (6 + (3 * j - 1 if j else 0))

        def l_w3(g, j):
            return l_w1(g, j) + 1

        def l_w2(g, j):
            return 3 * PT * g + (6 + 3 * j + (2 if j == PT - 1 else 4))

        def l_before(g, what, j):
            if j >= 2:
                return (l_w1, l_w3, l_w2)[what](g, j - 2) + 1
            return 3 * PT * g + ((1, 2, 5), (3, 4, 6))[j][what]

        inner = [(wiq, "q"), (wik, "k"), (wiv, "v")]
        rows = lambda w: w.rearrange("(r p) i -> r p i", p=P)

        def choose(engine, engine_type, dense, sparse):
            engine.wait_ge(flag_ready, 1)
            most = nc.values_load(flag[0:1, 0:1], engines=[engine_type], min_val=0, max_val=N)
            with engine.If(most > CAP):
                dense()
            with engine.Else():
                sparse()

        @block.sync
        def _(sp):
            for t in range(T):
                sp.dma_start(x[:, t, :], x_d[P * t:P * (t + 1), :]).then_inc(x_in[t], 16)
            outer = [(w, i) for w in (wq, wk, wv) for i in range(2)]
            inner_w = [(w, i) for i in range(2) for w, _ in inner]
            for k, (w, i) in enumerate(outer):
                sp.dma_start(raw[k][:], rows(w)[i]).then_inc(raw_in[k], 16)

            def stack(it, i, n, parts, own):
                split = (y_split, 4 * it + (2 * i + U_INNER - 16 + n))
                copied = (stack_copied, 4 * it + (2 * i - 16 + n))
                sp.wait_ge(*(split if n == 1 else copied))
                sp.dma_start(parts[1][0:DH, :], own[1][DH:P, :]).then_inc(stacked[i], 16)
                sp.wait_ge(*(copied if n == 1 else split))
                sp.dma_start(parts[0][DH:P, :], own[0][0:DH, :]).then_inc(stacked[i], 16)

            def round_(it, blocks, base, stacks=False):
                for k, (w, i) in enumerate(blocks):
                    sp.wait_ge(w_turned, 12 * it + (2 * k - 10))
                    sp.dma_start(raw[k][:], rows(w)[base + i]).then_inc(raw_in[k], 16)
                    if stacks and k in (2, 5):
                        stack(it - 1, k // 3, 1, q2_hi[k // 3], (q2[k // 3][1], q2[k // 3][1]))
                    if stacks and k in (3, 5):
                        stack(it - 1, k // 4, 2, k2_hi[k // 4], k2_hi[k // 4])

            with sp.Fori(1, 4) as it:
                round_(it, outer, 2 * it)
            round_(4, inner_w, 0)
            with sp.Fori(5, 8) as it:
                round_(it, inner_w, 2 * it - 8, True)
            round_(8, [(wo, i) for i in range(6)], 0, True)
            round_(9, [(wo, i) for i in range(2)], 6)

            def load13(slot, w, e, col):
                dst = raw[slot][:].rearrange("p (k c) -> p k c", k=KD)
                sp.dma_start(dst, w[e].rearrange("(k p) c -> p k c", p=P)[:, :, ds(col, P)]
                             ).then_inc(raw_in[slot], 16)

            for s in range(2):
                for w, slot in ((w1, w1_slot[s]), (w3, w1_slot[s] + 1)):
                    sp.wait_ge(w_turned, 2 * (U_OUT + (6 if slot < 2 else 0) + slot) + 2)
                    dst = raw[slot][:].rearrange("p (k c) -> p k c", k=KD)
                    for half, e, col in ((0, 2 * s, HID - HALF), (1, 2 * s + 1, 0)):
                        sp.dma_start(dst[:, :, HALF * half:HALF * (half + 1)],
                                     w[e].rearrange("(k p) c -> p k c", p=P)[:, :, col:col + HALF]
                                     ).then_inc(raw_in[slot], 16)
            w2_rows = w2.rearrange("e h d -> (e h) d")
            for s in range(2):
                sp.wait_ge(w_turned, 2 * (U_OUT + w2_slot[s]) + 2)
                row = 2 * s * HID + HID - HALF
                sp.dma_start(raw[w2_slot[s]][:], w2_rows[row:row + P, :]).then_inc(raw_in[w2_slot[s]], 16)
            for t in range(T):
                sp.wait_ge(xn_ready, T + t + 1)
                sp.dma_start(xn_dram[P * t:P * (t + 1), :], xn[:, t, :]).then_inc(scratch_written, 16)

            def step_loads(i, e, first):
                par = e % 2
                s = 4 * i + (2 + e)
                col = P * i + (HALF if par else 0)
                for j, w in enumerate((w1, w3)):
                    sp.wait_ge(f_lo, f_w1(s - 2) + j + 1)
                    load13(w1_slot[par] + j, w, e, col)
                slot = w2_slot[1 - par]
                if first and e == 0:
                    return
                pe_, pi = (NE - 1, i - 1) if e == 0 else (e - 1, i)
                row = P * pi + (HALF if pe_ % 2 else 0)
                sp.wait_ge(f_lo, f_w2(s - 3) + 1)
                sp.dma_start(raw[slot][:], w2[pe_][ds(row, P), :]
                             ).then_inc(raw_in[slot], 16)

            def dense():
                for e in range(NE):
                    step_loads(0, e, True)
                with sp.Fori(1, FULL) as i:
                    for e in range(NE):
                        step_loads(i, e, False)
                sp.wait_ge(f_lo, f_w2(NS - 3) + 1)
                sp.dma_start(raw[w2_slot[1]][:], w2[NE - 1, HID - P:HID, :]).then_inc(raw_in[w2_slot[1]], 16)
                for t in range(T):
                    sp.wait_ge(res_ready, 2 * t + 2)
                    sp.dma_start(out_d[P * t:P * (t + 1), :], res[:, t, :]).then_inc(out_done, 16)
                sp.wait_ge(out_done, 16 * T)

            def load_expert(slot, w, g, h, col):
                sp.dma_start(raw[slot][:].rearrange("p (o k c) -> p o k c", o=1, k=KD),
                             w.rearrange("e (k p) c -> p e k c", p=P)[:, ds(2 * g + h, 1), :, col:col + P]
                             ).then_inc(raw_in[slot], 16)

            def load_w2(g, j):
                h, i = j // FULL, j % FULL
                slot = w2_slot[j % 2]
                sp.wait_ge(f_lo, l_before(g, 2, j))
                sp.dma_start(raw[slot][:], w2_rows[ds(2 * HID * g + (HID * h + HALF * h + P * i), P), :]
                             ).then_inc(raw_in[slot], 16)

            def sparse():
                with sp.Fori(0, NE // 2) as g:
                    for j in range(PT):
                        h, i = j // FULL, j % FULL
                        for n, w in enumerate((w1, w3)):
                            sp.wait_ge(f_lo, l_before(g, n, j))
                            load_expert(w1_slot[j % 2] + n, w, g, h, P * i + HALF * h)
                        if j >= 1:
                            load_w2(g, j - 1)
                    load_w2(g, PT - 1)
                for n in range(2 * T):
                    t, cols = n % T, slice(512 * (n // T), 512 * (n // T + 1))
                    sp.wait_ge(res_ready, n + 1)
                    sp.dma_start(out_d[P * t:P * (t + 1), cols], x[:, t, cols]).then_inc(out_done, 16)
                sp.wait_ge(out_done, 16 * 2 * T)

            choose(sp, nc.sync.engine, dense, sparse)

        @block.gpsimd
        def _(pool):
            steps = [0]

            def link(ins):
                steps[0] += 1
                ins.then_inc(pool_step, 1)
                pool.wait_ge(pool_step, steps[0])

            pool.memset(ident[:], 0.0)
            link(pool.memset(mhalf[:], -0.5))
            pool.affine_select(out=ident[:], in_=ident[:], compare_op=ALU.not_equal, fill=1.0, base=0,
                               pattern=[[-1, P]], channel_multiplier=1).then_inc(ident_ready, 1)
            pool.memset(upper[:], 1.0)
            pool.memset(before[:], 1.0)
            pool.memset(after[:], 1.0)
            pool.iota(batch_i[:], pattern=[[4, NB]], base=32, channel_multiplier=0)
            link(pool.iota(iota_i[:], pattern=[[1, N]], base=0, channel_multiplier=0))

            def rstd_of(t, step, count):
                pool.wait_ge(step, count)
                pool.tensor_tensor(rstd[:, t:t + 1], veps[:, t:t + 1], mhalf[:, t:t + 1], ALU.pow).then_inc(rstd_made, 1)

            for t in range(T):
                rstd_of(t, norm_step, 4 * t + 4)
            pool.affine_select(out=upper[:], in_=upper[:], compare_op=ALU.is_gt, fill=0.0, base=0,
                               pattern=[[1, P]], channel_multiplier=-1)
            pool.affine_select(out=before[:], in_=before[:], compare_op=ALU.is_gt, fill=0.0, base=0,
                               pattern=[[1, NE], [-1, NE]], channel_multiplier=0)
            pool.affine_select(out=after[:], in_=after[:], compare_op=ALU.is_gt, fill=0.0, base=0,
                               pattern=[[-1, NE], [1, NE]], channel_multiplier=0)
            pool.tensor_copy(batch_e[:], batch_i[:]).then_inc(consts, 1)
            pool.wait_ge(edge_step, 1)
            for n in range(NB // 4):
                pool.tensor_copy(keyb[:, 4 * n:4 * n + 4, :],
                                 edge[:, 3, 4 * n:4 * n + 4].unsqueeze(2).to_broadcast([P, 4, P])
                                 ).then_inc(keyb_ready, 1)
            link(pool.memset(diag_col[:], 0.0))
            pool.affine_select(out=diag_col[:], in_=diag_col[:], compare_op=ALU.not_equal, fill=1.0, base=0,
                               pattern=[[-P, T], [1, N]], channel_multiplier=-1)
            pool.tensor_copy(iota[:], iota_i[:])
            pool.memset(ones16[:], 1.0)
            link(pool.iota(ids_i[:], pattern=[[P, T]], base=1, channel_multiplier=1))
            pool.tensor_copy(ids[:], ids_i[:])
            pool.tensor_copy(upper16[:], upper[:])
            pool.tensor_scalar(diag_w[:], ident[:], 2.0 ** (30 - 127), None, ALU.mult).then_inc(consts, 1)
            for t in range(T):
                pool.wait_ge(types_ready, t + 1)
                for k in range(4):
                    ins = pool.tensor_tensor(negmask[:, t, :], negmask[:, t, :], type_part[:, t, k, :], ALU.add)
                    if k < 3:
                        link(ins)
                ins.then_inc(mask_ready, 1)
            for t in range(T):
                rstd_of(t, norm2_step, KD * T + 2 * (t + 1))
            pool.wait_ge(route_step, 11)
            for e in range(NE):
                ins = pool.tensor_copy(cwx[e], cw[:, :, e].unsqueeze(2).to_broadcast([P, T, P]))
            ins.then_inc(cwx_ready, 1)

            def gather(dst, src, index, landed):
                pool.indirect_dma_start(dst, None, src, bass.IndirectOffsetOnAxis(ap=index, axis=0)
                                        ).then_inc(landed, 16)

            def sparse():
                pool.wait_ge(tok_ready, ST)
                pool.wait_ge(scratch_written, 16 * T)
                for e in range(NE + 1):
                    if e >= 2:
                        pool.wait_ge(xg_turned, 4 * (e - 1))
                    for st, rows_ in enumerate(SR):
                        c = NE * st + e % NE
                        gather(xrows[e % 2][0:rows_, st, :], xn_dram[:], tok[0:rows_, c:c + 1], rows_in[e % 2])
                pool.wait_ge(rows_made, 1)
                pool.wait_ge(scratch_written, 16 * T + 16 * ST * (NE - 1))
                for n, (dst, landed) in enumerate(((low, low_in), (high, high_in))):
                    for t in range(T):
                        gather(dst[t], y_dram[0:(NE - 1) * CAP, :], row_i[n][:, t:t + 1], landed[t])
                for t in range(T):
                    pool.wait_ge(low_in[t], 16)
                    link(pool.tensor_scalar(low[t], low[t], wgt[0][:, t:t + 1], None, ALU.mult))
                    pool.tensor_tensor(x[:, t, :], x[:, t, :], low[t], ALU.add).then_inc(low_added, 1)

            choose(pool, nc.gpsimd.engine, lambda: None, sparse)

        @block.tensor
        def _(pe):
            def turn3(c, out_bank_, srcs):
                for j in range(3):
                    mm = pe.transpose(out_bank_[:, P * j:P * (j + 1)], srcs(j), ident[:])
                mm.then_inc(t3_turned, 1)

            def layer_norm_turns(c0, t):
                pe.wait_ge(xn_ready, (T if c0 else 0) + t + 1)
                for c in (2 * t, 2 * t + 1):
                    if c0 + c >= 4:
                        pe.wait_ge(t3_split, c0 + c - 3)
                    for j in range(4):
                        k = 4 * (c % 2) + j
                        mm = pe.transpose(ln_bank[c % 4][:, P * j:P * (j + 1)], xn[:, t, P * k:P * (k + 1)], ident[:])
                    mm.then_inc(t3_turned, 1)

            def turn_w(it, k, first=False):
                pe.wait_ge(raw_in[k], 16 * (it + 1))
                for half in range(2):
                    if not first:
                        pe.wait_ge(w_lo, 12 * it + (2 * k - 1 + half))
                    for j in range(4):
                        kk = 4 * half + j
                        mm = pe.transpose(turn_bank[half][:, P * j:P * (j + 1)],
                                          raw[k][:, P * kk:P * (kk + 1)], ident[:])
                    mm.then_inc(w_turned, 1)

            def turn_next(it, k):
                turn_w(it if k < 5 else it + 1, (k + 1) % 6)

            def w_ready(it, k):
                pe.wait_ge(w_lo, 12 * it + (2 * k + 2))

            def product(acc, w, act, ks, last):
                for k in ks:
                    for wi, ai in ((0, 0), (0, 1), (1, 0)):
                        mm = pe.matmul(acc, w[wi][:, k, :], act[ai][:, k, :],
                                       start=(k == 0 and wi == 0 and ai == 0),
                                       stop=(k == KD - 1 and wi == 1))
                if last:
                    mm.then_inc(mm_done, 1)

            def key_turns(n):
                pe.wait_ge(keyb_ready, n + 1)
                if n >= 2:
                    pe.wait_ge(keys_compared, n - 1)
                for j in range(4):
                    mm = pe.transpose(score_bank[n % 2][:, P * j:P * (j + 1)], keyb[:, 4 * n + j, :], ident[:])
                mm.then_inc(keys_turned, 1)

            def diagonal(start):
                for t in range(T):
                    mm = pe.matmul(edge_bank[t][:, 0:N], diag_w[:], diag_col[:, t, :], start=start, stop=not start)
                if not start:
                    mm.then_inc(edges_summed, 1)

            def add_batch(it, n):
                pe.wait_ge(oh_ready, 16 * it + (n - 15))
                for t in range(T):
                    mm = pe.matmul(edge_bank[t][:, 0:N], oh_src[n % OH][:, P * t:P * (t + 1)], oh_dst[n % OH][:],
                                   start=False, stop=False)
                mm.then_inc(oh_used, 1)

            pe.wait_ge(ident_ready, 1)
            for _ in range(WARM_UP):
                pe.transpose(turn_bank[1][:, 0:P], ident[:], ident[:])
            layer_norm_turns(0, 0)
            turn_w(0, 0, first=True)
            pe.wait_ge(edges_f_ready, 1)
            for j in range(4):
                mm = pe.transpose(acc_bank[1][:, 64 * j:64 * j + NB], edges_f[:, j, :], ident[0:NB, 0:NB])
            mm.then_inc(edges_turned, 1)
            layer_norm_turns(0, 1)
            layer_norm_turns(0, 2)
            w_ready(0, 0)
            for t in range(T):
                pe.wait_ge(t3_split, 2 * (t + 1))
                cols = slice(P * t, P * (t + 1))
                product(acc_bank[0][:, cols], wb[0], [xt[0][:, :, cols], xt[1][:, :, cols]], range(KD), t == T - 1)
                if t == 0:
                    turn_next(0, 0)
                elif t == 1:
                    pe.wait_ge(bias_in, 16 * 7)
                    pe.transpose(pv_bank[:, 0:7 * KD], bias_rows[:],
                                 ident[0:7 * KD, 0:7 * KD]).then_inc(bias_turned, 1)
            n = 0
            for k in range(1, 6):
                turn_next(0, k)
                w_ready(0, k)
                if k == 1:
                    pe.wait_ge(edge_step, 2)
                else:
                    pe.wait_ge(y_hi, k - 1)
                    pe.wait_ge(y_ready, k - 1)
                product(acc_bank[k % 2][:, 0:N], wb[k % 3], xt, range(KD), True)
                for _ in range(keys_per_unit[k]):
                    key_turns(n)
                    n += 1
            pe.wait_ge(keys_compared, NB // 4)
            pe.wait_ge(consts, 2)
            diagonal(True)
            per_unit = [3, 3, 3, 3, 2, 2]
            with pe.Fori(1, 4) as it:
                n = 0
                for k in range(6):
                    turn_next(it, k)
                    w_ready(it, k)
                    pe.wait_ge(y_hi, 6 * it + (k - 1))
                    pe.wait_ge(y_ready, 6 * it + (k - 1))
                    product(acc_bank[k % 2][:, 0:N], wb[k % 3], xt, range(KD), True)
                    for _ in range(per_unit[k]):
                        add_batch(it, n)
                        n += 1
            diagonal(False)

            def att_step(r, par, k, scores, tail, first):
                a = 6 * r + (k - 6)
                tp = 1 - par
                if scores:
                    hh, t = k // 3, k % 3
                    lo, hi = DH * hh, DH * (hh + 1)
                    if k < 2:
                        pe.wait_ge(y_split, 2 * r + U_INNER)
                        pe.wait_ge(stacked[par], 32 * r + (32 if par == 0 else 0))
                    if not (first and k < 2):
                        pe.wait_ge(masked_max, a - 1)
                    q_stack = q2_hi[par][hh]
                    pe.matmul(score_bank[k % 2][:, 0:N], q_stack[:, P * t:P * (t + 1)], k2_hi[par][hh][:],
                              start=True, stop=False)
                    mm = pe.matmul(score_bank[k % 2][:, 0:N], q_stack[lo:hi, P * t:P * (t + 1)],
                                   k2[par][1][lo:hi, :], start=False, stop=True)
                    mm.then_inc(scored, 1)
                if (k == 0 and tail) or (k > 0 and scores):
                    c = turn_count(r, f"P{(k - 1) % 6}", first)
                    pe.wait_ge(prob_ready, a)
                    pe.wait_ge(t3_split, c)
                    turn3(c, t3_bank, lambda j: probs[(k - 1) % 2][:, P * j:P * (j + 1)])
                if (k < 2 and tail) or (k >= 2 and scores):
                    kk = (k - 2) % 6
                    vb = v2[tp if k < 2 else par]
                    hh = kk // 3
                    c = turn_count(r, f"P{kk}", first) if k >= 2 else None
                    if k >= 2:
                        pe.wait_ge(t3_split, c + 1)
                    elif k == 1:
                        pe.wait_ge(t3_split, turn_count(r, "P5", False) + 1)
                    else:
                        pe.wait_ge(t3_split, c_base(r))
                    if not (first and k == 2):
                        pe.wait_ge(att_ready, a - 2)
                    n = 0
                    for j in range(T):
                        for pi, vi in ((0, 0), (0, 1), (1, 0)):
                            mm = pe.matmul(pv_bank[:, 0:DH], pt[k % 2][pi][:, j, :],
                                           vb[vi][:, j, DH * hh:DH * (hh + 1)], start=(n == 0), stop=(n == 8))
                            n += 1
                    mm.then_inc(pv_done, 1)

            def value_turn(r, first):
                c = turn_count(r, "V", first)
                pe.wait_ge(y_ready, 3 * r + U_INNER)
                pe.wait_ge(t3_split, c)
                turn3(c, t3_bank, lambda j: yv[:, P * j:P * (j + 1)])

            def output_turn(r, tp):
                c = turn_count(r, "O", False)
                pe.wait_ge(att_ready, 6 * r - 6)
                pe.wait_ge(t3_split, c)
                turn3(c, t3_bank, lambda j: att[tp][:, j, :])

            def inner_phase(r, it, i, first, att_on, tail):
                for m, n in enumerate("qkv"):
                    k6 = 3 * i + m
                    turn_next(it, k6)
                    w_ready(it, k6)
                    if first:
                        pe.wait_ge(y_split, U_INNER - 4 + 2 * m)
                    pe.wait_ge(y_ready, 6 * it + (k6 - 1))
                    pe.wait_ge(y_hi, 2 * r + (U_INNER + (m == 2)) if not (first and m == 0) else U_INNER - 1)
                    acc = acc_bank[(i + m) % 2][:, 0:N]
                    product(acc, wb[m], proj[n], range(0, 1), False)
                    if m == 0 and att_on:
                        value_turn(r, not tail)
                    if m == 1 and tail:
                        output_turn(r, i)
                    product(acc, wb[m], proj[n], range(1, 3), False)
                    if att_on:
                        att_step(r, 1 - i, 2 * m, True, tail, not tail)
                    product(acc, wb[m], proj[n], range(3, 6), False)
                    if att_on:
                        att_step(r, 1 - i, 2 * m + 1, True, tail, not tail)
                    product(acc, wb[m], proj[n], range(6, KD), True)

            inner_phase(0, 4, 0, True, False, False)
            pe.wait_ge(types_ready, T)
            inner_phase(1, 4, 1, False, True, False)
            with pe.Fori(5, 8) as it:
                for i in range(2):
                    inner_phase(2 * it + (i - 8), it, i, False, True, True)
            def early(r, ks):
                product(acc_bank[r][:, 0:N], wb[r], ot, ks, False)

            turn_next(8, 0)
            w_ready(8, 0)
            pe.wait_ge(y_ready, U_OUT)
            value_turn(8, False)
            for k in range(6):
                if k == 2:
                    output_turn(8, 0)
                early(0, [k])
                att_step(8, 1, k, True, True, False)
            w_ready(8, 1)
            early(1, [0])
            att_step(9, 0, 0, False, True, False)
            early(1, [1, 2])
            att_step(9, 0, 1, False, True, False)
            early(1, [3, 4, 5])
            output_turn(9, 1)

            def out_turn(r):
                c = C_OUT + r
                pe.wait_ge(y_ready, U_OUT + r + 1)
                pe.wait_ge(t3_split, c)
                turn3(c, t3_bank, lambda j: ybuf[r % 2][:, P * j:P * (j + 1)])

            pe.wait_ge(t3_split, C_OUT)
            for r in range(KD):
                u = U_OUT + r
                if 1 <= r < KD - 1:
                    turn_w((u + 1) // 6, (u + 1) % 6)
                if r >= 2:
                    w_ready(u // 6, u % 6)
                    pe.wait_ge(y_ready, u - 1)
                acc = acc_bank[u % 2][:, 0:N]
                if r >= 2:
                    product(acc, wb[u % 3], ot, range(3), False)
                if r >= 1:
                    out_turn(r - 1)
                product(acc, wb[u % 3], ot, range(3 if r >= 2 else 6, KD), True)
            pe.wait_ge(gate_in, 16)
            pe.wait_ge(y_ready, U_ALL)
            for k in range(KD):
                mm = pe.transpose(acc_bank[1][:, NE * k:NE * (k + 1)], gate_n[:, P * k:P * (k + 1)], ident[0:NE, 0:NE])
            mm.then_inc(gate_turned, 1)
            out_turn(KD - 1)
            for _ in range(KEEP_UP):
                pe.transpose(turn_bank[1][:, 0:P], ident[:], ident[:])
            for t in range(T):
                layer_norm_turns(C_LN2, t)

            pe.wait_ge(gate_split, 1)
            pe.wait_ge(f_lo, 1)
            for t in range(T):
                pe.wait_ge(t3_split, C_LN2 + 2 * (t + 1))
                cols = slice(P * t, P * (t + 1))
                n = 0
                for k in range(KD):
                    for xi, gi in ((0, 0), (0, 1), (1, 0)):
                        mm = pe.matmul(acc_bank[1][:, 64 + NE * t:64 + NE * (t + 1)], xt[xi][:, k, cols],
                                       gt[gi][:, k, :], start=(n == 0), stop=(n == 3 * KD - 1))
                        n += 1
                if t == T - 1:
                    mm.then_inc(logits_done, 1)
                for k in range(KD):
                    for wi, ai in ((0, 0), (0, 1), (1, 0)):
                        mm = pe.matmul(bank[0][:, cols], wb[0][wi][:, k, :], xt[ai][:, k, cols],
                                       start=(k == 0 and wi == 0 and ai == 0), stop=(k == KD - 1 and wi == 1))
            mm.then_inc(f_used, 1)

            def up(s, which, ks=range(KD)):
                if 0 in ks:
                    pe.wait_ge(f_lo, f_w1(s) + which + 1)
                    if not (isinstance(s, int) and s == 0):
                        pe.wait_ge(gated, 2 * s - 1 + which)
                w = wb[which]
                for k in ks:
                    for wi, ai in ((0, 0), (0, 1), (1, 0)):
                        mm = pe.matmul(bank[which][:, 0:N], w[wi][:, k, :], xt[ai][:, k, :],
                                       start=(k == 0 and wi == 0 and ai == 0), stop=(k == KD - 1 and wi == 1))
                if KD - 1 in ks:
                    mm.then_inc(f_used, 1)

            def down(s, par, first=False, last=False):
                pe.wait_ge(f_lo, f_w2(s) + 1)
                pe.wait_ge(hid_split, s + 1)
                w = [wb[2][i][:].rearrange("p k c -> p (k c)") for i in range(2)]
                for t in range(T):
                    for half in range(2):
                        for n, (hi_, wi) in enumerate(((0, 0), (0, 1), (1, 0))):
                            mm = pe.matmul(out_bank[2 * t + half][:], ht[par][hi_][:, P * t:P * (t + 1)],
                                           w[wi][:, 512 * half:512 * (half + 1)],
                                           start=(first and n == 0), stop=(last and n == 2))
                        if last:
                            mm.then_inc(tile_done, 1)
                if not last:
                    mm.then_inc(f_used, 1)

            up(0, 1, range(0, 5))
            pe.wait_ge(consts, 2)
            pe.wait_ge(chosen_ready, 1)
            for t in range(T + 1):
                for n in range(min(t + 1, T)):
                    mm = pe.matmul(slot_bank[:, NE * t:NE * (t + 1)], (upper16 if n == t else ones16)[:],
                                   chosen16[:, n, :], start=(n == 0), stop=(n == min(t, T - 1)))
            mm.then_inc(slots_counted, 1)
            up(0, 1, range(5, KD))
            up(1, 0)
            pe.wait_ge(hot_ready, 1)
            for c in range(NE * ST):
                st, e = c // NE, c % NE
                for t in range(T):
                    mm = pe.matmul(tok_bank[0:SR[st], c:c + 1], slot_hot[e][:, t, P * st:P * st + SR[st]],
                                   ids[:, t:t + 1], start=(t == 0), stop=(t == T - 1))
            mm.then_inc(tok_made, 1)
            pe.wait_ge(cwx_ready, 1)
            for e in range(NE):
                for t in range(T):
                    mm = pe.transpose(bank[2 + e][:, P * t:P * (t + 1)], cwx[e][:, t, :], ident[:])
                mm.then_inc(cw_turned, 1)
            up(1, 1)
            pe.wait_ge(cw_ready, NE)
            pe.wait_ge(tok_ready, ST)
            down(0, 0, first=True)

            def dense():
                with pe.Fori(0, FULL) as i:
                    for e in range(NE):
                        s = 4 * i + (2 + e)
                        up(s, 0)
                        up(s, 1)
                        down(s - 1, (e + 1) % 2)
                down(NS - 1, 1, last=True)

            def turn_rows(e_par, q, banks):
                for k in range(2):
                    for st, rows_ in enumerate(SR):
                        mm = pe.transpose(banks[q % 2][:, CAP * k + P * st:CAP * k + P * st + rows_],
                                          xrows[e_par][0:rows_, st, P * (2 * q + k):P * (2 * q + k + 1)],
                                          ident[0:rows_, 0:rows_])
                mm.then_inc(xg_turned, 1)

            def sparse_up(g, j, which):
                pe.wait_ge(f_lo, l_w1(g, j) + (which + 1))
                if which == 0:
                    pe.wait_ge(gated, PT * g + (4 + j))
                    if j % FULL == 0:
                        pe.wait_ge(xg_split, 8 * g + (4 * (j // FULL) + 4))
                else:
                    pe.wait_ge(hid_ready, PT * g + (2 + j))
                w, xe = wb[which], xg[j // FULL]
                for k in range(KD):
                    for wi, ai in ((0, 0), (0, 1), (1, 0)):
                        mm = pe.matmul(bank[which][:, 0:CAP], w[wi][:, k, :], xe[ai][:, k, :],
                                       start=(k == 0 and wi == 0 and ai == 0), stop=(k == KD - 1 and wi == 1))
                mm.then_inc(f_used, 1)

            def sparse_down(g, j):
                h, i = j // FULL, j % FULL
                pe.wait_ge(f_lo, l_w2(g, j) + 1)
                pe.wait_ge(hid_split, PT * g + (3 + j))
                if i == 0:
                    pe.wait_ge(banks_read, 8 * g + (2 * T + 4 * h))
                w = w2b[j % 2]
                for half in range(2):
                    for st, rows_ in enumerate(SR):
                        for n, (hi_, wi) in enumerate(((0, 0), (0, 1), (1, 0))):
                            mm = pe.matmul(out_bank[2 * st + half][0:rows_, :], ht[j % 2][hi_][:, P * st:P * st + rows_],
                                           w[wi][:, 512 * half:512 * (half + 1)],
                                           start=(i == 0 and n == 0), stop=(i == FULL - 1 and n == 2))
                        if i == FULL - 1 and not (st == ST - 1 and half == 1):
                            mm.then_inc(expert_done, 1)
                mm.then_inc(f_used, 1)

            def sparse():
                pe.wait_ge(rows_in[0], 16 * ST)
                pe.wait_ge(gated, 4)
                turn_rows(0, 0, bank[0:2])
                turn_rows(0, 1, bank[0:2])
                down_mixed(0)
                down_mixed(1)
                for q in (2, 3):
                    pe.wait_ge(xg_split, q - 1)
                    turn_rows(0, q, bank[0:2])
                down_mixed(2)
                with pe.Fori(0, NE // 2) as g:
                    for j in range(PT):
                        h, i = j // FULL, j % FULL
                        sparse_up(g, j, 0)
                        sparse_up(g, j, 1)
                        if j >= 1:
                            sparse_down(g, j - 1)
                        if i < FULL - 1:
                            q = i
                            if q == 0:
                                pe.wait_ge(banks_read, 2 * T)
                                pe.wait_ge(rows_in[1 - h], 16 * ST * g + 16 * ST * (1 + h))
                            pe.wait_ge(xg_split, 8 * g + (4 * h + 3 + q))
                            turn_rows(1 - h, q, bank[6:8])
                    sparse_down(g, PT - 1)
                for n in range(2 * T):
                    half, t = n // T, n % T
                    dst = (bank[6], bank[7], bank[0], bank[1])[n % 4]
                    if n == 0:
                        pe.wait_ge(xg_split, 4 * (NE + 1))
                    if n == 2:
                        pe.wait_ge(gated, NE * FULL + 4)
                        pe.wait_ge(hid_ready, NE * FULL + 2)
                    if n >= 4:
                        pe.wait_ge(res_ready, n - 3)
                    if t == 0:
                        pe.wait_ge(last_split, ST * (half + 1))
                    for st, rows_ in enumerate(SR):
                        for part in range(2):
                            mm = pe.matmul(dst[:], last_hot[0:rows_, st, P * t:P * (t + 1)],
                                           last16[part][0:rows_, st, 512 * half:512 * (half + 1)],
                                           start=(st == 0 and part == 0), stop=(st == ST - 1 and part == 1))
                    mm.then_inc(last_spread, 1)

            def down_mixed(t):
                if t == 0:
                    pe.wait_ge(f_lo, 6)
                    pe.wait_ge(hid_split, 2)
                for half in range(2):
                    for n, (hi_, wi) in enumerate(((0, 0), (0, 1), (1, 0))):
                        mm = pe.matmul(out_bank[2 * t + half][:], ht[1][hi_][:, P * t:P * (t + 1)],
                                       mixed_w[wi][:, 512 * half:512 * (half + 1)], start=False, stop=(n == 2))
                    if not (t == T - 1 and half == 1):
                        mm.then_inc(tile_done, 1)
                if t == T - 1:
                    mm.then_inc(f_used, 1)

            choose(pe, nc.tensor.engine, dense, sparse)

        @block.scalar
        def _(act):
            act.dma_start(edges_i[:, 0, :], src_d.rearrange("(b p) -> b p", p=P)).then_inc(edges_in, 16)
            act.dma_start(edges_i[:, 1, :], dst_d.rearrange("(b p) -> b p", p=P)).then_inc(edges_in, 16)
            act.dma_start(edges_i[:, 2, :], etype_d.rearrange("(b p) -> b p", p=P)).then_inc(edges_in, 16)
            act.dma_start(etw[:], etw_d.partition_broadcast(P)).then_inc(etw_in, 16)
            for n, b in enumerate((bq, bk, bv, biq, bik, biv, bo)):
                act.dma_start(bias_rows[KD * n:KD * (n + 1), :], b.rearrange("(r p) -> r p", p=P)).then_inc(bias_in, 16)

            def layer_norm_hi(c0, t):
                for c in (2 * t, 2 * t + 1):
                    half = c % 2
                    act.wait_ge(t3_turned, c0 + c + 1)
                    act.activation(xt[0][:, 4 * half:4 * half + 4, P * t:P * (t + 1)],
                                   ln_bank[c % 4][:].rearrange("p (k c) -> p k c", k=4), ACT.Copy).then_inc(t3_hi, 1)

            def w_part(it, k):
                if not (isinstance(it, int) and 6 * it + k < 3):
                    act.wait_ge(mm_done, 6 * it + (k - 2))
                for half in range(2):
                    act.wait_ge(w_turned, 12 * it + (2 * k + half + 1))
                    act.activation(wb[k % 3][0][:, 4 * half:4 * half + 4, :],
                                   turn_bank[half][:].rearrange("p (k c) -> p k c", k=4), ACT.Copy,
                                   scale=W_SCALE).then_inc(w_hi, 1)

            def w_ahead(it, k):
                w_part(it if k < 5 else it + 1, (k + 1) % 6)

            layer_norm_hi(0, 0)
            w_part(0, 0)
            layer_norm_hi(0, 1)
            layer_norm_hi(0, 2)
            def y_part(it, k, n, b, dst, count, scale):
                act.wait_ge(mm_done, 6 * it + (k + 1))
                act.activation(dst, acc_bank[k % 2][:, 0:N], ACT.Identity, bias=b, scale=scale).then_inc(y_hi, 1)

            act.wait_ge(bias_ready, 1)
            for k in range(6):
                w_ahead(0, k)
                n, i = k // 2, k % 2
                y_part(0, k, n, bias[:, n, i:i + 1], proj["qkv"[n]][0][:, i, :], k + 1, W_BACK)
                if k == 2:
                    act.wait_ge(soft_a, 1)
                    act.activation(sp_b[:], sp_a[:], ACT.Exp, scale=-1.0).then_inc(soft_b, 1)
                    act.wait_ge(soft_b, 1)
                    act.activation(sp_c[:], sp_b[:], ACT.Ln, bias=1.0).then_inc(soft_b, 1)
            with act.Fori(1, 4) as it:
                for k in range(6):
                    w_ahead(it, k)
                    n, i = k // 2, k % 2
                    y_part(it, k, n, bias[:, n, ds(2 * it + i, 1)], proj["qkv"[n]][0][:, 2 * it + i, :],
                           6 * it + (k + 1), W_BACK)

            def att_step(r, par, k, scores, tail, first):
                a = 6 * r + (k - 6)
                tp = 1 - par
                if (k == 0 and tail) or (k > 0 and scores):
                    c = turn_count(r, f"P{(k - 1) % 6}", first)
                    if not (first and k < 3):
                        act.wait_ge(pv_done, a - 2)
                    act.wait_ge(t3_turned, c + 1)
                    act.activation(pt[k % 2 ^ 1][0][:].rearrange("p t c -> p (t c)"), t3_bank[:, 0:N],
                                   ACT.Copy).then_inc(t3_hi, 1)
                if scores:
                    act.wait_ge(masked_max, a + 1)
                    act.activation(probs[k % 2][:], masked[k % 2][:], ACT.Exp, scale=-1.0,
                                   bias=negmax[:, k:k + 1], accum_out=rowsum[:, k:k + 1]).then_inc(prob_ready, 1)

            def value_part(r, par, first):
                c = turn_count(r, "V", first)
                act.wait_ge(t3_turned, c + 1)
                act.activation(v2[par][0][:].rearrange("p t c -> p (t c)"), t3_bank[:, 0:N],
                               ACT.Copy).then_inc(t3_hi, 1)

            def output_part(r):
                c = turn_count(r, "O", False)
                act.wait_ge(t3_turned, c + 1)
                act.activation(ot[0][:, r - 2, :], t3_bank[:, 0:N], ACT.Copy).then_inc(t3_hi, 1)

            def stack(count, parts):
                act.wait_ge(y_hi, count)
                act.activation(parts[1][DH:P, :], parts[0][DH:P, :], ACT.Copy).then_inc(stack_copied, 1)

            def inner_phase(r, it, i, att_on, tail):
                for m in range(3):
                    k6 = 3 * i + m
                    w_ahead(it, k6)
                    if m == 0 and att_on:
                        value_part(r, 1 - i, not tail)
                    if m == 1:
                        stack(2 * r + (U_INNER + 1), q2_hi[i])
                    elif m == 2:
                        stack(2 * r + (U_INNER + 2), k2_hi[i])
                    if m == 1 and tail:
                        output_part(r)
                    if att_on:
                        att_step(r, 1 - i, 2 * m, True, tail, not tail)
                        att_step(r, 1 - i, 2 * m + 1, True, tail, not tail)
                    if m == 0:
                        y_part(it, k6, 3, biasq[:, ds(r, 1)], q2[i][0][:], None, -0.125 * W_BACK)
                    elif m == 1:
                        y_part(it, k6, 4, bias[:, 4, ds(r, 1)], k2[i][0][:], None, W_BACK)

            inner_phase(0, 4, 0, False, False)
            act.dma_start(gate_n[:], gate_w[0:NE, :]).then_inc(gate_in, 16)
            inner_phase(1, 4, 1, True, False)
            with act.Fori(5, 8) as it:
                for i in range(2):
                    inner_phase(2 * it + (i - 8), it, i, True, True)
            w_part(8, 1)
            value_part(8, 1, False)
            for k in range(6):
                if k == 2:
                    output_part(8)
                att_step(8, 1, k, True, True, False)
            for k in range(2):
                att_step(9, 0, k, False, True, False)
            output_part(9)
            for r in range(2, KD):
                w_part((U_OUT + r) // 6, (U_OUT + r) % 6)

            def f_part(slot, landed, b, wait):
                act.wait_ge(raw_in[slot], landed)
                if wait is not None:
                    act.wait_ge(*wait)
                act.activation(wb[b][0][:].rearrange("p k c -> p (k c)"), raw[slot][:], ACT.Copy,
                               scale=W_SCALE).then_inc(f_hi, 1)

            f_part(0, w1_landed(0, 0, 0), 0, (mm_done, U_ALL - 1))
            f_part(1, w1_landed(0, 0, 1), 1, (mm_done, U_ALL))
            act.wait_ge(gate_turned, 1)
            act.activation(gt[0][:].rearrange("p k e -> p (k e)"), acc_bank[1][:, 0:NE * KD], ACT.Copy,
                           scale=W_SCALE).then_inc(gate_hi, 1)
            for t in range(T):
                layer_norm_hi(C_LN2, t)
            act.wait_ge(route_step, 3)
            act.activation(pr[:], lg[:], ACT.Exp).then_inc(route_exp, 1)
            act.activation(early_sig[:], lmax[:], ACT.Sigmoid)

            def step(s, s_half, par, nxt, own=True):
                b = par
                if nxt:
                    nh = s_half + (1 if par else 0)
                    f_part(w1_slot[1 - par], w1_landed(nh, 1 - par, 0), 0, (f_used, f_w1(s) + 1))
                act.wait_ge(f_used, f_w1(s) + 1)
                if not (isinstance(s, int) and s < 2):
                    act.wait_ge(gated, 2 * s - 3)
                act.activation(sig[b], bank[0][:, 0:N], ACT.Sigmoid, scale=W_BACK).then_inc(sig_ready, 1)
                if nxt:
                    f_part(w1_slot[1 - par] + 1, w1_landed(nh, 1 - par, 1), 1, (f_used, f_w3(s) + 1))
                first = isinstance(s, int) and s == 0
                if first:
                    f_part(w2_slot[par], w2_landed(s_half, par), 2, (mm_done, U_ALL - 2))
                act.wait_ge(hid_ready, s + 1)
                if not (isinstance(s, int) and s < 2):
                    act.wait_ge(f_used, f_w2(s - 2) + 1)
                act.activation(ht[b][0], hid[b], ACT.Copy).then_inc(hid_hi, 1)
                if own and not first:
                    f_part(w2_slot[par], w2_landed(s_half, par), 2, (f_used, f_w2(s - 1) + 1))

            step(0, 0, 0, True)
            step(1, 0, 1, False, own=False)

            def dense():
                f_part(w1_slot[0], w1_landed(1, 0, 0), 0, (f_used, f_w1(1) + 1))
                f_part(w1_slot[0] + 1, w1_landed(1, 0, 1), 1, (f_used, f_w3(1) + 1))
                f_part(w2_slot[1], w2_landed(0, 1), 2, (f_used, f_w2(0) + 1))
                with act.Fori(0, FULL - 1) as i:
                    for e in range(NE):
                        step(4 * i + (2 + e), 2 * i + (1 + e // 2), e % 2, True)
                for e in range(NE):
                    step(4 * (FULL - 1) + 2 + e, 2 * (FULL - 1) + 1 + e // 2, e % 2, e < NE - 1)

            def rows_hi(h, c, q, banks):
                act.wait_ge(xg_turned, c + 1)
                act.activation(xg_flat[h][0][:, 2 * CAP * q:2 * CAP * (q + 1)], banks[q % 2][:, 0:2 * CAP], ACT.Copy
                               ).then_inc(xg_hi, 1)

            def landed(g, j, w):
                nth = FULL * g + (2 + j // 2)
                return slot_count(w1_slot[j % 2] + w if w < 2 else w2_slot[j % 2], nth)

            def results(g, h):
                act.wait_ge(scratch_written, 32 * ST * g + 16 * (T + ST * h))
                for st, rows_ in enumerate(SR):
                    act.wait_ge(expert_done, 6 * g + (3 * h + st + 1))
                    act.activation(staged[0:rows_, st, 0:512], out_bank[2 * st][0:rows_, :], ACT.Copy, scale=W_BACK
                                   ).then_inc(banks_read, 1)
                act.wait_ge(banks_read, 8 * g + (2 * T + 4 * h + 4))
                for st, rows_ in enumerate(SR):
                    act.dma_start(y_dram[ds(2 * CAP * g + (CAP * h + P * st), rows_), :], staged[0:rows_, st, :]
                                  ).then_inc(scratch_written, 16)

            def sparse():
                act.wait_ge(raw_in[w2_slot[1]], w2_landed(0, 1))
                act.activation(mixed_w[0], raw[w2_slot[1]][:], ACT.Copy, scale=W_SCALE).then_inc(f_hi, 1)
                f_part(w1_slot[0], landed(0, 0, 0), 0, (f_used, l_before(0, 0, 1)))
                f_part(w1_slot[0] + 1, landed(0, 0, 1), 1, (f_used, l_before(0, 1, 1)))
                for q in range(4):
                    rows_hi(0, q, q, bank[0:2])
                with act.Fori(0, NE // 2) as g:
                    for j in range(PT):
                        h, i = j // FULL, j % FULL
                        b, nxt = j % 2, j < PT - 1
                        if nxt:
                            f_part(w1_slot[1 - b], landed(g, j + 1, 0), 0, (f_used, l_w1(g, j) + 1))
                        act.wait_ge(f_used, l_w1(g, j) + 1)
                        act.wait_ge(gated, PT * g + (j + 3))
                        act.activation(sig[b][:, 0:CAP], bank[0][:, 0:CAP], ACT.Sigmoid, scale=W_BACK
                                       ).then_inc(sig_ready, 1)
                        if nxt:
                            f_part(w1_slot[1 - b] + 1, landed(g, j + 1, 1), 1, (f_used, l_w3(g, j) + 1))
                        act.wait_ge(f_used, l_before(g, 2, j))
                        act.wait_ge(hid_ready, PT * g + (j + 3))
                        act.activation(ht[b][0][:, 0:CAP], hid[b][:, 0:CAP], ACT.Copy).then_inc(hid_hi, 1)
                        act.wait_ge(raw_in[w2_slot[b]], landed(g, j, 2))
                        act.activation(w2b[b][0], raw[w2_slot[b]][:], ACT.Copy, scale=W_SCALE).then_inc(f_hi, 1)
                        if j == FULL:
                            results(g, 0)
                        if i < FULL - 1:
                            rows_hi(1 - h, 8 * g + (4 * h + 4 + i), i, bank[6:8])
                    with act.If(g < NE // 2 - 1):
                        f_part(w1_slot[0], landed(g, PT, 0), 0, (f_used, l_w1(g, PT - 1) + 1))
                        f_part(w1_slot[0] + 1, landed(g, PT, 1), 1, (f_used, l_w3(g, PT - 1) + 1))
                        results(g, 1)
                act.wait_ge(xg_split, 4 * (NE + 1))
                for n in range(2 * ST):
                    half, st = n // ST, n % ST
                    if n < 2 * ST - 1:
                        act.wait_ge(expert_done, 3 * (NE - 1) + n + 1)
                    else:
                        act.wait_ge(f_used, l_w2(NE // 2 - 1, PT - 1) + 1)
                    act.activation(last16[0][0:SR[st], st, 512 * half:512 * (half + 1)],
                                   out_bank[2 * st + half][0:SR[st], :],
                                   ACT.Copy, scale=W_BACK).then_inc(last_hi, 1)

            choose(act, nc.scalar.engine, dense, sparse)

        @block.vector
        def _(dve):
            counts = {}

            def link(ins, s):
                counts[s] = counts.get(s, 0) + 1
                ins.then_inc(s, 1)
                dve.wait_ge(s, counts[s])

            def var_of(t, n, chunks, step, base):
                dve.bn_aggr(mv[:, t, :], stats[:, t, 0:chunks].rearrange("p h s -> p (h s)")).then_inc(step, 1)
                dve.wait_ge(step, base + 1)
                dve.tensor_scalar(veps[:, t:t + 1], mv[:, t, 1:2], EPS, None, ALU.add).then_inc(step, 1)

            def norm1_stats(t):
                dve.wait_ge(x_in[t], 16)
                for h in range(2):
                    dve.bn_stats(stats[:, t, h, :], x[:, t, 512 * h:512 * (h + 1)]).then_inc(norm_step, 1)
                dve.wait_ge(norm_step, 4 * t + 2)
                var_of(t, 1, 2, norm_step, 4 * t + 2)

            def normed(n, t):
                dve.wait_ge(rstd_made, T * (n - 1) + t + 1)
                dve.tensor_scalar(xn[:, t, :], x[:, t, :], mv[:, t, 0:1], rstd[:, t:t + 1],
                                  ALU.subtract, ALU.mult).then_inc(xn_ready, 1)

            def layer_norm_lo(c0, hi0, t):
                for c in (2 * t, 2 * t + 1):
                    half = c % 2
                    part = (slice(None), slice(4 * half, 4 * half + 4), slice(P * t, P * (t + 1)))
                    lo_of_turn(c0 + c, hi0 + c + 1, ln_bank[c % 4][:].rearrange("p (k c) -> p k c", k=4),
                               xt[0][part], xt[1][part])

            def lo_of_turn(c, hi_count, src, hi_part, lo_part):
                dve.wait_ge(t3_hi, hi_count)
                dve.tensor_tensor(lo_part, src, hi_part, ALU.subtract).then_inc(t3_split, 1)

            def w_part(it, k):
                for half in range(2):
                    dve.wait_ge(w_hi, 12 * it + (2 * k + half + 1))
                    part = slice(4 * half, 4 * half + 4)
                    dve.scalar_tensor_tensor(out=wb[k % 3][1][:, part, :],
                                             in0=turn_bank[half][:].rearrange("p (k c) -> p k c", k=4),
                                             scalar=W_SCALE, in1=wb[k % 3][0][:, part, :],
                                             op0=ALU.mult, op1=ALU.subtract).then_inc(w_lo, 1)

            def w_ahead(it, k):
                w_part(it if k < 5 else it + 1, (k + 1) % 6)

            norm1_stats(0)
            norm1_stats(1)
            normed(1, 0)
            dve.wait_ge(edges_in, 48)
            dve.tensor_copy(edges_f[:, 0, :], edges_i[:, 0, :])
            dve.tensor_copy(edges_f[:, 1, :], edges_i[:, 1, :])
            link(dve.tensor_scalar(edges_f[:, 3, :], edges_i[:, 2, :], 0.0, 4.0, ALU.is_equal, ALU.mult), mask_step)
            link(dve.scalar_tensor_tensor(out=edges_f[:, 2, :], in0=edges_i[:, 2, :], scalar=-1.0,
                                          in1=edges_f[:, 3, :], op0=ALU.add, op1=ALU.add), mask_step)
            dve.scalar_tensor_tensor(out=edges_f[:, 3, :], in0=edges_i[:, 0, :], scalar=float(N),
                                     in1=edges_i[:, 1, :], op0=ALU.mult, op1=ALU.add).then_inc(edges_f_ready, 1)
            norm1_stats(2)
            normed(1, 1)
            layer_norm_lo(0, 0, 0)
            normed(1, 2)
            w_part(0, 0)
            layer_norm_lo(0, 0, 1)
            dve.wait_ge(edges_turned, 1)
            dve.tensor_copy(edge[:, 3, :], acc_bank[1][:, 192:192 + NB]).then_inc(edge_step, 1)
            layer_norm_lo(0, 0, 2)
            dve.tensor_copy(edge[:, 0:3, :], acc_bank[1][:, 0:192].rearrange("p (j b) -> p j b", j=3)[:, :, 0:NB]
                            ).then_inc(edge_step, 1)
            dve.wait_ge(bias_turned, 1)
            dve.tensor_copy(bias[:].rearrange("p n r -> p (n r)"), pv_bank[:, 0:7 * KD]).then_inc(bias_ready, 1)
            dve.wait_ge(bias_ready, 1)
            link(dve.tensor_scalar(biasq[:], bias[:, 3, :], -0.125, None, ALU.mult), mask_step)

            def y_part(it, k, b, y, scale, hi_count=None):
                if hi_count is None:
                    dve.wait_ge(mm_done, 6 * it + (k + 1))
                else:
                    dve.wait_ge(y_hi, hi_count)
                dve.tensor_scalar(y, acc_bank[k % 2][:, 0:N], scale, b, ALU.mult, ALU.add).then_inc(y_ready, 1)

            def y_lo(u1, hi_count, y, hi_part, lo_part):
                dve.wait_ge(y_ready, u1)
                dve.wait_ge(y_hi, hi_count)
                dve.tensor_tensor(lo_part, y, hi_part, ALU.subtract).then_inc(y_split, 1)

            def compare_keys(n):
                dve.wait_ge(keys_turned, n + 1)
                if n >= 2:
                    dve.wait_ge(keys_compared, n - 1)
                for j in range(4):
                    b = 4 * n + j
                    ins = dve.scalar_tensor_tensor(out=same[:, P * (4 * (n % 2) + j):P * (4 * (n % 2) + j + 1)], in0=score_bank[n % 2][:, P * j:P * (j + 1)],
                                                   scalar=edge[:, 3, b:b + 1], in1=upper[:], op0=ALU.is_equal,
                                                   op1=ALU.mult, accum_out=later[:, b:b + 1])
                ins.then_inc(keys_compared, 1)

            c = 0
            for k in range(6):
                w_ahead(0, k)
                if k == 1:
                    dve.wait_ge(edge_step, 1)
                    dve.wait_ge(consts, 1)
                for _ in range(keys_per_unit[k]):
                    compare_keys(c)
                    c += 1
                if k == 2:
                    dve.wait_ge(etw_in, 16)
                    link(dve.tensor_scalar(sp_c[:], etw[:], -1.0, None, ALU.mult), mask_step)
                    dve.tensor_tensor(sp_a[:], etw[:], sp_c[:], ALU.max).then_inc(soft_a, 1)
                n, i = k // 2, k % 2
                y_part(0, k, bias[:, n, i:i + 1], ybuf[k % 2][:], W_BACK, k + 1)
                y_lo(k + 1, k + 1, ybuf[k % 2][:], proj["qkv"[n]][0][:, i, :], proj["qkv"[n]][1][:, i, :])

            dve.wait_ge(consts, 2)
            dve.wait_ge(keys_compared, NB // 4)
            link(dve.tensor_scalar(keep[:], later[:], 0.5, None, ALU.is_lt), mask_step)
            link(dve.tensor_tensor(expo[:], edge[:, 2, :], batch_e[:], ALU.add), mask_step)
            link(dve.tensor_scalar(val_i[:], expo[:], float(2 ** 23), None, ALU.mult), mask_step)
            link(dve.tensor_tensor(val[:], val_i[:].bitcast(F32), keep[:], ALU.mult), mask_step)

            def one_hots(it, n):
                b = 16 * it + (n - 16)
                dve.wait_ge(oh_used, b - (OH - 1))
                dve.tensor_scalar(oh_src[n % OH][:], iota[:], edge[:, 0, ds(b, 1)], None, ALU.is_equal)
                dve.tensor_scalar(oh_dst[n % OH][:], iota[:], edge[:, 1, ds(b, 1)], val[:, ds(b, 1)],
                                  ALU.is_equal, ALU.mult).then_inc(oh_ready, 1)

            per_unit = [3, 3, 3, 3, 2, 2]

            def round_(it, static):
                n = 0
                for k in range(6):
                    w_ahead(it, k)
                    for _ in range(per_unit[k]):
                        if static and n < OH:
                            b = n
                            dve.tensor_scalar(oh_src[n % OH][:], iota[:], edge[:, 0, b:b + 1], None, ALU.is_equal)
                            dve.tensor_scalar(oh_dst[n % OH][:], iota[:], edge[:, 1, b:b + 1], val[:, b:b + 1],
                                              ALU.is_equal, ALU.mult).then_inc(oh_ready, 1)
                        else:
                            one_hots(it, n)
                        n += 1
                    m, i = k // 2, k % 2
                    y_part(it, k, bias[:, m, ds(2 * it + i, 1)], ybuf[k % 2][:], W_BACK, 6 * it + (k + 1))
                    y_lo(6 * it + (k + 1), 6 * it + (k + 1), ybuf[k % 2][:], proj["qkv"[m]][0][:, 2 * it + i, :],
                         proj["qkv"[m]][1][:, 2 * it + i, :])

            round_(1, True)
            with dve.Fori(2, 4) as it:
                round_(it, False)

            def minus_softplus():
                dve.wait_ge(soft_b, 2)
                link(dve.scalar_tensor_tensor(out=nsoft[:], in0=etw[:], scalar=0.0, in1=sp_c[:],
                                              op0=ALU.max, op1=ALU.add), mask_step)
                link(dve.tensor_scalar(nsoft[:], nsoft[:], -1.0, None, ALU.mult), mask_step)

            def read_edge_sums(t):
                dve.tensor_scalar(negmask[:, t, :], edge_bank[t][:, 0:N], 0.0, ABSENT, ALU.is_le, ALU.mult)
                link(dve.tensor_scalar(etyp[:, t, :], edge_bank[t][:, 0:N].bitcast(I32), 23, 3,
                                       ALU.logical_shift_right, ALU.bitwise_and), mask_step)
                for k in range(4):
                    ins = dve.tensor_scalar(type_part[:, t, k, :], etyp[:, t, :], float(k), nsoft[:, k:k + 1],
                                            ALU.is_equal, ALU.mult)
                ins.then_inc(types_ready, 1)

            def att_step(r, par, k, scores, tail, first):
                a = 6 * r + (k - 6)
                tp = 1 - par
                if scores:
                    dve.wait_ge(scored, a + 1)
                if (k == 0 and tail) or (k > 0 and scores):
                    kk = (k - 1) % 6
                    dve.wait_ge(prob_ready, a)
                    dve.reciprocal(rinv[:, kk:kk + 1], rowsum[:, kk:kk + 1]).then_inc(inv_ready, 1)
                if first and scores and k < T:
                    dve.wait_ge(mask_ready, k + 1)
                if scores:
                    dve.tensor_tensor_reduce(out=masked[k % 2][:], in0=score_bank[k % 2][:, 0:N],
                                             in1=negmask[:, k % 3, :], scale=1.0, scalar=3.0e38, op0=ALU.add,
                                             op1=ALU.min, accum_out=negmax[:, k:k + 1]).then_inc(masked_max, 1)
                if (k == 0 and tail) or (k > 0 and scores):
                    c = turn_count(r, f"P{(k - 1) % 6}", first)
                    b = k % 2 ^ 1
                    lo_of_turn(c, c + 1, t3_bank[:, 0:N], pt[b][0][:].rearrange("p t c -> p (t c)"),
                               pt[b][1][:].rearrange("p t c -> p (t c)"))
                if (k < 2 and tail) or (k >= 2 and scores):
                    kk = (k - 2) % 6
                    dve.wait_ge(pv_done, a - 1)
                    dve.wait_ge(inv_ready, a - 1)
                    dve.tensor_scalar(att[tp if k < 2 else par][:, kk % 3, DH * (kk // 3):DH * (kk // 3 + 1)],
                                      pv_bank[:, 0:DH], rinv[:, kk:kk + 1], None, ALU.mult).then_inc(att_ready, 1)

            def value_part(r, par, first):
                c = turn_count(r, "V", first)
                lo_of_turn(c, c + 1, t3_bank[:, 0:N], v2[par][0][:].rearrange("p t c -> p (t c)"),
                           v2[par][1][:].rearrange("p t c -> p (t c)"))

            def output_part(r):
                c = turn_count(r, "O", False)
                lo_of_turn(c, c + 1, t3_bank[:, 0:N], ot[0][:, r - 2, :], ot[1][:, r - 2, :])

            def inner_phase(r, it, i, att_on, tail):
                for m in range(3):
                    k6 = 3 * i + m
                    w_ahead(it, k6)
                    if not att_on:
                        read_edge_sums(m)
                    if m == 0 and att_on:
                        value_part(r, 1 - i, not tail)
                    if m == 1 and tail:
                        output_part(r)
                    if att_on:
                        att_step(r, 1 - i, 2 * m, True, tail, not tail)
                        att_step(r, 1 - i, 2 * m + 1, True, tail, not tail)
                    u1 = 6 * it + (k6 + 1)
                    if m == 0:
                        y_part(it, k6, biasq[:, ds(r, 1)], ybuf[0][:], -0.125 * W_BACK, 2 * r + (U_INNER + 1))
                        y_lo(u1, 2 * r + (U_INNER + 1), ybuf[0][:], q2[i][0][:], q2[i][1][:])
                    elif m == 1:
                        y_part(it, k6, bias[:, 4, ds(r, 1)], ybuf[1][:], W_BACK, 2 * r + (U_INNER + 2))
                        y_lo(u1, 2 * r + (U_INNER + 2), ybuf[1][:], k2[i][0][:], k2[i][1][:])
                    else:
                        y_part(it, k6, bias[:, 5, ds(r, 1)], yv[:], W_BACK)

            minus_softplus()
            dve.wait_ge(edges_summed, 1)
            inner_phase(0, 4, 0, False, False)
            inner_phase(1, 4, 1, True, False)
            with dve.Fori(5, 8) as it:
                for i in range(2):
                    inner_phase(2 * it + (i - 8), it, i, True, True)
            w_part(8, 1)
            value_part(8, 1, False)
            for k in range(6):
                if k == 2:
                    output_part(8)
                att_step(8, 1, k, True, True, False)
            for k in range(2):
                att_step(9, 0, k, False, True, False)
            output_part(9)

            def residual(r):
                c = C_OUT + r
                dve.wait_ge(t3_turned, c + 1)
                part = x[:, :, P * r:P * (r + 1)]
                dve.tensor_tensor(part, t3_bank[:, 0:N].rearrange("p (t c) -> p t c", t=T), part,
                                  ALU.add).then_inc(t3_split, 1)
                dve.wait_ge(t3_split, c + 1)
                for t in range(T):
                    dve.bn_stats(stats[:, t, r, :], x[:, t, P * r:P * (r + 1)]).then_inc(norm2_step, 1)

            for r in range(KD):
                u = U_OUT + r
                if 1 <= r < KD - 1:
                    w_part((u + 1) // 6, (u + 1) % 6)
                if r >= 1:
                    residual(r - 1)
                y_part(u // 6, u % 6, bias[:, 6, r:r + 1], ybuf[r % 2][:], W_BACK)

            def f_part(f1, slot, b):
                dve.wait_ge(f_hi, f1)
                dve.scalar_tensor_tensor(out=wb[b][1][:].rearrange("p k c -> p (k c)"), in0=raw[slot][:],
                                         scalar=W_SCALE, in1=wb[b][0][:].rearrange("p k c -> p (k c)"),
                                         op0=ALU.mult, op1=ALU.subtract).then_inc(f_lo, 1)

            residual(KD - 1)
            dve.wait_ge(norm2_step, KD * T)
            for t in range(T):
                var_of(t, 2, KD, norm2_step, KD * T + 2 * t)
            for t in range(T):
                normed(2, t)
            dve.wait_ge(gate_hi, 1)
            dve.scalar_tensor_tensor(out=gt[1][:].rearrange("p k e -> p (k e)"), in0=acc_bank[1][:, 0:NE * KD],
                                     scalar=W_SCALE, in1=gt[0][:].rearrange("p k e -> p (k e)"),
                                     op0=ALU.mult, op1=ALU.subtract).then_inc(gate_split, 1)
            f_part(1, 0, 0)
            for t in range(T):
                layer_norm_lo(C_LN2, C_LN2 - KD, t)
            f_part(2, 1, 1)

            dve.wait_ge(logits_done, 1)
            logits = acc_bank[1][:, 64:64 + T * NE].rearrange("p (t e) -> p t e", e=NE)
            spread = lambda a: a.unsqueeze(2).to_broadcast([P, T, NE])
            link(dve.tensor_scalar(lg[:], logits, W_BACK, None, ALU.mult), route_step)
            link(dve.tensor_reduce(lmax[:], lg[:], AX.X, ALU.max), route_step)
            link(dve.tensor_tensor(lg[:], lg[:], spread(lmax[:]), ALU.subtract), route_step)
            dve.wait_ge(route_exp, 1)
            mine = pr[:].unsqueeze(3).to_broadcast([P, T, NE, NE])
            other = pr[:].unsqueeze(2).to_broadcast([P, T, NE, NE])
            dve.tensor_tensor(cmp_a[:], other, mine, ALU.is_ge)
            link(dve.tensor_tensor(cmp_b[:], other, mine, ALU.is_gt), route_step)
            for t in range(T):
                dve.tensor_tensor(cmp_a[:, t], cmp_a[:, t], before[:], ALU.mult)
                ins = dve.tensor_tensor(cmp_b[:, t], cmp_b[:, t], after[:], ALU.mult)
            link(ins, route_step)
            link(dve.tensor_tensor(cmp_a[:], cmp_a[:], cmp_b[:], ALU.add), route_step)
            link(dve.tensor_reduce(rank[:], cmp_a[:], AX.X, ALU.add), route_step)
            dve.tensor_scalar(chosen[:], rank[:], 1.5, None, ALU.is_lt)
            dve.tensor_scalar(chosen16[:], rank[:], 1.5, None, ALU.is_lt).then_inc(chosen_ready, 1)
            link(dve.scalar_tensor_tensor(out=cw[:], in0=rank[:], scalar=1.5, in1=pr[:],
                                          op0=ALU.is_lt, op1=ALU.mult), route_step)
            link(dve.tensor_reduce(csum[:], cw[:], AX.X, ALU.add), route_step)
            link(dve.reciprocal(cinv[:], csum[:]), route_step)
            link(dve.tensor_tensor(cw[:], cw[:], spread(cinv[:]), ALU.mult), route_step)

            def slots():
                dve.wait_ge(slots_counted, 1)
                link(dve.tensor_copy(flat(pos), slot_bank[:, 0:T * NE]), slot_step)
                link(dve.tensor_reduce(count_max[:], slot_bank[:, T * NE:(T + 1) * NE], AX.X, ALU.max), slot_step)
                dve.tensor_copy(flag[:], count_max[:]).then_inc(flag_ready, 1)
                link(dve.scalar_tensor_tensor(out=posm[:], in0=pos[:], scalar=1.0, in1=chosen[:],
                                              op0=ALU.add, op1=ALU.mult), slot_step)
                link(dve.tensor_scalar(posm[:], posm[:], -1.0, None, ALU.add), slot_step)
                for e in range(NE):
                    for t in range(T):
                        ins = dve.tensor_scalar(slot_hot[e][:, t, :], iota[:, 0:CAP], posm[:, t, e:e + 1], None,
                                                ALU.is_equal)
                ins.then_inc(hot_ready, 1)

            def tokens():
                dve.wait_ge(tok_made, 1)
                for st, rows_ in enumerate(SR):
                    part = (slice(0, rows_), slice(NE * st, NE * (st + 1)))
                    link(dve.tensor_scalar(tok_f[part], tok_bank[part], -1.0, None, ALU.add), slot_step)
                    dve.tensor_scalar(tok[part], tok_f[part], 0.0, None, ALU.max).then_inc(tok_ready, 1)
                for st, rows_ in enumerate(SR):
                    c = NE * (st + 1) - 1
                    dve.tensor_scalar(last_hot[0:rows_, st, :], iota[0:rows_, :], tok_f[0:rows_, c:c + 1],
                                      None, ALU.is_equal)

            def picks():
                link(dve.memset(cum[:, :, 0], 0.0), slot_step)
                for e in range(1, NE):
                    link(dve.tensor_tensor(cum[:, :, e], cum[:, :, e - 1], chosen[:, :, e - 1], ALU.add), slot_step)
                for e in range(1, NE):
                    ins = dve.tensor_scalar(pos[:, :, e], pos[:, :, e], float(CAP * e), None, ALU.add)
                link(ins, slot_step)
                for n in range(2):
                    dve.memset(pick[n][:, :, NE - 1], 0.0)
                    link(dve.scalar_tensor_tensor(out=pick[n][:, :, 0:NE - 1], in0=cum[:, :, 0:NE - 1], scalar=float(n),
                                                  in1=chosen[:, :, 0:NE - 1], op0=ALU.is_equal, op1=ALU.mult), slot_step)
                    link(dve.tensor_tensor(spick[:], pick[n][:], pos[:], ALU.mult), slot_step)
                    link(dve.tensor_reduce(row_f[n][:], spick[:], AX.X, ALU.add), slot_step)
                    dve.tensor_copy(row_i[n][:], row_f[n][:])
                    link(dve.tensor_tensor(spick[:], pick[n][:], cw[:], ALU.mult), slot_step)
                    ins = dve.tensor_reduce(wgt[n][:], spick[:], AX.X, ALU.add)
                    if n == 0:
                        link(ins, slot_step)
                ins.then_inc(rows_made, 1)

            def step(s, par, nxt, e, mixed=None, own=True):
                b = par
                if nxt:
                    f_part(f_w1(s + 1) + 1, w1_slot[1 - par], 0)
                dve.wait_ge(sig_ready, s + 1)
                dve.scalar_tensor_tensor(out=g1[b], in0=bank[0][:, 0:N], scalar=W_BACK, in1=sig[b],
                                         op0=ALU.mult, op1=ALU.mult).then_inc(gated, 1)
                if mixed == 0:
                    slots()
                if nxt:
                    f_part(f_w3(s + 1) + 1, w1_slot[1 - par] + 1, 1)
                dve.wait_ge(f_used, f_w3(s) + 1)
                if mixed is None:
                    dve.scalar_tensor_tensor(out=g3[b], in0=bank[1][:, 0:N], scalar=W_BACK,
                                             in1=cwb[e], op0=ALU.mult, op1=ALU.mult).then_inc(gated, 1)
                    dve.wait_ge(gated, 2 * s + 2)
                    dve.tensor_tensor(hid[b], g1[b], g3[b], ALU.mult).then_inc(hid_ready, 1)
                else:
                    dve.wait_ge(gated, 2 * s + 1)
                    dve.scalar_tensor_tensor(out=g3[b], in0=bank[1][:, 0:N], scalar=W_BACK,
                                             in1=g1[b], op0=ALU.mult, op1=ALU.mult).then_inc(gated, 1)
                    if mixed == 0:
                        tokens()
                        for e_ in range(NE):
                            dve.wait_ge(cw_turned, e_ + 1)
                            dve.tensor_copy(cwb[e_], bank[2 + e_][:, 0:N]).then_inc(cw_ready, 1)
                        dve.wait_ge(cw_ready, NE)
                    dve.wait_ge(gated, 2 * s + 2)
                    for h in range(2):
                        rows_ = slice(HALF * h, HALF * (h + 1))
                        ins = dve.tensor_tensor(hid[b][rows_, :], g3[b][rows_, :], cwb[2 * mixed + h][rows_, :], ALU.mult)
                    ins.then_inc(hid_ready, 1)
                if mixed == 0:
                    f_part(f_w2(s) + 1, w2_slot[par], 2)
                dve.wait_ge(hid_hi, s + 1)
                dve.tensor_tensor(ht[b][1], hid[b], ht[b][0], ALU.subtract).then_inc(hid_split, 1)
                if own and mixed != 0:
                    f_part(f_w2(s) + 1, w2_slot[par], 2)

            step(0, 0, True, None, mixed=0)
            step(1, 1, False, None, mixed=1, own=False)

            def dense():
                f_part(f_w1(2) + 1, w1_slot[0], 0)
                f_part(f_w3(2) + 1, w1_slot[0] + 1, 1)
                f_part(f_w2(1) + 1, w2_slot[1], 2)
                with dve.Fori(0, FULL - 1) as i:
                    for e in range(NE):
                        step(4 * i + (2 + e), e % 2, True, e)
                for e in range(NE):
                    step(4 * (FULL - 1) + 2 + e, e % 2, e < NE - 1, e)
                for t in range(T):
                    for half in range(2):
                        dve.wait_ge(tile_done, 2 * t + half + 1)
                        cols = slice(512 * half, 512 * (half + 1))
                        dve.scalar_tensor_tensor(out=res[:, t, cols], in0=out_bank[2 * t + half][:], scalar=W_BACK,
                                                 in1=x[:, t, cols], op0=ALU.mult, op1=ALU.add).then_inc(res_ready, 1)

            def rows_lo(h, c, q, banks):
                cols = slice(2 * CAP * q, 2 * CAP * (q + 1))
                dve.wait_ge(xg_hi, c + 1)
                dve.tensor_tensor(xg_flat[h][1][:, cols], banks[q % 2][:, 0:2 * CAP], xg_flat[h][0][:, cols], ALU.subtract
                                  ).then_inc(xg_split, 1)

            def results(g, h):
                dve.wait_ge(scratch_written, 32 * ST * g + 16 * (T + ST * h))
                for st, rows_ in enumerate(SR):
                    if st == 0:
                        dve.wait_ge(expert_done, 6 * g + (3 * h + 3))
                    else:
                        dve.wait_ge(f_used, l_w2(g, FULL * (h + 1) - 1) + 1)
                    dve.tensor_scalar(staged[0:rows_, st, 512:1024], out_bank[2 * st + 1][0:rows_, :], W_BACK, None, ALU.mult
                                      ).then_inc(banks_read, 1)

            def sparse():
                dve.wait_ge(f_hi, 6)
                dve.scalar_tensor_tensor(out=mixed_w[1], in0=raw[w2_slot[1]][:], scalar=W_SCALE, in1=mixed_w[0],
                                         op0=ALU.mult, op1=ALU.subtract).then_inc(f_lo, 1)
                f_part(l_w1(0, 0) + 1, w1_slot[0], 0)
                f_part(l_w3(0, 0) + 1, w1_slot[0] + 1, 1)

                def mixed_result(t):
                    for half in range(2):
                        if t == T - 1 and half == 1:
                            dve.wait_ge(f_used, 6)
                        else:
                            dve.wait_ge(tile_done, 2 * t + half + 1)
                        part = x[:, t, 512 * half:512 * (half + 1)]
                        dve.scalar_tensor_tensor(out=part, in0=out_bank[2 * t + half][:], scalar=W_BACK,
                                                 in1=part, op0=ALU.mult, op1=ALU.add).then_inc(banks_read, 1)

                def high_result(t):
                    dve.wait_ge(low_added, t + 1)
                    dve.wait_ge(high_in[t], 16)
                    dve.scalar_tensor_tensor(out=x[:, t, :], in0=high[t], scalar=wgt[1][:, t:t + 1],
                                             in1=x[:, t, :], op0=ALU.mult, op1=ALU.add).then_inc(high_added, 1)

                for q in range(2):
                    rows_lo(0, q, q, bank[0:2])
                mixed_result(0)
                mixed_result(1)
                for q in (2, 3):
                    rows_lo(0, q, q, bank[0:2])
                mixed_result(2)
                picks()
                with dve.Fori(0, NE // 2) as g:
                    for j in range(PT):
                        h, i = j // FULL, j % FULL
                        b, nxt = j % 2, j < PT - 1
                        if nxt:
                            f_part(l_w1(g, j + 1) + 1, w1_slot[1 - b], 0)
                        dve.wait_ge(sig_ready, PT * g + (j + 3))
                        dve.scalar_tensor_tensor(out=g1[b][:, 0:CAP], in0=bank[0][:, 0:CAP], scalar=W_BACK,
                                                 in1=sig[b][:, 0:CAP], op0=ALU.mult, op1=ALU.mult).then_inc(gated, 1)
                        if nxt:
                            f_part(l_w3(g, j + 1) + 1, w1_slot[1 - b] + 1, 1)
                        dve.wait_ge(f_used, l_w3(g, j) + 1)
                        dve.wait_ge(gated, PT * g + (j + 5))
                        dve.scalar_tensor_tensor(out=hid[b][:, 0:CAP], in0=bank[1][:, 0:CAP], scalar=W_BACK,
                                                 in1=g1[b][:, 0:CAP], op0=ALU.mult, op1=ALU.mult).then_inc(hid_ready, 1)
                        dve.wait_ge(hid_hi, PT * g + (j + 3))
                        dve.tensor_tensor(ht[b][1][:, 0:CAP], hid[b][:, 0:CAP], ht[b][0][:, 0:CAP], ALU.subtract
                                          ).then_inc(hid_split, 1)
                        dve.wait_ge(f_hi, l_w2(g, j) + 1)
                        dve.scalar_tensor_tensor(out=w2b[b][1], in0=raw[w2_slot[b]][:], scalar=W_SCALE, in1=w2b[b][0],
                                                 op0=ALU.mult, op1=ALU.subtract).then_inc(f_lo, 1)
                        if j == FULL:
                            results(g, 0)
                        if i < FULL - 1:
                            rows_lo(1 - h, 8 * g + (4 * h + 4 + i), i, bank[6:8])
                        if j >= PT - 2:
                            with dve.If(g > NE // 2 - 2):
                                high_result(j - (PT - 2))
                    with dve.If(g < NE // 2 - 1):
                        f_part(3 * PT * g + (l_w1(1, 0) + 1), w1_slot[0], 0)
                        f_part(3 * PT * g + (l_w3(1, 0) + 1), w1_slot[0] + 1, 1)
                        results(g, 1)
                high_result(2)
                for n in range(2 * ST):
                    half, st = n // ST, n % ST
                    cols = slice(512 * half, 512 * (half + 1))
                    dve.wait_ge(last_hi, n + 1)
                    rows_ = SR[st]
                    dve.scalar_tensor_tensor(out=last16[1][0:rows_, st, cols], in0=out_bank[2 * st + half][0:rows_, :],
                                             scalar=W_BACK, in1=last16[0][0:rows_, st, cols], op0=ALU.mult,
                                             op1=ALU.subtract).then_inc(last_split, 1)
                dve.wait_ge(high_added, T)
                for n in range(2 * T):
                    half, t = n // T, n % T
                    part = x[:, t, 512 * half:512 * (half + 1)]
                    dve.wait_ge(last_spread, n + 1)
                    dve.scalar_tensor_tensor(out=part, in0=(bank[6], bank[7], bank[0], bank[1])[n % 4][:],
                                             scalar=cw[:, t, NE - 1:NE], in1=part, op0=ALU.mult,
                                             op1=ALU.add).then_inc(res_ready, 1)

            choose(dve, nc.vector.engine, dense, sparse)


_INS = ["x", "src", "dst", "edge_type_5", "L0_gnn_edge_type_weights", "L0_gnn_wq", "L0_gnn_bq", "L0_gnn_wk",
        "L0_gnn_bk", "L0_gnn_wv", "L0_gnn_bv", "L0_gnn_wiq", "L0_gnn_biq", "L0_gnn_wik", "L0_gnn_bik",
        "L0_gnn_wiv", "L0_gnn_biv", "L0_gnn_wo", "L0_gnn_bo", "L0_ffn_gate_w", "L0_ffn_w1", "L0_ffn_w2",
        "L0_ffn_w3"]


def kernel(**inputs):
    import numpy as _np
    import concourse.bacc as _bacc
    from concourse import mybir as _mybir
    from concourse.bass_utils import run_bass_kernel_spmd as _run

    nc = _bacc.Bacc("TRN2", target_bir_lowering=False, num_devices=1)
    arrays, args = {}, []
    for name in _INS:
        a = _np.ascontiguousarray(inputs[name])
        arrays[f"in_{name}"] = a
        args.append(nc.dram_tensor(f"in_{name}", a.shape, _mybir.dt.from_np(a.dtype), kind="ExternalInput").ap())
    shape = tuple(inputs["x"].shape)
    args.append(nc.dram_tensor("out_0", shape, F32, kind="ExternalOutput").ap())
    gnn_moe_kernel(nc, *args)
    r = _run(nc, [arrays], core_ids=[0])
    return r.results[0]["out_0"]
```
